# Optimizing a Trainium2 kernel written in Bass

```python
import numpy as np
import jax
import jax.numpy as jnp

def _softmax(x, axis=-1):
    return jax.nn.softmax(x, axis=axis)

def _gelu(x):
    return jax.nn.gelu(x, approximate=True)

def _silu(x):
    return jax.nn.silu(x)

def _sigmoid(x):
    return jax.nn.sigmoid(x)

def _layernorm(x, axis=-1, eps=1e-05):
    m = jnp.mean(x, axis=axis, keepdims=True)
    v = jnp.var(x, axis=axis, keepdims=True)
    return (x - m) / jnp.sqrt(v + eps)

def _scatter_add(tgt, idx, src, axis=0):
    return tgt.at[idx].add(src)

def _segment_sum(src, seg, n):
    return jax.ops.segment_sum(src, seg, n)
kernel_name = 'mk_decoder_postln_d4_seqx_r8_0c52f2'

def setup_inputs(seed: int=0):
    np.random.seed(seed)
    _w = jnp.asarray

    def _rec_inputs():
        import jax
        import jax.numpy as jnp
        _rk = jax.random.key(seed)
        x = -0.0002928 + 1 * jax.random.normal(jax.random.fold_in(_rk, 1), (32, 128, 128), jnp.float32)
        _lenS = 128 - jax.random.randint(jax.random.fold_in(_rk, 7), (32,), 0, max(1, 128 // 4) + 1, jnp.int32)
        _lenS2 = 120 - jax.random.randint(jax.random.fold_in(_rk, 8), (32,), 0, max(1, 120 // 4) + 1, jnp.int32)
        _ctx_1024P = jax.random.normal(jax.random.fold_in(_rk, 11), (32, 16, 128), jnp.float32)
        _ctx_1024c = jax.random.dirichlet(jax.random.fold_in(_rk, 511), 0.3 * jnp.ones((16,), jnp.float32), (32, 120))
        _ctx_1024t = jnp.einsum('bsk,bkd->bsd', _ctx_1024c, _ctx_1024P)
        _ctx_1024t = _ctx_1024t * jax.lax.rsqrt(jnp.mean(jnp.square(_ctx_1024t)) + 1e-12) * 0.953939
        ctx_1024 = -1.39393e-06 + 0.999914 * (_ctx_1024t + 0.3 * jax.random.normal(jax.random.fold_in(_rk, 611), (32, 120, 128), jnp.float32))
        fside_Bx16xSxS2_0 = -3.27644e-05 + 1.00007 * jax.random.normal(jax.random.fold_in(_rk, 14), (32, 16, 128, 120), jnp.float32)
        _validS = jnp.arange(128)[None, :] < _lenS[:, None]
        _validS2 = jnp.arange(120)[None, :] < _lenS2[:, None]
        _causal = jnp.tril(jnp.ones((128, 128), dtype=bool))
        mask_BxSxS2_bf1 = jnp.ones((32, 128, 120), dtype=bool)
        mask_Bx1xSxS2_ik1 = jnp.where(jnp.broadcast_to(_validS2[:, None, None, :], (32, 1, 128, 120)), 1, 0).astype(jnp.int32)
        return (x, ctx_1024, fside_Bx16xSxS2_0, mask_BxSxS2_bf1, mask_Bx1xSxS2_ik1)
    x, ctx_1024, fside_Bx16xSxS2_0, mask_BxSxS2_bf1, mask_Bx1xSxS2_ik1 = _rec_inputs()

    def _L0_attn_setup():
        import jax, jax.numpy as jnp
        import numpy as np
        D_MODEL = 128
        N_HEADS = 16
        D_LATENT = 32
        HEAD_DIM = D_MODEL // N_HEADS

        def apply_rope(x):
            B, T, H, D = x.shape
            inv_freq = 1.0 / 10000.0 ** (jnp.arange(0, D, 2, dtype=jnp.float32) / D)
            t = jnp.arange(T, dtype=jnp.float32)
            freqs = t[:, None] * inv_freq[None, :]
            sin_f = jnp.sin(freqs)[None, :, None, :]
            cos_f = jnp.cos(freqs)[None, :, None, :]
            x1, x2 = jnp.split(x, 2, axis=-1)
            return jnp.concatenate([x1 * cos_f - x2 * sin_f, x1 * sin_f + x2 * cos_f], axis=-1)
        key = jax.random.key(seed)
        ks = jax.random.split(key, 10)
        B, T = (4, 512)
        s = lambda fan_in: 1.0 / np.sqrt(fan_in)
        return {'x': jax.random.normal(ks[0], (B, T, D_MODEL), dtype=jnp.float32), 'Wq': jax.random.normal(ks[1], (D_MODEL, D_MODEL), dtype=jnp.float32) * s(D_MODEL), 'bq': jnp.zeros((D_MODEL,), jnp.float32), 'Wdown': jax.random.normal(ks[2], (D_MODEL, D_LATENT), dtype=jnp.float32) * s(D_MODEL), 'bdown': jnp.zeros((D_LATENT,), jnp.float32), 'Wup': jax.random.normal(ks[3], (D_LATENT, 2 * D_MODEL), dtype=jnp.float32) * s(D_LATENT), 'bup': jnp.zeros((2 * D_MODEL,), jnp.float32), 'Wout': jax.random.normal(ks[4], (D_MODEL, D_MODEL), dtype=jnp.float32) * s(D_MODEL), 'bout': jnp.zeros((D_MODEL,), jnp.float32)}
    _L0_attn_all = _L0_attn_setup()
    _L0_attn_in = {k: v for k, v in _L0_attn_all.items() if k in ('Wq', 'bq', 'Wdown', 'bdown', 'Wup', 'bup', 'Wout', 'bout')}
    del _L0_attn_all

    def _L0_xattn_setup():
        import jax, jax.numpy as jnp
        import numpy as np
        N_EMBD = 128
        N_HEADS = 16
        HEAD_DIM = N_EMBD // N_HEADS
        key = jax.random.key(seed)
        ks = jax.random.split(key, 12)
        B, T, S, C = (2, 256, 256, N_EMBD)
        std = 1.0 / np.sqrt(C)
        inp = {'x': jax.random.normal(ks[0], (B, T, C), dtype=jnp.float32), 'context': jax.random.normal(ks[1], (B, S, C), dtype=jnp.float32), 'q_w': jax.random.uniform(ks[2], (C, C), minval=-std, maxval=std, dtype=jnp.float32), 'q_b': jax.random.uniform(ks[3], (C,), minval=-std, maxval=std, dtype=jnp.float32), 'k_w': jax.random.uniform(ks[4], (C, C), minval=-std, maxval=std, dtype=jnp.float32), 'k_b': jax.random.uniform(ks[5], (C,), minval=-std, maxval=std, dtype=jnp.float32), 'v_w': jax.random.uniform(ks[6], (C, C), minval=-std, maxval=std, dtype=jnp.float32), 'v_b': jax.random.uniform(ks[7], (C,), minval=-std, maxval=std, dtype=jnp.float32), 'o_w': jax.random.uniform(ks[8], (C, C), minval=-std, maxval=std, dtype=jnp.float32), 'o_b': jax.random.uniform(ks[9], (C,), minval=-std, maxval=std, dtype=jnp.float32)}
        return inp
    _L0_xattn_all = _L0_xattn_setup()
    _L0_xattn_in = {k: v for k, v in _L0_xattn_all.items() if k in ('q_w', 'q_b', 'k_w', 'k_b', 'v_w', 'v_b', 'o_w', 'o_b')}
    del _L0_xattn_all

    def _L0_ffn_setup():
        import jax, jax.numpy as jnp
        import numpy as np
        HID, FFN, E, K = (128, 512, 8, 2)
        CAP_FACTOR = 1.25
        key = jax.random.key(seed)
        k1, k2, k3, k4 = jax.random.split(key, 4)
        B, T = (4, 256)
        x = jax.random.normal(k1, (B, T, HID), dtype=jnp.float32)
        router_w = jax.random.normal(k2, (E, HID), dtype=jnp.float32) * 0.02
        w1 = jax.random.normal(k3, (E, HID, FFN), dtype=jnp.float32) * 0.02
        w2 = jax.random.normal(k4, (E, FFN, HID), dtype=jnp.float32) * 0.02
        return {'x': x, 'router_w': router_w, 'w1': w1, 'w2': w2}
    _L0_ffn_all = _L0_ffn_setup()
    _L0_ffn_in = {k: v for k, v in _L0_ffn_all.items() if k in ('router_w', 'w1', 'w2')}
    del _L0_ffn_all

    def _L1_attn_setup():
        import jax, jax.numpy as jnp
        import numpy as np
        B, N, D, H = (2, 256, 128, 16)
        HD = D // H

        def l2norm(x, eps=1e-12):
            n = jnp.sqrt(jnp.sum(x * x, axis=-1, keepdims=True))
            return x / jnp.maximum(n, eps)

        def dplr_delta_rule(q, k, v, a, gk):
            qm, km, vm, am, gm = (jnp.moveaxis(t, 1, 0) for t in (q, k, v, a, gk))

            def step(S, inp):
                qt, kt, vt, at, gkt = inp
                Sp = S * jnp.exp(gkt)[..., None]
                u = jnp.einsum('bhk,bhkv->bhv', at, Sp) + vt
                S = Sp + jnp.einsum('bhk,bhv->bhkv', kt, u)
                o = jnp.einsum('bhk,bhkv->bhv', qt, S)
                return (S, o)
            S0 = jnp.zeros((q.shape[0], q.shape[2], q.shape[3], v.shape[3]), q.dtype)
            _, o = jax.lax.scan(step, S0, (qm, km, vm, am, gm))
            return jnp.moveaxis(o, 0, 1)

        def _forward(x, Wq, Wk, Wv, Wgamma, Wf, Wg1, Wg2, Wo, norm_w):
            b, n, d = x.shape
            silu = jax.nn.silu
            q = silu(x @ Wq)
            k = silu(x @ Wk)
            v = silu(x @ Wv)
            log_f = jax.nn.log_sigmoid(x @ Wf)
            gamma = -jax.nn.sigmoid(x @ Wgamma)
            q = q.reshape(b, n, H, HD)
            k = l2norm(k.reshape(b, n, H, HD))
            v = v.reshape(b, n, H, HD)
            gk = jnp.broadcast_to(log_f[..., None], (b, n, H, HD))
            a = k * gamma[..., None] * jnp.exp(gk)
            out = dplr_delta_rule(q, k, v, a, gk)
            out = out.reshape(b, n, d)
            gate = jax.nn.sigmoid(x @ Wg1 @ Wg2)
            out = out * gate
            mu = jnp.mean(out, axis=-1, keepdims=True)
            var = jnp.mean(jnp.square(out - mu), axis=-1, keepdims=True)
            out = (out - mu) * jax.lax.rsqrt(var + 1e-05) * norm_w
            return out @ Wo
        key = jax.random.key(seed)
        ks = jax.random.split(key, 10)
        s = 0.02
        return {'x': jax.random.normal(ks[0], (B, N, D), jnp.float32), 'Wq': jax.random.normal(ks[1], (D, D), jnp.float32) * s, 'Wk': jax.random.normal(ks[2], (D, D), jnp.float32) * s, 'Wv': jax.random.normal(ks[3], (D, D), jnp.float32) * s, 'Wgamma': jax.random.normal(ks[4], (D, H), jnp.float32) * s, 'Wf': jax.random.normal(ks[5], (D, H), jnp.float32) * s, 'Wg1': jax.random.normal(ks[6], (D, HD), jnp.float32) * s, 'Wg2': jax.random.normal(ks[7], (HD, D), jnp.float32) * s, 'Wo': jax.random.normal(ks[8], (D, D), jnp.float32) * s, 'norm_w': jnp.ones((D,), jnp.float32)}
    _L1_attn_all = _L1_attn_setup()
    _L1_attn_in = {k: v for k, v in _L1_attn_all.items() if k in ('Wq', 'Wk', 'Wv', 'Wgamma', 'Wf', 'Wg1', 'Wg2', 'Wo', 'norm_w')}
    del _L1_attn_all

    def _L1_xattn_setup():
        import jax, jax.numpy as jnp
        import numpy as np
        D_MODEL = 128
        NUM_HEADS = 16
        D_H = D_MODEL // NUM_HEADS

        def _xavier(key, out_f, in_f):
            limit = np.sqrt(6.0 / (in_f + out_f))
            return jax.random.uniform(key, (out_f, in_f), jnp.float32, -limit, limit)
        key = jax.random.key(seed)
        ks = jax.random.split(key, 8)
        B, S = (2, 256)
        q = jax.random.normal(ks[0], (B, S, D_MODEL), jnp.float32)
        k = jax.random.normal(ks[1], (B, S, D_MODEL), jnp.float32)
        v = jax.random.normal(ks[2], (B, S, D_MODEL), jnp.float32)
        attn_mask = jnp.ones((B, S, S), dtype=bool)
        Wq = _xavier(ks[3], D_MODEL, D_MODEL)
        bq = jnp.zeros((D_MODEL,), jnp.float32)
        Wk = _xavier(ks[4], D_MODEL, D_MODEL)
        bk = jnp.zeros((D_MODEL,), jnp.float32)
        Wv = _xavier(ks[5], D_MODEL, D_MODEL)
        bv = jnp.zeros((D_MODEL,), jnp.float32)
        Wo = _xavier(ks[6], D_MODEL, D_MODEL)
        bo = jnp.zeros((D_MODEL,), jnp.float32)
        return {'q': q, 'k': k, 'v': v, 'attn_mask': attn_mask, 'Wq': Wq, 'bq': bq, 'Wk': Wk, 'bk': bk, 'Wv': Wv, 'bv': bv, 'Wo': Wo, 'bo': bo}
    _L1_xattn_all = _L1_xattn_setup()
    _L1_xattn_in = {k: v for k, v in _L1_xattn_all.items() if k in ('Wq', 'bq', 'Wk', 'bk', 'Wv', 'bv', 'Wo', 'bo')}
    del _L1_xattn_all

    def _L1_ffn_setup():
        import jax, jax.numpy as jnp
        import numpy as np
        E = 8
        K = 2
        H = 128
        F = 448
        B, S = (1, 256)
        key = jax.random.key(seed)
        ks = jax.random.split(key, 5)
        scale_h = 1.0 / np.sqrt(H)
        scale_f = 1.0 / np.sqrt(F)
        return {'hidden_states': jax.random.normal(ks[0], (B, S, H), jnp.float32), 'gate_w': jax.random.normal(ks[1], (E, H), jnp.float32) * scale_h, 'w1': jax.random.normal(ks[2], (E, F, H), jnp.float32) * scale_h, 'w3': jax.random.normal(ks[3], (E, F, H), jnp.float32) * scale_h, 'w2': jax.random.normal(ks[4], (E, H, F), jnp.float32) * scale_f}
    _L1_ffn_all = _L1_ffn_setup()
    _L1_ffn_in = {k: v for k, v in _L1_ffn_all.items() if k in ('gate_w', 'w1', 'w3', 'w2')}
    del _L1_ffn_all

    def _L2_attn_setup():
        import jax, jax.numpy as jnp
        import numpy as np
        D_MODEL = 128
        N_HEADS = 16
        D_HEAD = D_MODEL // N_HEADS
        LUT_SIZE = 512
        TWO_PI = 2.0 * np.pi
        SCALE = np.sqrt(2.0 * D_HEAD).astype(np.float32)
        _GRID = (TWO_PI * np.arange(LUT_SIZE) / LUT_SIZE).astype(np.float32)
        _SIN_TABLE = jnp.asarray(np.sin(_GRID))
        _COS_TABLE = jnp.asarray(np.cos(_GRID))

        def _lut_sin_cos(theta):
            idx = jnp.mod(jnp.round(theta * (LUT_SIZE / TWO_PI)).astype(jnp.int32), LUT_SIZE)
            return (_SIN_TABLE[idx], _COS_TABLE[idx])
        key = jax.random.key(seed)
        ks = jax.random.split(key, 7)
        B, S = (2, 256)
        x = jax.random.normal(ks[0], (B, S, D_MODEL), dtype=jnp.float32)
        w_q = 0.02 * jax.random.normal(ks[1], (N_HEADS, D_HEAD), dtype=jnp.float32)
        b_q = jnp.zeros((N_HEADS, D_HEAD), dtype=jnp.float32)
        w_k = 0.02 * jax.random.normal(ks[2], (N_HEADS, D_HEAD), dtype=jnp.float32)
        b_k = jnp.zeros((N_HEADS, D_HEAD), dtype=jnp.float32)
        v_w = jax.random.normal(ks[3], (D_MODEL, D_MODEL), dtype=jnp.float32) / np.sqrt(D_MODEL)
        out_w = jax.random.normal(ks[4], (D_MODEL, D_MODEL), dtype=jnp.float32) / np.sqrt(D_MODEL)
        return {'x': x, 'w_q': w_q, 'b_q': b_q, 'w_k': w_k, 'b_k': b_k, 'v_w': v_w, 'out_w': out_w}
    _L2_attn_all = _L2_attn_setup()
    _L2_attn_in = {k: v for k, v in _L2_attn_all.items() if k in ('w_q', 'b_q', 'w_k', 'b_k', 'v_w', 'out_w')}
    del _L2_attn_all

    def _L2_xattn_setup():
        import jax, jax.numpy as jnp
        import numpy as np
        DIM = 128
        NUM_HEADS = 16
        HEAD_DIM = DIM // NUM_HEADS
        SCALE = HEAD_DIM ** (-0.5)
        B, T1, T2 = (4, 256, 256)
        key = jax.random.key(seed)
        ks = jax.random.split(key, 6)
        s = 0.02
        return {'x': jax.random.normal(ks[0], (B, T1, DIM), dtype=jnp.float32), 'context': jax.random.normal(ks[1], (B, T2, DIM), dtype=jnp.float32), 'Wq': jax.random.normal(ks[2], (DIM, DIM), dtype=jnp.float32) * s, 'Wkv': jax.random.normal(ks[3], (2 * DIM, DIM), dtype=jnp.float32) * s, 'Wproj': jax.random.normal(ks[4], (DIM, DIM), dtype=jnp.float32) * s, 'bproj': jax.random.normal(ks[5], (DIM,), dtype=jnp.float32) * s}
    _L2_xattn_all = _L2_xattn_setup()
    _L2_xattn_in = {k: v for k, v in _L2_xattn_all.items() if k in ('Wq', 'Wkv', 'Wproj', 'bproj')}
    del _L2_xattn_all

    def _L2_ffn_setup():
        import jax, jax.numpy as jnp
        import numpy as np
        D_MODEL = 128
        M = 64
        INNER = 16
        key = jax.random.key(seed)
        ks = jax.random.split(key, 9)

        def init(k, shape, fan_in):
            bound = 1.0 / np.sqrt(fan_in)
            return jax.random.uniform(k, shape, jnp.float32, -bound, bound)
        x = jax.random.normal(ks[0], (16, 512, D_MODEL), dtype=jnp.float32)
        Win = init(ks[1], (D_MODEL, M), D_MODEL)
        bin_ = init(ks[2], (M,), D_MODEL)
        W1 = init(ks[3], (M, INNER), 1)
        b1 = init(ks[4], (M, INNER), 1)
        W2 = init(ks[5], (M, INNER), INNER)
        b2 = init(ks[6], (M,), INNER)
        Wout = init(ks[7], (M, D_MODEL), M)
        bout = init(ks[8], (D_MODEL,), M)
        return {'x': x, 'Win': Win, 'bin_': bin_, 'W1': W1, 'b1': b1, 'W2': W2, 'b2': b2, 'Wout': Wout, 'bout': bout}
    _L2_ffn_all = _L2_ffn_setup()
    _L2_ffn_in = {k: v for k, v in _L2_ffn_all.items() if k in ('Win', 'bin_', 'W1', 'b1', 'W2', 'b2', 'Wout', 'bout')}
    del _L2_ffn_all

    def _L3_attn_setup():
        import jax, jax.numpy as jnp
        import numpy as np
        B_, T_, D_MODEL = (2, 128, 128)
        D_STATE, D_CONV, EXPAND = (16, 4, 2)
        D_INNER = D_MODEL * EXPAND

        def _ssm_forward(x, ln_g, ln_b, W_in, b_in, conv_w, conv_b, A, W_B, b_B, W_C, b_C, D, W_out, b_out):
            eps = 1e-05
            mu = jnp.mean(x, axis=-1, keepdims=True)
            var = jnp.var(x, axis=-1, keepdims=True)
            xn = (x - mu) / jnp.sqrt(var + eps) * ln_g + ln_b
            proj = xn @ W_in + b_in
            xp, gate = jnp.split(proj, 2, axis=-1)
            xc = jax.lax.conv_general_dilated(xp.transpose(0, 2, 1), conv_w, window_strides=(1,), padding=[(D_CONV - 1, 0)], dimension_numbers=('NCH', 'OIH', 'NCH'), feature_group_count=D_INNER).transpose(0, 2, 1) + conv_b
            xc = jax.nn.silu(xc)
            Bt = xc @ W_B + b_B
            Ct = xc @ W_C + b_C
            a = jax.nn.sigmoid(A)
            u = Bt[:, :, None, :] * xc[:, :, :, None]
            a_full = jnp.broadcast_to(a, u.shape)

            def combine(c1, c2):
                a1, u1 = c1
                a2, u2 = c2
                return (a2 * a1, a2 * u1 + u2)
            _, h = jax.lax.associative_scan(combine, (a_full, u), axis=1)
            y = jnp.einsum('btns,bts->btn', h, Ct) + D * xc
            y = y * jax.nn.silu(gate)
            return y @ W_out + b_out + x
        key = jax.random.key(seed)
        ks = jax.random.split(key, 12)

        def s(k, shape, sc=0.02):
            return jax.random.normal(k, shape, jnp.float32) * sc
        return {'x': jax.random.normal(ks[0], (B_, T_, D_MODEL), jnp.float32), 'ln_g': jnp.ones((D_MODEL,), jnp.float32), 'ln_b': jnp.zeros((D_MODEL,), jnp.float32), 'W_in': s(ks[1], (D_MODEL, 2 * D_INNER)), 'b_in': s(ks[2], (2 * D_INNER,)), 'conv_w': s(ks[3], (D_INNER, 1, D_CONV)), 'conv_b': s(ks[4], (D_INNER,)), 'A': s(ks[5], (D_INNER, D_STATE), 0.1), 'W_B': s(ks[6], (D_INNER, D_STATE)), 'b_B': s(ks[7], (D_STATE,)), 'W_C': s(ks[8], (D_INNER, D_STATE)), 'b_C': s(ks[9], (D_STATE,)), 'D': jnp.ones((D_INNER,), jnp.float32), 'W_out': s(ks[10], (D_INNER, D_MODEL)), 'b_out': s(ks[11], (D_MODEL,))}
    _L3_attn_all = _L3_attn_setup()
    _L3_attn_in = {k: v for k, v in _L3_attn_all.items() if k in ('ln_g', 'ln_b', 'W_in', 'b_in', 'conv_w', 'conv_b', 'A', 'W_B', 'b_B', 'W_C', 'b_C', 'D', 'W_out', 'b_out')}
    del _L3_attn_all

    def _L3_xattn_setup():
        import jax, jax.numpy as jnp
        import numpy as np
        DIM = 128
        NUM_HEADS = 16
        HEAD_DIM = DIM // NUM_HEADS
        SCALE = HEAD_DIM ** (-0.5)
        key = jax.random.key(seed)
        ks = jax.random.split(key, 13)
        B, L, S = (2, 256, 256)
        inp = {'query': jax.random.normal(ks[0], (B, L, DIM), jnp.float32), 'key': jax.random.normal(ks[1], (B, S, DIM), jnp.float32), 'value': jax.random.normal(ks[2], (B, S, DIM), jnp.float32), 'mask': jax.random.randint(ks[3], (B, 1, L, S), 0, 2, jnp.int32), 'attn_bias': jax.random.normal(ks[4], (B, NUM_HEADS, L, S), jnp.float32), 'Wq': jax.random.normal(ks[5], (DIM, DIM), jnp.float32) * DIM ** (-0.5), 'bq': jax.random.normal(ks[6], (DIM,), jnp.float32) * 0.02, 'Wk': jax.random.normal(ks[7], (DIM, DIM), jnp.float32) * DIM ** (-0.5), 'bk': jax.random.normal(ks[8], (DIM,), jnp.float32) * 0.02, 'Wv': jax.random.normal(ks[9], (DIM, DIM), jnp.float32) * DIM ** (-0.5), 'bv': jax.random.normal(ks[10], (DIM,), jnp.float32) * 0.02, 'Wo': jax.random.normal(ks[11], (DIM, DIM), jnp.float32) * DIM ** (-0.5), 'bo': jax.random.normal(ks[12], (DIM,), jnp.float32) * 0.02}
        return inp
    _L3_xattn_all = _L3_xattn_setup()
    _L3_xattn_in = {k: v for k, v in _L3_xattn_all.items() if k in ('Wq', 'bq', 'Wk', 'bk', 'Wv', 'bv', 'Wo', 'bo')}
    del _L3_xattn_all

    def _L3_ffn_setup():
        import jax, jax.numpy as jnp
        import numpy as np
        B, S, D = (4, 64, 128)
        E, K, H = (64, 8, 32)
        ES, HS = (2, 256)
        key = jax.random.key(seed)
        ks = jax.random.split(key, 8)
        scale = 0.02
        rn = lambda k, shape, s: jax.random.normal(k, shape, jnp.float32) * s
        return {'x': rn(ks[0], (B, S, D), 1.0), 'router_w': rn(ks[1], (D, E), scale), 'router_b': jnp.zeros((E,), jnp.float32), 'w1': rn(ks[2], (E, D, H), scale), 'b1': jnp.zeros((E, H), jnp.float32), 'w2': rn(ks[3], (E, H, D), scale), 'b2': jnp.zeros((E, D), jnp.float32), 'sw1': rn(ks[4], (ES, D, HS), scale), 'sb1': jnp.zeros((ES, HS), jnp.float32), 'sw2': rn(ks[5], (ES, HS, D), scale), 'sb2': jnp.zeros((ES, D), jnp.float32)}
    _L3_ffn_all = _L3_ffn_setup()
    _L3_ffn_in = {k: v for k, v in _L3_ffn_all.items() if k in ('router_w', 'router_b', 'w1', 'b1', 'w2', 'b2', 'sw1', 'sb1', 'sw2', 'sb2')}
    del _L3_ffn_all
    return {'x': x, 'ctx_1024': ctx_1024, 'fside_Bx16xSxS2_0': fside_Bx16xSxS2_0, 'mask_BxSxS2_bf1': mask_BxSxS2_bf1, 'mask_Bx1xSxS2_ik1': mask_Bx1xSxS2_ik1, 'L0_attn_Wq': _L0_attn_in['Wq'], 'L0_attn_bq': _L0_attn_in['bq'], 'L0_attn_Wdown': _L0_attn_in['Wdown'], 'L0_attn_bdown': _L0_attn_in['bdown'], 'L0_attn_Wup': _L0_attn_in['Wup'], 'L0_attn_bup': _L0_attn_in['bup'], 'L0_attn_Wout': _L0_attn_in['Wout'], 'L0_attn_bout': _L0_attn_in['bout'], 'L0_xattn_q_w': _L0_xattn_in['q_w'], 'L0_xattn_q_b': _L0_xattn_in['q_b'], 'L0_xattn_k_w': _L0_xattn_in['k_w'], 'L0_xattn_k_b': _L0_xattn_in['k_b'], 'L0_xattn_v_w': _L0_xattn_in['v_w'], 'L0_xattn_v_b': _L0_xattn_in['v_b'], 'L0_xattn_o_w': _L0_xattn_in['o_w'], 'L0_xattn_o_b': _L0_xattn_in['o_b'], 'L0_ffn_router_w': _L0_ffn_in['router_w'], 'L0_ffn_w1': _L0_ffn_in['w1'], 'L0_ffn_w2': _L0_ffn_in['w2'], 'L1_attn_Wq': _L1_attn_in['Wq'], 'L1_attn_Wk': _L1_attn_in['Wk'], 'L1_attn_Wv': _L1_attn_in['Wv'], 'L1_attn_Wgamma': _L1_attn_in['Wgamma'], 'L1_attn_Wf': _L1_attn_in['Wf'], 'L1_attn_Wg1': _L1_attn_in['Wg1'], 'L1_attn_Wg2': _L1_attn_in['Wg2'], 'L1_attn_Wo': _L1_attn_in['Wo'], 'L1_attn_norm_w': _L1_attn_in['norm_w'], 'L1_xattn_Wq': _L1_xattn_in['Wq'], 'L1_xattn_bq': _L1_xattn_in['bq'], 'L1_xattn_Wk': _L1_xattn_in['Wk'], 'L1_xattn_bk': _L1_xattn_in['bk'], 'L1_xattn_Wv': _L1_xattn_in['Wv'], 'L1_xattn_bv': _L1_xattn_in['bv'], 'L1_xattn_Wo': _L1_xattn_in['Wo'], 'L1_xattn_bo': _L1_xattn_in['bo'], 'L1_ffn_gate_w': _L1_ffn_in['gate_w'], 'L1_ffn_w1': _L1_ffn_in['w1'], 'L1_ffn_w3': _L1_ffn_in['w3'], 'L1_ffn_w2': _L1_ffn_in['w2'], 'L2_attn_w_q': _L2_attn_in['w_q'], 'L2_attn_b_q': _L2_attn_in['b_q'], 'L2_attn_w_k': _L2_attn_in['w_k'], 'L2_attn_b_k': _L2_attn_in['b_k'], 'L2_attn_v_w': _L2_attn_in['v_w'], 'L2_attn_out_w': _L2_attn_in['out_w'], 'L2_xattn_Wq': _L2_xattn_in['Wq'], 'L2_xattn_Wkv': _L2_xattn_in['Wkv'], 'L2_xattn_Wproj': _L2_xattn_in['Wproj'], 'L2_xattn_bproj': _L2_xattn_in['bproj'], 'L2_ffn_Win': _L2_ffn_in['Win'], 'L2_ffn_bin_': _L2_ffn_in['bin_'], 'L2_ffn_W1': _L2_ffn_in['W1'], 'L2_ffn_b1': _L2_ffn_in['b1'], 'L2_ffn_W2': _L2_ffn_in['W2'], 'L2_ffn_b2': _L2_ffn_in['b2'], 'L2_ffn_Wout': _L2_ffn_in['Wout'], 'L2_ffn_bout': _L2_ffn_in['bout'], 'L3_attn_ln_g': _L3_attn_in['ln_g'], 'L3_attn_ln_b': _L3_attn_in['ln_b'], 'L3_attn_W_in': _L3_attn_in['W_in'], 'L3_attn_b_in': _L3_attn_in['b_in'], 'L3_attn_conv_w': _L3_attn_in['conv_w'], 'L3_attn_conv_b': _L3_attn_in['conv_b'], 'L3_attn_A': _L3_attn_in['A'], 'L3_attn_W_B': _L3_attn_in['W_B'], 'L3_attn_b_B': _L3_attn_in['b_B'], 'L3_attn_W_C': _L3_attn_in['W_C'], 'L3_attn_b_C': _L3_attn_in['b_C'], 'L3_attn_D': _L3_attn_in['D'], 'L3_attn_W_out': _L3_attn_in['W_out'], 'L3_attn_b_out': _L3_attn_in['b_out'], 'L3_xattn_Wq': _L3_xattn_in['Wq'], 'L3_xattn_bq': _L3_xattn_in['bq'], 'L3_xattn_Wk': _L3_xattn_in['Wk'], 'L3_xattn_bk': _L3_xattn_in['bk'], 'L3_xattn_Wv': _L3_xattn_in['Wv'], 'L3_xattn_bv': _L3_xattn_in['bv'], 'L3_xattn_Wo': _L3_xattn_in['Wo'], 'L3_xattn_bo': _L3_xattn_in['bo'], 'L3_ffn_router_w': _L3_ffn_in['router_w'], 'L3_ffn_router_b': _L3_ffn_in['router_b'], 'L3_ffn_w1': _L3_ffn_in['w1'], 'L3_ffn_b1': _L3_ffn_in['b1'], 'L3_ffn_w2': _L3_ffn_in['w2'], 'L3_ffn_b2': _L3_ffn_in['b2'], 'L3_ffn_sw1': _L3_ffn_in['sw1'], 'L3_ffn_sb1': _L3_ffn_in['sb1'], 'L3_ffn_sw2': _L3_ffn_in['sw2'], 'L3_ffn_sb2': _L3_ffn_in['sb2']}

def reference(x, ctx_1024, fside_Bx16xSxS2_0, mask_BxSxS2_bf1, mask_Bx1xSxS2_ik1, L0_attn_Wq, L0_attn_bq, L0_attn_Wdown, L0_attn_bdown, L0_attn_Wup, L0_attn_bup, L0_attn_Wout, L0_attn_bout, L0_xattn_q_w, L0_xattn_q_b, L0_xattn_k_w, L0_xattn_k_b, L0_xattn_v_w, L0_xattn_v_b, L0_xattn_o_w, L0_xattn_o_b, L0_ffn_router_w, L0_ffn_w1, L0_ffn_w2, L1_attn_Wq, L1_attn_Wk, L1_attn_Wv, L1_attn_Wgamma, L1_attn_Wf, L1_attn_Wg1, L1_attn_Wg2, L1_attn_Wo, L1_attn_norm_w, L1_xattn_Wq, L1_xattn_bq, L1_xattn_Wk, L1_xattn_bk, L1_xattn_Wv, L1_xattn_bv, L1_xattn_Wo, L1_xattn_bo, L1_ffn_gate_w, L1_ffn_w1, L1_ffn_w3, L1_ffn_w2, L2_attn_w_q, L2_attn_b_q, L2_attn_w_k, L2_attn_b_k, L2_attn_v_w, L2_attn_out_w, L2_xattn_Wq, L2_xattn_Wkv, L2_xattn_Wproj, L2_xattn_bproj, L2_ffn_Win, L2_ffn_bin_, L2_ffn_W1, L2_ffn_b1, L2_ffn_W2, L2_ffn_b2, L2_ffn_Wout, L2_ffn_bout, L3_attn_ln_g, L3_attn_ln_b, L3_attn_W_in, L3_attn_b_in, L3_attn_conv_w, L3_attn_conv_b, L3_attn_A, L3_attn_W_B, L3_attn_b_B, L3_attn_W_C, L3_attn_b_C, L3_attn_D, L3_attn_W_out, L3_attn_b_out, L3_xattn_Wq, L3_xattn_bq, L3_xattn_Wk, L3_xattn_bk, L3_xattn_Wv, L3_xattn_bv, L3_xattn_Wo, L3_xattn_bo, L3_ffn_router_w, L3_ffn_router_b, L3_ffn_w1, L3_ffn_b1, L3_ffn_w2, L3_ffn_b2, L3_ffn_sw1, L3_ffn_sb1, L3_ffn_sw2, L3_ffn_sb2):
    import jax
    import jax.numpy as jnp

    def _L0_attn_ref(x, Wq, bq, Wdown, bdown, Wup, bup, Wout, bout):
        import jax, jax.numpy as jnp
        import numpy as np
        D_MODEL = 128
        N_HEADS = 16
        D_LATENT = 32
        HEAD_DIM = D_MODEL // N_HEADS

        def apply_rope(x):
            B, T, H, D = x.shape
            inv_freq = 1.0 / 10000.0 ** (jnp.arange(0, D, 2, dtype=jnp.float32) / D)
            t = jnp.arange(T, dtype=jnp.float32)
            freqs = t[:, None] * inv_freq[None, :]
            sin_f = jnp.sin(freqs)[None, :, None, :]
            cos_f = jnp.cos(freqs)[None, :, None, :]
            x1, x2 = jnp.split(x, 2, axis=-1)
            return jnp.concatenate([x1 * cos_f - x2 * sin_f, x1 * sin_f + x2 * cos_f], axis=-1)
        B, T, D = x.shape
        H, Dh = (N_HEADS, HEAD_DIM)
        q = x @ Wq + bq
        kv_latent = x @ Wdown + bdown
        kv = kv_latent @ Wup + bup
        q = q.reshape(B, T, H, Dh)
        kv = kv.reshape(B, T, H, 2 * Dh)
        k, v = jnp.split(kv, 2, axis=-1)
        q = apply_rope(q)
        k = apply_rope(k)
        att = jnp.einsum('bthd,btgd->bthg', q, k) / jnp.sqrt(jnp.float32(Dh))
        att = jax.nn.softmax(att, axis=-1)
        out = jnp.einsum('bthg,btgd->bthd', att, v)
        out = out.reshape(B, T, D)
        return out @ Wout + bout

    def _L0_xattn_ref(x, context, q_w, q_b, k_w, k_b, v_w, v_b, o_w, o_b):
        import jax, jax.numpy as jnp
        import numpy as np
        N_EMBD = 128
        N_HEADS = 16
        HEAD_DIM = N_EMBD // N_HEADS
        B, T, C = x.shape
        S = context.shape[1]
        H, D = (N_HEADS, HEAD_DIM)
        q = (x @ q_w + q_b).reshape(B, T, H, D).transpose(0, 2, 1, 3)
        k = (context @ k_w + k_b).reshape(B, S, H, D).transpose(0, 2, 1, 3)
        v = (context @ v_w + v_b).reshape(B, S, H, D).transpose(0, 2, 1, 3)
        att = jnp.einsum('bhtd,bhsd->bhts', q, k) / jnp.sqrt(jnp.float32(D))
        causal = jnp.tril(jnp.ones((T, S), dtype=bool))
        att = jnp.where(causal[None, None, :, :], att, -jnp.inf)
        att = jax.nn.softmax(att, axis=-1)
        y = jnp.einsum('bhts,bhsd->bhtd', att, v)
        y = y.transpose(0, 2, 1, 3).reshape(B, T, C)
        return y @ o_w + o_b

    def _L0_ffn_ref(x, router_w, w1, w2):
        import jax, jax.numpy as jnp
        import numpy as np
        HID, FFN, E, K = (128, 512, 8, 2)
        CAP_FACTOR = 1.25
        B, T, H = x.shape
        N = B * T
        x_flat = x.reshape(N, H)
        C = max(1, int(CAP_FACTOR * N / E * K))
        logits = x_flat @ router_w.T
        probs = jax.nn.softmax(logits, axis=-1)
        top_v, top_i = jax.lax.top_k(probs, K)
        top_v = top_v / jnp.sum(top_v, axis=-1, keepdims=True)
        out = jnp.zeros_like(x_flat)
        for k in range(K):
            eid = top_i[:, k]
            gate = top_v[:, k]
            onehot = jax.nn.one_hot(eid, E, dtype=jnp.int32)
            pos = jnp.take_along_axis(jnp.cumsum(onehot, axis=0), eid[:, None], axis=1)[:, 0] - 1
            keep = pos < C
            slot = jnp.where(keep, eid * C + pos, E * C)
            buf = jnp.zeros((E * C + 1, H), dtype=x.dtype).at[slot].add(x_flat * keep[:, None].astype(x.dtype))
            expert_in = buf[:E * C].reshape(E, C, H)
            h = jax.nn.gelu(jnp.einsum('ech,ehf->ecf', expert_in, w1), approximate=False)
            y = jnp.einsum('ecf,efh->ech', h, w2)
            tok = y.reshape(E * C, H)[jnp.minimum(slot, E * C - 1)]
            out = out + tok * (gate * keep.astype(x.dtype))[:, None]
        return out.reshape(B, T, H)

    def _L1_attn_ref(x, Wq, Wk, Wv, Wgamma, Wf, Wg1, Wg2, Wo, norm_w):
        import jax, jax.numpy as jnp
        import numpy as np
        B, N, D, H = (2, 256, 128, 16)
        HD = D // H

        def l2norm(x, eps=1e-12):
            n = jnp.sqrt(jnp.sum(x * x, axis=-1, keepdims=True))
            return x / jnp.maximum(n, eps)

        def dplr_delta_rule(q, k, v, a, gk):
            qm, km, vm, am, gm = (jnp.moveaxis(t, 1, 0) for t in (q, k, v, a, gk))

            def step(S, inp):
                qt, kt, vt, at, gkt = inp
                Sp = S * jnp.exp(gkt)[..., None]
                u = jnp.einsum('bhk,bhkv->bhv', at, Sp) + vt
                S = Sp + jnp.einsum('bhk,bhv->bhkv', kt, u)
                o = jnp.einsum('bhk,bhkv->bhv', qt, S)
                return (S, o)
            S0 = jnp.zeros((q.shape[0], q.shape[2], q.shape[3], v.shape[3]), q.dtype)
            _, o = jax.lax.scan(step, S0, (qm, km, vm, am, gm))
            return jnp.moveaxis(o, 0, 1)

        def _forward(x, Wq, Wk, Wv, Wgamma, Wf, Wg1, Wg2, Wo, norm_w):
            b, n, d = x.shape
            silu = jax.nn.silu
            q = silu(x @ Wq)
            k = silu(x @ Wk)
            v = silu(x @ Wv)
            log_f = jax.nn.log_sigmoid(x @ Wf)
            gamma = -jax.nn.sigmoid(x @ Wgamma)
            q = q.reshape(b, n, H, HD)
            k = l2norm(k.reshape(b, n, H, HD))
            v = v.reshape(b, n, H, HD)
            gk = jnp.broadcast_to(log_f[..., None], (b, n, H, HD))
            a = k * gamma[..., None] * jnp.exp(gk)
            out = dplr_delta_rule(q, k, v, a, gk)
            out = out.reshape(b, n, d)
            gate = jax.nn.sigmoid(x @ Wg1 @ Wg2)
            out = out * gate
            mu = jnp.mean(out, axis=-1, keepdims=True)
            var = jnp.mean(jnp.square(out - mu), axis=-1, keepdims=True)
            out = (out - mu) * jax.lax.rsqrt(var + 1e-05) * norm_w
            return out @ Wo
        return _forward(x, Wq, Wk, Wv, Wgamma, Wf, Wg1, Wg2, Wo, norm_w)

    def _L1_xattn_ref(q, k, v, attn_mask, Wq, bq, Wk, bk, Wv, bv, Wo, bo):
        import jax, jax.numpy as jnp
        import numpy as np
        D_MODEL = 128
        NUM_HEADS = 16
        D_H = D_MODEL // NUM_HEADS

        def _xavier(key, out_f, in_f):
            limit = np.sqrt(6.0 / (in_f + out_f))
            return jax.random.uniform(key, (out_f, in_f), jnp.float32, -limit, limit)
        B, S, _ = q.shape
        H, Dh = (NUM_HEADS, D_H)
        Q = jnp.einsum('bsd,ed->bse', q, Wq) + bq
        K = jnp.einsum('bsd,ed->bse', k, Wk) + bk
        V = jnp.einsum('bsd,ed->bse', v, Wv) + bv
        Qm = Q.reshape(B, S, H, Dh).transpose(0, 2, 1, 3)
        Km = K.reshape(B, -1, H, Dh).transpose(0, 2, 1, 3)
        Vm = V.reshape(B, -1, H, Dh).transpose(0, 2, 1, 3)
        scores = jnp.einsum('bhqd,bhkd->bhqk', Qm, Km) / jnp.sqrt(jnp.float32(Dh))
        fill = jnp.finfo(scores.dtype).min
        scores = jnp.where(attn_mask[:, None, :, :], scores, fill)
        attn = jax.nn.softmax(scores, axis=-1)
        A = jnp.einsum('bhqk,bhkd->bhqd', attn, Vm)
        A = A.transpose(0, 2, 1, 3).reshape(B, S, H * Dh)
        O = jnp.einsum('bsd,ed->bse', A, Wo) + bo
        return O

    def _L1_ffn_ref(hidden_states, gate_w, w1, w3, w2):
        import jax, jax.numpy as jnp
        import numpy as np
        E = 8
        K = 2
        H = 128
        F = 448
        B, S = (1, 256)
        b, s, h = hidden_states.shape
        x = hidden_states.reshape(-1, h)
        T = x.shape[0]
        router_logits = x @ gate_w.T
        routing_weights = jax.nn.softmax(router_logits.astype(jnp.float32), axis=-1)
        topk_w, topk_idx = jax.lax.top_k(routing_weights, K)
        topk_w = topk_w / jnp.sum(topk_w, axis=-1, keepdims=True)
        tok = jnp.arange(T)
        expert_weights = jnp.zeros((T, E), jnp.float32).at[tok[:, None], topk_idx].add(topk_w)
        g = jnp.einsum('th,efh->etf', x, w1)
        u = jnp.einsum('th,efh->etf', x, w3)
        act = jax.nn.silu(g) * u
        y = jnp.einsum('etf,ehf->eth', act, w2)
        out = jnp.einsum('eth,te->th', y, expert_weights.astype(y.dtype))
        return out.reshape(b, s, h)

    def _L2_attn_ref(x, w_q, b_q, w_k, b_k, v_w, out_w):
        import jax, jax.numpy as jnp
        import numpy as np
        D_MODEL = 128
        N_HEADS = 16
        D_HEAD = D_MODEL // N_HEADS
        LUT_SIZE = 512
        TWO_PI = 2.0 * np.pi
        SCALE = np.sqrt(2.0 * D_HEAD).astype(np.float32)
        _GRID = (TWO_PI * np.arange(LUT_SIZE) / LUT_SIZE).astype(np.float32)
        _SIN_TABLE = jnp.asarray(np.sin(_GRID))
        _COS_TABLE = jnp.asarray(np.cos(_GRID))

        def _lut_sin_cos(theta):
            idx = jnp.mod(jnp.round(theta * (LUT_SIZE / TWO_PI)).astype(jnp.int32), LUT_SIZE)
            return (_SIN_TABLE[idx], _COS_TABLE[idx])
        B, S, D = x.shape
        x_heads = x.reshape(B, S, N_HEADS, D_HEAD)
        theta_q = x_heads / (1.0 + jnp.abs(w_q)) + b_q
        sin_q, cos_q = _lut_sin_cos(theta_q)
        Q = jnp.concatenate([cos_q, sin_q], axis=-1)
        theta_k = x_heads / (1.0 + jnp.abs(w_k)) + b_k
        sin_k, cos_k = _lut_sin_cos(theta_k)
        K = jnp.concatenate([cos_k, sin_k], axis=-1)
        V = (x @ v_w.T).reshape(B, S, N_HEADS, D_HEAD)
        scores = jnp.einsum('bqhe,bkhe->bhqk', Q, K) / SCALE
        causal = jnp.triu(jnp.ones((S, S), dtype=bool), k=1)
        scores = jnp.where(causal, -jnp.inf, scores)
        attn = jax.nn.softmax(scores, axis=-1)
        out = jnp.einsum('bhqk,bkhd->bqhd', attn, V).reshape(B, S, D)
        return out @ out_w.T

    def _L2_xattn_ref(x, context, Wq, Wkv, Wproj, bproj):
        import jax, jax.numpy as jnp
        import numpy as np
        DIM = 128
        NUM_HEADS = 16
        HEAD_DIM = DIM // NUM_HEADS
        SCALE = HEAD_DIM ** (-0.5)
        B, T1, T2 = (4, 256, 256)
        Bx, T1x, C = x.shape
        T2x = context.shape[1]
        q = (x @ Wq.T).reshape(Bx, T1x, NUM_HEADS, HEAD_DIM).transpose(0, 2, 1, 3)
        kv = (context @ Wkv.T).reshape(Bx, T2x, 2, NUM_HEADS, HEAD_DIM)
        kv = kv.transpose(2, 0, 3, 1, 4)
        k, v = (kv[0], kv[1])
        attn = jnp.einsum('bhqd,bhkd->bhqk', q, k) * SCALE
        attn = jax.nn.softmax(attn, axis=-1)
        out = jnp.einsum('bhqk,bhkd->bhqd', attn, v)
        out = out.transpose(0, 2, 1, 3).reshape(Bx, T1x, C)
        return out @ Wproj.T + bproj

    def _L2_ffn_ref(x, Win, bin_, W1, b1, W2, b2, Wout, bout):
        import jax, jax.numpy as jnp
        import numpy as np
        D_MODEL = 128
        M = 64
        INNER = 16
        s = jnp.einsum('btd,dm->btm', x, Win) + bin_
        h = jax.nn.relu(s[..., None] * W1 + b1)
        g = jnp.einsum('btmh,mh->btm', h, W2) + b2
        out = jnp.einsum('btm,md->btd', g, Wout) + bout
        return out

    def _L3_attn_ref(x, ln_g, ln_b, W_in, b_in, conv_w, conv_b, A, W_B, b_B, W_C, b_C, D, W_out, b_out):
        import jax, jax.numpy as jnp
        import numpy as np
        B_, T_, D_MODEL = (2, 128, 128)
        D_STATE, D_CONV, EXPAND = (16, 4, 2)
        D_INNER = D_MODEL * EXPAND

        def _ssm_forward(x, ln_g, ln_b, W_in, b_in, conv_w, conv_b, A, W_B, b_B, W_C, b_C, D, W_out, b_out):
            eps = 1e-05
            mu = jnp.mean(x, axis=-1, keepdims=True)
            var = jnp.var(x, axis=-1, keepdims=True)
            xn = (x - mu) / jnp.sqrt(var + eps) * ln_g + ln_b
            proj = xn @ W_in + b_in
            xp, gate = jnp.split(proj, 2, axis=-1)
            xc = jax.lax.conv_general_dilated(xp.transpose(0, 2, 1), conv_w, window_strides=(1,), padding=[(D_CONV - 1, 0)], dimension_numbers=('NCH', 'OIH', 'NCH'), feature_group_count=D_INNER).transpose(0, 2, 1) + conv_b
            xc = jax.nn.silu(xc)
            Bt = xc @ W_B + b_B
            Ct = xc @ W_C + b_C
            a = jax.nn.sigmoid(A)
            u = Bt[:, :, None, :] * xc[:, :, :, None]
            a_full = jnp.broadcast_to(a, u.shape)

            def combine(c1, c2):
                a1, u1 = c1
                a2, u2 = c2
                return (a2 * a1, a2 * u1 + u2)
            _, h = jax.lax.associative_scan(combine, (a_full, u), axis=1)
            y = jnp.einsum('btns,bts->btn', h, Ct) + D * xc
            y = y * jax.nn.silu(gate)
            return y @ W_out + b_out + x
        return _ssm_forward(x, ln_g, ln_b, W_in, b_in, conv_w, conv_b, A, W_B, b_B, W_C, b_C, D, W_out, b_out)

    def _L3_xattn_ref(query, key, value, mask, attn_bias, Wq, bq, Wk, bk, Wv, bv, Wo, bo):
        import jax, jax.numpy as jnp
        import numpy as np
        DIM = 128
        NUM_HEADS = 16
        HEAD_DIM = DIM // NUM_HEADS
        SCALE = HEAD_DIM ** (-0.5)
        B, L, _ = query.shape
        S = key.shape[1]
        H, D = (NUM_HEADS, HEAD_DIM)
        q = (query @ Wq + bq).reshape(B, L, H, D).transpose(0, 2, 1, 3)
        k = (key @ Wk + bk).reshape(B, S, H, D).transpose(0, 2, 1, 3)
        v = (value @ Wv + bv).reshape(B, S, H, D).transpose(0, 2, 1, 3)
        scores = jnp.einsum('bhld,bhsd->bhls', q, k) * SCALE + attn_bias
        scores = jnp.where(mask == 0, -jnp.inf, scores)
        probs = jax.nn.softmax(scores, axis=-1)
        out = jnp.einsum('bhls,bhsd->bhld', probs, v)
        out = out.transpose(0, 2, 1, 3).reshape(B, L, DIM)
        return out @ Wo + bo

    def _L3_ffn_ref(x, router_w, router_b, w1, b1, w2, b2, sw1, sb1, sw2, sb2):
        import jax, jax.numpy as jnp
        import numpy as np
        B, S, D = (4, 64, 128)
        E, K, H = (64, 8, 32)
        ES, HS = (2, 256)
        b_, s_, d_ = x.shape
        xf = x.reshape(-1, d_)
        probs = jax.nn.softmax(xf @ router_w + router_b, axis=-1)
        tw, ti = jax.lax.top_k(probs, K)
        tw = tw / jnp.sum(tw, axis=-1, keepdims=True)

        def body(acc, p):
            W1, B1, W2, B2, e = p
            h = jax.nn.silu(xf @ W1 + B1) @ W2 + B2
            cw = jnp.sum(jnp.where(ti == e, tw, 0.0), axis=-1)
            return (acc + cw[:, None] * h, None)
        routed, _ = jax.lax.scan(body, jnp.zeros_like(xf), (w1, b1, w2, b2, jnp.arange(w1.shape[0])))

        def shared_mlp(W1, B1, W2, B2):
            return jax.nn.silu(xf @ W1 + B1) @ W2 + B2
        shared = jnp.sum(jax.vmap(shared_mlp)(sw1, sb1, sw2, sb2), axis=0)
        return (routed + shared).reshape(b_, s_, d_)
    x = _layernorm(x + _L0_attn_ref(x, L0_attn_Wq, L0_attn_bq, L0_attn_Wdown, L0_attn_bdown, L0_attn_Wup, L0_attn_bup, L0_attn_Wout, L0_attn_bout), axis=-1)
    x = _layernorm(x + _L0_xattn_ref(x, ctx_1024, L0_xattn_q_w, L0_xattn_q_b, L0_xattn_k_w, L0_xattn_k_b, L0_xattn_v_w, L0_xattn_v_b, L0_xattn_o_w, L0_xattn_o_b), axis=-1)
    x = _layernorm(x + _L0_ffn_ref(x, L0_ffn_router_w, L0_ffn_w1, L0_ffn_w2), axis=-1)
    x = _layernorm(x + _L1_attn_ref(x, L1_attn_Wq, L1_attn_Wk, L1_attn_Wv, L1_attn_Wgamma, L1_attn_Wf, L1_attn_Wg1, L1_attn_Wg2, L1_attn_Wo, L1_attn_norm_w), axis=-1)
    x = _layernorm(x + _L1_xattn_ref(x, ctx_1024, ctx_1024, mask_BxSxS2_bf1, L1_xattn_Wq, L1_xattn_bq, L1_xattn_Wk, L1_xattn_bk, L1_xattn_Wv, L1_xattn_bv, L1_xattn_Wo, L1_xattn_bo), axis=-1)
    x = _layernorm(x + _L1_ffn_ref(x, L1_ffn_gate_w, L1_ffn_w1, L1_ffn_w3, L1_ffn_w2), axis=-1)
    x = _layernorm(x + _L2_attn_ref(x, L2_attn_w_q, L2_attn_b_q, L2_attn_w_k, L2_attn_b_k, L2_attn_v_w, L2_attn_out_w), axis=-1)
    x = _layernorm(x + _L2_xattn_ref(x, ctx_1024, L2_xattn_Wq, L2_xattn_Wkv, L2_xattn_Wproj, L2_xattn_bproj), axis=-1)
    x = _layernorm(x + _L2_ffn_ref(x, L2_ffn_Win, L2_ffn_bin_, L2_ffn_W1, L2_ffn_b1, L2_ffn_W2, L2_ffn_b2, L2_ffn_Wout, L2_ffn_bout), axis=-1)
    x = _layernorm(x + _L3_attn_ref(x, L3_attn_ln_g, L3_attn_ln_b, L3_attn_W_in, L3_attn_b_in, L3_attn_conv_w, L3_attn_conv_b, L3_attn_A, L3_attn_W_B, L3_attn_b_B, L3_attn_W_C, L3_attn_b_C, L3_attn_D, L3_attn_W_out, L3_attn_b_out), axis=-1)
    x = _layernorm(x + _L3_xattn_ref(x, ctx_1024, ctx_1024, mask_Bx1xSxS2_ik1, fside_Bx16xSxS2_0, L3_xattn_Wq, L3_xattn_bq, L3_xattn_Wk, L3_xattn_bk, L3_xattn_Wv, L3_xattn_bv, L3_xattn_Wo, L3_xattn_bo), axis=-1)
    x = _layernorm(x + _L3_ffn_ref(x, L3_ffn_router_w, L3_ffn_router_b, L3_ffn_w1, L3_ffn_b1, L3_ffn_w2, L3_ffn_b2, L3_ffn_sw1, L3_ffn_sb1, L3_ffn_sw2, L3_ffn_sb2), axis=-1)
    return x

_drawn_inputs = setup_inputs


def setup_inputs(seed=0):
    import zlib

    import numpy as np

    out = dict(_drawn_inputs(seed))
    spreads = {'L0_attn_bq': (0.0, 0.1),
     'L0_attn_bdown': (0.0, 0.1),
     'L0_attn_bup': (0.0, 0.1),
     'L0_attn_bout': (0.0, 0.1),
     'L1_attn_norm_w': (1.0, 0.2),
     'L1_xattn_bq': (0.0, 0.1),
     'L1_xattn_bk': (0.0, 2.0),
     'L1_xattn_bv': (0.0, 0.1),
     'L1_xattn_bo': (0.0, 0.1),
     'L2_attn_b_q': (0.0, 0.8),
     'L2_attn_b_k': (0.0, 0.8),
     'L3_attn_ln_g': (1.0, 0.6),
     'L3_attn_ln_b': (0.0, 0.8),
     'L3_attn_D': (1.0, 0.6),
     'L3_ffn_router_b': (0.0, 0.342),
     'L3_ffn_b1': (0.0, 0.8),
     'L3_ffn_b2': (0.0, 0.1),
     'L3_ffn_sb1': (0.0, 0.367),
     'L3_ffn_sb2': (0.0, 0.1)}
    factors = {'L0_xattn_q_b': 5.63,
     'L0_xattn_k_b': 64.0,
     'L1_attn_Wgamma': 7.933,
     'L1_attn_Wg1': 7.022,
     'L1_attn_Wg2': 7.642,
     'L2_attn_w_q': 25.414,
     'L2_attn_w_k': 22.517,
     'L2_xattn_Wq': 22.565,
     'L2_xattn_bproj': 2.726,
     'L2_ffn_bin_': 8.0,
     'L3_attn_W_in': 8.0,
     'L3_attn_b_in': 8.0,
     'L3_attn_conv_w': 8.0,
     'L3_attn_conv_b': 8.0,
     'L3_attn_A': 8.0,
     'L3_attn_W_B': 8.0,
     'L3_attn_b_B': 8.0,
     'L3_attn_W_C': 8.0,
     'L3_attn_b_C': 8.0,
     'L3_attn_W_out': 8.0,
     'L3_attn_b_out': 17.126,
     'L3_xattn_bq': 8.0,
     'L3_xattn_bk': 64.0,
     'L3_xattn_bo': 3.472,
     'L3_ffn_w1': 8.0,
     'L3_ffn_w2': 8.0}
    for name, (base, spread) in spreads.items():
        noise = np.random.default_rng([zlib.crc32(name.encode()), seed]).standard_normal(out[name].shape)
        drawn = base * np.exp(spread * noise) if base else spread * noise
        out[name] = jnp.asarray(drawn.astype(out[name].dtype))
    for name, factor in factors.items():
        out[name] = (out[name] * factor).astype(out[name].dtype)
    return out
```

```python
from contextlib import ExitStack

import concourse.bass as bass
from concourse import mybir

F32 = mybir.dt.float32
BF16 = mybir.dt.bfloat16
I32 = mybir.dt.int32
U8 = mybir.dt.uint8
ALU = mybir.AluOpType
ACT = mybir.ActivationFunctionType
AXX = mybir.AxisListType.X

P = 128
B = 32
T = 128
D = 128
H = 16
HD = 8
S2 = 120
U = 4
NIT = B // U
W = U * T
CH = 4
EPS = 1e-5
MASKED = -1.0e30


class Phase:

    def __init__(self, nc, name):
        self.nc, self.name, self.ctx, self.sems = nc, name, ExitStack(), []

    def sb(self, name, shape, dt=F32):
        return self.ctx.enter_context(self.nc.sbuf_tensor(f"{self.name}_{name}", shape, dt))

    def ps(self, name, shape, dt=F32):
        return self.ctx.enter_context(self.nc.psum_tensor(f"{self.name}_ps_{name}", shape, dt))

    def sem(self, name):
        s = self.ctx.enter_context(self.nc.semaphore(f"{self.name}_{name}"))
        self.sems.append(s)
        return s

    def close(self):
        for s in self.sems:
            self.nc.sync.sem_clear(s)
        self.nc.all_engine_barrier()
        self.ctx.close()


def bcast(ap, axis, n):
    a = ap.unsqueeze(axis)
    shape = list(a.shape)
    shape[axis] = n
    return a.broadcast_to(shape)


class Rows:

    def __init__(self, ph, x):
        self.x = x
        self.xs = ph.sb("x_rows", [P, U, D])
        self.ready = ph.sem("rows_ready")
        self.free = ph.sem("rows_free")

    def gpsimd(self, pool, i, first=False):
        if not first:
            pool.wait_ge(self.free, i)
        pool.tensor_copy(self.xs[:, :, :], self.x[:, bass.ds(i * U, U), :]).then_inc(self.ready, 1)

    def tensor(self, pe, i, out, ident):
        pe.wait_ge(self.ready, i + 1)
        for u in range(U):
            mm = pe.transpose(out[:, u * T:(u + 1) * T], self.xs[:, u, :], ident)
        mm.then_inc(self.free, 1)


class Stats:

    def __init__(self, ph, consts, tag=""):
        self.c = consts
        self.st = ph.sb(tag + "bnst", [P, U, 6])
        self.mv = ph.sb(tag + "meanvar", [P, U, 2])
        self.ve = ph.sb(tag + "vareps", [P, U])
        self.rstd = ph.sb(tag + "rstd", [P, U])
        self.st_ready = ph.sem(tag + "bnst_ready")
        self.mv_ready = ph.sem(tag + "meanvar_ready")
        self.ve_ready = ph.sem(tag + "vareps_ready")
        self.rstd_ready = ph.sem(tag + "rstd_ready")

    def vector(self, dve, i, r):
        for u in range(U):
            dve.bn_stats(self.st[:, u, :], r[:, u, :]).then_inc(self.st_ready, 1)
        dve.wait_ge(self.st_ready, i * U + U)
        dve.memset(self.ve[:, :], EPS)
        for u in range(U):
            dve.bn_aggr(self.mv[:, u, :], self.st[:, u, :]).then_inc(self.mv_ready, 1)
        dve.wait_ge(self.mv_ready, i * U + U)
        dve.tensor_scalar(self.ve[:, :], self.mv[:, :, 1], EPS, None, ALU.add).then_inc(self.ve_ready, 1)

    def gpsimd(self, pool, i):
        pool.wait_ge(self.ve_ready, i + 1)
        pool.tensor_tensor(self.rstd[:, :], self.ve[:, :], self.c["neghalf"][:, 0:U],
                           ALU.pow).then_inc(self.rstd_ready, 1)


class Norm:

    def __init__(self, ph, x, consts, y, x_times=1.0):
        self.x, self.y, self.x_times = x, y, x_times
        self.r = ph.sb("resid", [P, U, D])
        self.stats = Stats(ph, consts)
        self.y_ready = ph.sem("y_ready")
        self.r_ready = ph.sem("resid_ready")
        self.x_done = ph.sem("x_done")

    def vector(self, dve, i):
        n = self
        dve.wait_ge(n.y_ready, i + 1)
        dve.scalar_tensor_tensor(n.r[:, :, :].rearrange("p u d -> p (u d)"),
                                 n.x[:, bass.ds(i * U, U), :].rearrange("p u d -> p (u d)"), n.x_times,
                                 n.y[:, :], ALU.mult, ALU.add).then_inc(n.r_ready, 1)
        dve.wait_ge(n.r_ready, i + 2)
        n.finish(dve, i)

    def finish(self, dve, i):
        n = self
        n.stats.vector(dve, i, n.r)
        dve.wait_ge(n.stats.rstd_ready, i + 1)
        for u in range(U):
            dve.tensor_scalar(n.x[:, bass.ds(i * U + u, 1), :].rearrange("p a d -> p (a d)"), n.r[:, u, :],
                              n.stats.mv[:, u, 0:1], n.stats.rstd[:, u:u + 1],
                              ALU.subtract, ALU.mult).then_inc(n.x_done, 1)
        dve.wait_ge(n.x_done, i * U + U)

    def gpsimd(self, pool, i):
        self.stats.gpsimd(pool, i)


def pick(w, table, name):
    rows, off, cols = table[name]
    return w[0:rows, off:off + cols]


def piecewise_phase(nc, x, consts, blob, table):
    ph = Phase(nc, "pw")
    NJ = 8
    w = ph.sb("w", list(blob.shape))
    xT = ph.sb("xT", [P, W])
    s = ph.sb("s", [P, W])
    h = ph.sb("h", [P, NJ, W])
    wc = ph.sb("wc", [P, NJ, D])
    pj = ph.ps("pj", [P, 2, W])
    y = ph.ps("y", [P, W])
    nm = Norm(ph, x, consts, y)
    rows = Rows(ph, x)
    w_in, xt, s_ps, s_sb, h_sb, wc_sb = (ph.sem(n) for n in (
        "w_loaded", "xT_ready", "s_in_psum", "s_ready", "h_ready", "outweights_ready"))
    Win, bin_ = pick(w, table, "Win"), pick(w, table, "bin")
    W1, b1, W2 = pick(w, table, "W1"), pick(w, table, "b1"), pick(w, table, "W2")
    Wout, b2, bout = pick(w, table, "Wout"), pick(w, table, "b2"), pick(w, table, "bout")

    with nc.Block() as block:
        @block.sync
        def _(sp):
            sp.dma_start(w[:, :], blob).then_inc(w_in, 16)

        @block.gpsimd
        def _(pool):
            rows.gpsimd(pool, 0, first=True)
            with pool.Fori(0, NIT - 1) as i:
                rows.gpsimd(pool, i + 1)
                nm.gpsimd(pool, i)
            nm.gpsimd(pool, NIT - 1)

        @block.tensor
        def _(pe):
            pe.wait_ge(w_in, 16)
            with pe.Fori(0, NIT) as i:
                rows.tensor(pe, i, pj[:, 0, :], consts["ident"][:, :])
                pe.wait_ge(xt, i + 1)
                pe.matmul(pj[:, 1, :], Win, xT[:, :], start=True, stop=True).then_inc(s_ps, 1)
                pe.wait_ge(nm.r_ready, i + 1)
                pe.wait_ge(wc_sb, NJ + 1)
                for u in range(U):
                    yu = y[:, u * D:(u + 1) * D]
                    pe.matmul(yu, consts["ones"][0:1, 0:P], bout, start=True, stop=False)
                    pe.matmul(yu, b2, Wout, start=False, stop=False)
                    for j in range(NJ):
                        if u == 0:
                            pe.wait_ge(h_sb, i * NJ + j + 1)
                        mm = pe.matmul(yu, h[:, j, u * T:(u + 1) * T], wc[:, j, :],
                                       start=False, stop=(j == NJ - 1))
                mm.then_inc(nm.y_ready, 1)

        @block.scalar
        def _(act):
            act.wait_ge(w_in, 16)
            with act.Fori(0, NIT) as i:
                act.wait_ge(rows.free, i + 1)
                act.activation(xT[:, :], pj[:, 0, :], ACT.Copy).then_inc(xt, 1)
                act.wait_ge(s_ps, i + 1)
                act.activation(s[:, :], pj[:, 1, :], ACT.Identity, bias=bin_).then_inc(s_sb, 1)
                act.wait_ge(s_sb, i + 1)
                for j in range(NJ):
                    act.activation(h[:, j, :], s[:, :], ACT.Relu, scale=W1[:, j:j + 1],
                                   bias=b1[:, j:j + 1]).then_inc(h_sb, 1)

        @block.vector
        def _(dve):
            dve.sem_inc(nm.r_ready, 1)
            dve.wait_ge(w_in, 16)
            for j in range(NJ):
                dve.tensor_scalar(wc[:, j, :], pick(w, table, "Wout2"), W2[:, j:j + 1], None,
                                  ALU.mult).then_inc(wc_sb, 1)
            dve.sem_inc(wc_sb, 1)
            with dve.Fori(0, NIT) as i:
                nm.vector(dve, i)
    ph.close()


def attention_phase(nc, name, x, consts, t, blob, table, *, scale, bias=None, lut=False):
    ph = Phase(nc, name)
    NK = T if lut else S2
    R = 2 * HD if lut else HD
    NU = U * 4
    SB = 3
    KW = U * NK
    w = ph.sb("w", list(blob.shape))
    xT = ph.sb("xT", [P, W])
    qP = ph.sb("q", [P, CH, W])
    kP = ph.sb("k", [P, CH, KW])
    V = ph.sb("v", [NK, U, H, HD + 1])
    TR = 4
    S_sb = ph.sb("scores", [P, TR, CH, NK])
    mx = ph.sb("max", [P, TR, 4])
    PT = ph.sb("weightsT", [NK, TR, 4, T])
    rden = ph.sb("rden", [P, U, H])
    o = ph.sb("o", [P, U, D])
    oT = ph.sb("oT", [P, U, T])
    s_ps = ph.ps("s", [P, SB, CH, T])
    pj = s_ps[:, :, :, :].rearrange("p b c t -> p b (c t)")
    t_ps = ph.ps("t", [P, 2, 4, T])
    o_ps = ph.ps("o", [P, 2, 512])
    y = ph.ps("y", [P, W])
    ov = lambda u: o_ps[:, u % 2, 0:H * (HD + 1)].rearrange("p (h e) -> p h e", e=HD + 1)
    ot_ps = lambda u: y[:, u * D:(u + 1) * D]
    rows = Rows(ph, x)
    nm = Norm(ph, x, consts, y)
    ident = consts["ident"][:, :]
    (w_in, v_one, pj_ready, pj_done, s_ready, b_ready, m_ready, sub_ready, e_ready, t_ready,
     pt_ready, o_ready, rd_ready, on_ready, ot_ready, ott_ready) = (ph.sem(n) for n in (
         "w_loaded", "ones_ready", "pj_ready", "pj_done", "s_ready", "biased_ready", "max_ready",
         "shifted_ready", "exp_ready", "t_ready", "pt_ready", "o_ready",
         "rden_ready", "normed_ready", "ot_in_psum", "ot_ready"))
    BANKS = 4
    s_done = b_ready if bias else sub_ready
    pw = lambda n: pick(w, table, n)
    if not lut:
        ctx = ph.sb("ctx", [P, KW])
        ctx_in = ph.sem("ctx_loaded")
    if bias in ("rows", "heads"):
        m_raw = ph.sb("mask_raw", [P, U, NK], t[name + "_mask"].dtype)
        m_bias = ph.sb("mask_bias", [P, U, NK])
        m_in, mb_ready = ph.sem("mask_loaded"), ph.sem("maskbias_ready")
    if bias == "heads":
        FR = 4
        fb = ph.sb("headbias", [P, FR, 4, NK])
        fb_in = [ph.sem(f"headbias_loaded{r}") for r in range(FR)]
        fb_sum = ph.sem("headbias_masked")
    if lut:
        TWO_PI_INV = 512.0 / 6.283185307179586
        ANG = 6.283185307179586 / 512.0
        MAGIC = 12582912.0
        NA = 2
        ang = ph.sb("angle", [P, NA, W])
        kk = ph.sb("index", [P, NA, 2, W])
        rr = ph.sb("turns", [P, NA, 2, W])
        sc = ph.sb("cossin", [P, NA, 2, W])
        (a_ready, k_ready, r1_ready, r2_ready, i_ready, cs_ready, den_ready) = (ph.sem(n) for n in (
            "angle_ready", "index_ready", "turns_raw", "turns_ready", "wrapped_ready", "cossin_ready", "rwidth_ready"))
        den = ph.sb("rwidth", [P, 2])
    NJ = 1 + CH + CH + 1

    LAG = 8

    with nc.Block() as block:
        @block.sync
        def _(sp):
            sp.dma_start(w[:, :], blob).then_inc(w_in, 16)
            with sp.Fori(0, NIT) as i:
                if not lut:
                    sp.wait_ge(pj_done, i * NJ + 1)
                    sp.dma_start(ctx[:, :], t["ctxT"][:, bass.ds(i * KW, KW)]).then_inc(ctx_in, 16)
                if bias in ("rows", "heads"):
                    sp.wait_ge(mb_ready, i + 1)
                    sp.dma_start(m_raw[:, :, :], t[name + "_mask"][bass.ds(i * U, U)].rearrange("u q k -> q u k")
                                 ).then_inc(m_in, 16)
                if bias == "heads":
                    for n in range(NU):
                        sp.wait_ge(b_ready, i * NU + n + 1)
                        sp.dma_start(fb[:, n % FR, :, :],
                                     t["fside"][bass.ds(i * U + n // 4, 1), n % 4:H:4]
                                     .rearrange("a h q k -> q (a h) k")).then_inc(fb_in[n % FR], 16)

        @block.gpsimd
        def _(pool):
            if bias == "heads":
                pool.sem_inc(fb_sum, 1)
            pool.memset(V[:, :, :, HD:HD + 1], 1.0).then_inc(v_one, 1)

            def masked_bias(i):
                if bias == "heads":
                    for n in range(NU):
                        pool.wait_ge(mb_ready, i + 2)
                        pool.wait_ge(fb_in[n % FR], (i * (NU // FR) + n // FR + 1) * 16)
                        pool.tensor_tensor(fb[:, n % FR, :, :], fb[:, n % FR, :, :],
                                           bcast(m_bias[:, n // 4, :], 1, 4), ALU.add).then_inc(fb_sum, 1)

            rows.gpsimd(pool, 0, first=True)
            with pool.Fori(0, NIT - 1) as i:
                rows.gpsimd(pool, i + 1)
                masked_bias(i)
                nm.gpsimd(pool, i)
            masked_bias(NIT - 1)
            nm.gpsimd(pool, NIT - 1)

        @block.tensor
        def _(pe):
            pe.sem_inc(t_ready, TR)
            pe.wait_ge(w_in, 16)

            def slot(i, j):
                if j < SB:
                    pe.wait_ge(s_done, i * NU + BANKS)
                else:
                    pe.wait_ge(pj_done, i * NJ + j - SB + 2)
                return pj[:, j % SB, :]

            with pe.Fori(0, NIT) as i:
                rows.tensor(pe, i, slot(i, 0), ident)
                if lut:
                    pe.wait_ge(cs_ready, i * 2 + 2)
                    for a in range(NA):
                        for c in range(CH):
                            bank = slot(i, 1 + a * CH + c)
                            pe.matmul(bank, pw("cos_sel")[:, c * P:(c + 1) * P], sc[:, a, 0, :], start=True, stop=False)
                            pe.matmul(bank, pw("sin_sel")[:, c * P:(c + 1) * P], sc[:, a, 1, :], start=False,
                                      stop=True).then_inc(pj_ready, 1)
                else:
                    pe.wait_ge(pj_done, i * NJ + 2)
                    for c in range(CH):
                        pe.matmul(slot(i, 1 + c), pw("wq")[:, c * P:(c + 1) * P], xT[:, :], start=True,
                                  stop=True).then_inc(pj_ready, 1)
                    pe.wait_ge(ctx_in, i * 16 + 16)
                    for c in range(CH):
                        pe.matmul(slot(i, 1 + CH + c)[:, 0:KW], pw("wk")[:, c * P:(c + 1) * P], ctx[:, :], start=True,
                                  stop=True).then_inc(pj_ready, 1)
                bank = slot(i, NJ - 1)
                for u in range(U):
                    src = xT[:, u * T:(u + 1) * T] if lut else ctx[:, u * NK:(u + 1) * NK]
                    vu = bank[0:NK, u * D:(u + 1) * D]
                    if not lut:
                        pe.matmul(vu, consts["ones"][0:1, 0:NK], pw("bv"), start=True, stop=False)
                    mm = pe.matmul(vu, src, pw("wv"), start=lut, stop=True)
                mm.then_inc(pj_ready, 1)
                pe.wait_ge(pj_done, i * NJ + NJ + 1)
                for n in range(NU + LAG):
                    if n < NU:
                        u, j = n // 4, n % 4
                        if n >= SB:
                            pe.wait_ge(s_done, i * NU + n - SB + 1 + BANKS)
                        for c in range(CH):
                            mm = pe.matmul(s_ps[:, n % SB, c, 0:NK], qP[32 * j:32 * j + R, c, u * T:(u + 1) * T],
                                           kP[32 * j:32 * j + R, c, u * NK:(u + 1) * NK], start=True, stop=True)
                        mm.then_inc(s_ready, 1)
                    m = n - 2
                    if 0 <= m < NU:
                        pe.wait_ge(e_ready, i * NU + m + 1)
                        pe.wait_ge(pt_ready, i * NU + m + 1)
                        for j in range(4):
                            mm = pe.transpose(t_ps[0:NK, m % 2, j, :], S_sb[:, m % TR, j, :], ident)
                        mm.then_inc(t_ready, 1)
                    m = n - 4
                    if 0 <= m < NU:
                        u, j = m // 4, m % 4
                        pe.wait_ge(pt_ready, i * NU + m + 3)
                        if j == 0:
                            pe.wait_ge(on_ready, i * U + u + 1)
                        for c in range(CH):
                            mm = pe.matmul(ov(u)[:, c * 4 + j, :], PT[:, m % TR, c, :], V[:, u, c * 4 + j, :],
                                           start=True, stop=True)
                        mm.then_inc(o_ready, 1)
                    m = n - 6
                    if m >= 0 and m % CH == CH - 1 and m < NU:
                        u = m // CH
                        pe.wait_ge(on_ready, i * U + u + 3)
                        if u == 0:
                            pe.wait_ge(nm.r_ready, i + 1)
                        pe.transpose(ot_ps(u), o[:, u, :], ident).then_inc(ot_ready, 1)
                    m = n - 8
                    if m >= 0 and m % CH == CH - 1:
                        u = m // CH
                        pe.wait_ge(ott_ready, i * U + u + 1)
                        yu = y[:, u * D:(u + 1) * D]
                        if "bo" in table:
                            pe.matmul(yu, consts["ones"][0:1, 0:P], pw("bo"), start=True, stop=False)
                        mm = pe.matmul(yu, oT[:, u, :], pw("wo"), start="bo" not in table, stop=True)
                        if u == U - 1:
                            mm.then_inc(nm.y_ready, 1)

        @block.scalar
        def _(act):
            act.sem_inc(pj_done, 1)
            act.sem_inc(pt_ready, 2)
            act.wait_ge(w_in, 16)
            act.wait_ge(v_one, 1)
            with act.Fori(0, NIT) as i:
                act.wait_ge(rows.free, i + 1)
                act.activation(xT[:, :], pj[:, 0, :], ACT.Copy).then_inc(pj_done, 1)
                if lut:
                    for a in range(NA):
                        act.wait_ge(i_ready, i * NA + a + 1)
                        act.activation(sc[:, a, :, :], kk[:, a, :, :], ACT.Sin, scale=ANG).then_inc(cs_ready, 1)
                for j in range(1, NJ):
                    act.wait_ge(pj_ready, i * (NJ - 1) + j)
                    bank = pj[:, j % SB, :]
                    if j < 1 + CH:
                        dst, src, b = qP[:, j - 1, :], bank, "bq"
                    elif j < 1 + 2 * CH:
                        dst, src, b = kP[:, j - 1 - CH, :], bank[:, 0:KW], "bk"
                    else:
                        dst = V[:, :, :, 0:HD]
                        src, b = bank[0:NK, :].rearrange("p (u h e) -> p u h e", u=U, h=H), None
                    if b in table:
                        act.activation(dst, src, ACT.Identity,
                                       bias=pw(b)[:, (j - 1) % CH:(j - 1) % CH + 1]).then_inc(pj_done, 1)
                    else:
                        act.activation(dst, src, ACT.Copy).then_inc(pj_done, 1)
                for n in range(NU + LAG):
                    if n < NU:
                        act.wait_ge(sub_ready, i * NU + n + 1 + (0 if bias else BANKS))
                        act.activation(S_sb[:, n % TR, :, :], S_sb[:, n % TR, :, :], ACT.Exp,
                                       scale=(1.0 if bias else scale)).then_inc(e_ready, 1)
                    m = n - 2
                    if 0 <= m < NU:
                        act.wait_ge(t_ready, i * NU + m + 1 + TR)
                        act.activation(PT[:, m % TR, :, :], t_ps[0:NK, m % 2, :, :], ACT.Copy
                                       ).then_inc(pt_ready, 1)
                    m = n - 6
                    if m >= 0 and m % CH == CH - 1 and m < NU:
                        u = m // CH
                        act.wait_ge(ot_ready, i * U + u + 1)
                        act.activation(oT[:, u, :], ot_ps(u), ACT.Copy).then_inc(ott_ready, 1)

        @block.vector
        def _(dve):
            dve.sem_inc(nm.r_ready, 1)
            dve.sem_inc(s_done, BANKS)
            dve.sem_inc(on_ready, 2)
            dve.wait_ge(w_in, 16)
            if bias in ("rows", "heads"):
                dve.sem_inc(mb_ready, 1)
            if lut:
                dve.tensor_scalar(den[:, :], pw("wid"), -1.0, None, ALU.mult).then_inc(den_ready, 1)
                dve.wait_ge(den_ready, 1)
                dve.tensor_tensor(den[:, :], den[:, :], pw("wid"), ALU.max).then_inc(den_ready, 1)
                dve.wait_ge(den_ready, 2)
                dve.tensor_scalar(den[:, :], den[:, :], 1.0, None, ALU.add).then_inc(den_ready, 1)
                dve.wait_ge(den_ready, 3)
                dve.reciprocal(den[:, :], den[:, :]).then_inc(den_ready, 1)
                dve.wait_ge(den_ready, 4)
            with dve.Fori(0, NIT) as i:
                if lut:
                    dve.wait_ge(pj_done, i * NJ + 2)
                    for a in range(NA):
                        dve.tensor_scalar(ang[:, a, :], xT[:, :], den[:, a:a + 1], pw("shift")[:, a:a + 1],
                                          ALU.mult, ALU.add).then_inc(a_ready, 1)
                    for a in range(NA):
                        dve.wait_ge(a_ready, i * NA + a + 1)
                        for f in range(2):
                            dve.tensor_scalar(rr[:, a, f, :], ang[:, a, :], TWO_PI_INV, MAGIC, ALU.mult,
                                              ALU.add).then_inc(k_ready, 1)
                    for a in range(NA):
                        dve.wait_ge(k_ready, i * 2 * NA + 2 * a + 2)
                        for f in range(2):
                            dve.tensor_scalar(kk[:, a, f, :], rr[:, a, f, :], -MAGIC, 128.0 * (1 - f), ALU.add,
                                              ALU.add).then_inc(r1_ready, 1)
                    for a in range(NA):
                        dve.wait_ge(r1_ready, i * 2 * NA + 2 * a + 2)
                        dve.tensor_scalar(rr[:, a, :, :], kk[:, a, :, :], 1.0 / 512, MAGIC, ALU.mult,
                                          ALU.add).then_inc(r2_ready, 1)
                    for a in range(NA):
                        dve.wait_ge(r2_ready, i * 2 * NA + a + 1)
                        dve.tensor_scalar(rr[:, a, :, :], rr[:, a, :, :], -MAGIC, -512.0, ALU.add,
                                          ALU.mult).then_inc(r2_ready, 1)
                    for a in range(NA):
                        dve.wait_ge(r2_ready, i * 2 * NA + NA + a + 1)
                        dve.tensor_tensor(kk[:, a, :, :], kk[:, a, :, :], rr[:, a, :, :],
                                          ALU.add).then_inc(i_ready, 1)
                if bias in ("rows", "heads"):
                    dve.wait_ge(m_in, i * 16 + 16)
                    if bias == "heads":
                        dve.wait_ge(fb_sum, i * NU + 1)
                    dve.tensor_scalar(m_bias[:, :, :], m_raw[:, :, :], 0.0, MASKED, ALU.is_equal,
                                      ALU.mult).then_inc(mb_ready, 1)
                    dve.wait_ge(mb_ready, i + 2)
                for n in range(NU + LAG):
                    if n < NU:
                        u = n // 4
                        sc_n = S_sb[:, n % TR, :, :]
                        src = s_ps[:, n % SB, :, 0:NK]
                        dve.wait_ge(s_ready, i * NU + n + 1)
                        dve.wait_ge(t_ready, i * NU + n + 1)
                        if bias:
                            if bias == "causal":
                                add = bcast(pw("causal"), 1, 4)
                            elif bias == "rows":
                                add = bcast(m_bias[:, u, :], 1, 4)
                            else:
                                dve.wait_ge(fb_sum, i * NU + n + 2)
                                add = fb[:, n % FR, :, :]
                            dve.scalar_tensor_tensor(sc_n, src, scale, add, ALU.mult, ALU.add).then_inc(b_ready, 1)
                            dve.wait_ge(b_ready, i * NU + n + 1 + BANKS)
                            src = sc_n
                        dve.tensor_reduce(mx[:, n % TR, :], src, AXX, ALU.max).then_inc(m_ready, 1)
                        dve.wait_ge(m_ready, i * NU + n + 1)
                        dve.tensor_tensor(sc_n, src, bcast(mx[:, n % TR, :], 2, NK), ALU.subtract
                                          ).then_inc(sub_ready, 1)
                    m = n - 5
                    if m >= 0 and m % CH == CH - 1 and m < NU:
                        u = m // CH
                        dve.wait_ge(o_ready, i * NU + m + 1)
                        dve.reciprocal(rden[:, u, :], ov(u)[:, :, HD]).then_inc(rd_ready, 1)
                        dve.wait_ge(rd_ready, i * U + u + 1)
                        dve.tensor_tensor(o[:, u, :].rearrange("p (h e) -> p h e", h=H), ov(u)[:, :, 0:HD],
                                          bcast(rden[:, u, :], 2, HD), ALU.mult).then_inc(on_ready, 1)
                nm.vector(dve, i)
    ph.close()


def top_one(dve, wait, ready, base, pr, best, eq, cum, reset, onehot):
    E = pr.shape[2]
    dve.tensor_reduce(best, pr, AXX, ALU.max).then_inc(ready, 1)
    dve.wait_ge(ready, base + 1)
    dve.tensor_tensor(eq, pr, bcast(best, 2, E), ALU.is_equal).then_inc(ready, 1)
    dve.wait_ge(ready, base + 2)
    dve.tensor_tensor_scan(cum.rearrange("p u e -> p (u e)"), reset, eq.rearrange("p u e -> p (u e)"), 0.0,
                           ALU.mult, ALU.add).then_inc(ready, 1)
    dve.wait_ge(ready, base + 3)
    dve.scalar_tensor_tensor(onehot, cum, 1.0, eq, ALU.is_equal, ALU.mult).then_inc(ready, 1)
    dve.wait_ge(ready, base + 4)


def moe_phase(nc, name, x, consts, blob, table, *, F, gated, capacity=None):
    ph = Phase(nc, name)
    E, FC = 8, 4
    FW = F // FC
    HR = 4
    w = ph.sb("w", list(blob.shape))
    xT = ph.sb("xT", [P, W])
    G = ph.sb("hidden", [FW, 2, FC, W])
    small = lambda n, shape=(P, U, E): ph.sb(n, list(shape))
    pr, p2, eq, cum, cw = (small(n) for n in ("probs", "rest", "equal", "cumul", "share"))
    oh, kept, part = (small(n, (P, U, 2, E)) for n in ("onehot", "kept", "gated"))
    v = small("best", (P, U, 2))
    gate = small("gate", (P, U, 2))
    m1, sm, rs, ss, rss = (small(n, (P, U)) for n in ("lmax", "lsum", "rlsum", "vsum", "rvsum"))
    run = small("run", (P, 2, E))
    misc = ph.ps("misc", [P, 512])
    rt = ph.ps("router", [P, 512])
    h_ps = ph.ps("h", [P, HR, W])
    ye = ph.ps("ye", [P, 2, W])
    rows = Rows(ph, x)
    nm = Norm(ph, x, consts, None)
    (w_in, xt, lg_ready, rstep, ex_ready, oh_ready, pos_ready, run_ready, h_ready, act_ready, g_ready, ye_ready,
     acc_ready, cw_ready) = (ph.sem(n) for n in (
         "w_loaded", "xT_ready", "logits_ready", "router_step", "exp_ready", "onehot_ready", "pos_ready", "run_ready",
         "h_ready", "act_ready", "hidden_ready", "ye_ready", "acc_ready", "share_ready"))
    pw = lambda n: pick(w, table, n)
    RS = 19
    NH = 2 if gated else 1
    NHE = E * FC * NH
    cw2 = ph.sem("weights_ready")
    if gated:
        a_sb = ph.sb("silu", [FW, 2, W])

    def w1(e, f, k):
        o = (e * FC + f) * FW
        return pw("w1" if k == 0 else "w3")[:, o:o + FW]

    with nc.Block() as block:
        @block.sync
        def _(sp):
            sp.dma_start(w[:, :], blob).then_inc(w_in, 16)

        @block.gpsimd
        def _(pool):
            rows.gpsimd(pool, 0, first=True)
            with pool.Fori(0, NIT - 1) as i:
                rows.gpsimd(pool, i + 1)
                nm.gpsimd(pool, i)
            nm.gpsimd(pool, NIT - 1)

        @block.tensor
        def _(pe):
            pe.wait_ge(w_in, 16)
            with pe.Fori(0, NIT) as i:
                rows.tensor(pe, i, misc, consts["ident"][:, :])
                pe.wait_ge(xt, i + 1)
                for u in range(U):
                    mm = pe.matmul(rt[:, u * E:(u + 1) * E], xT[:, u * T:(u + 1) * T], pw("router"), start=True,
                                   stop=True)
                mm.then_inc(lg_ready, 1)

                def hidden(e):
                    for f in range(FC):
                        for k in range(NH):
                            n = (e * FC + f) * NH + k
                            if gated:
                                pe.wait_ge(g_ready, i * E * FC + (e * FC + f) + 1)
                            else:
                                pe.wait_ge(g_ready, i * NHE + n + 1)
                            pe.matmul(h_ps[0:FW, n % HR, :], w1(e, f, k), xT[:, :], start=True,
                                      stop=True).then_inc(h_ready, 1)

                def down(e):
                    pe.wait_ge(acc_ready, i * E + e + 1)
                    for u in range(U):
                        for f in range(FC):
                            if u == 0:
                                pe.wait_ge(g_ready, i * E * FC + e * FC + f + 1 + HR // NH)
                            mm = pe.matmul(ye[:, e % 2, u * D:(u + 1) * D], G[:, e % 2, f, u * T:(u + 1) * T],
                                           pw("w2")[0:FW, (e * FC + f) * D:(e * FC + f + 1) * D],
                                           start=(f == 0), stop=(f == FC - 1))
                    mm.then_inc(ye_ready, 1)

                hidden(0)
                if capacity:
                    pe.wait_ge(oh_ready, i + 1)
                    pe.wait_ge(run_ready, i * U + 1)
                    for u in range(U):
                        out = rt[:, 64 + u * 2 * E:64 + (u + 1) * 2 * E]
                        flat = lambda q: oh[:, q, :, :].rearrange("p k e -> p (k e)")
                        pe.matmul(out, pw("upto"), flat(u), start=True, stop=False)
                        for q in range(u):
                            pe.matmul(out, consts["ones"][:, 0:P], flat(q), start=False, stop=False)
                        mm = pe.matmul(out, consts["ones"][:, 0:P], run[:, :, :].rearrange("p k e -> p (k e)"),
                                       start=False, stop=True)
                    mm.then_inc(pos_ready, 1)
                for e in range(1, E):
                    hidden(e)
                    down(e - 1)
                down(E - 1)

        @block.scalar
        def _(act):
            with act.Fori(0, NIT) as i:
                act.wait_ge(rows.free, i + 1)
                act.activation(xT[:, :], misc[:, :], ACT.Copy).then_inc(xt, 1)
                act.wait_ge(rstep, i * RS + 2)
                act.activation(pr[:, :, :], pr[:, :, :], ACT.Exp).then_inc(ex_ready, 1)
                for n in range(E * FC):
                    e, f = n // FC, n % FC
                    act.wait_ge(h_ready, i * NHE + NH * n + 1)
                    if f == 0:
                        act.wait_ge(ye_ready, i * E + e + 1)
                    if gated:
                        act.wait_ge(g_ready, i * E * FC + n + 1)
                        act.activation(a_sb[:, n % 2, :], h_ps[0:FW, (2 * n) % HR, :], ACT.Silu
                                       ).then_inc(act_ready, 1)
                    else:
                        act.activation(G[:, e % 2, f, :], h_ps[0:FW, n % HR, :], ACT.Gelu).then_inc(g_ready, 1)

        @block.vector
        def _(dve):
            dve.sem_inc(acc_ready, 2)
            dve.sem_inc(g_ready, HR // NH)
            dve.sem_inc(ye_ready, 2)
            dve.memset(run[:, :, :], 0.0).then_inc(run_ready, 1)
            dve.wait_ge(run_ready, 1)
            dve.wait_ge(w_in, 16)
            with dve.Fori(0, NIT) as i:
                k = i * RS
                reset = pw("reset")
                dve.wait_ge(lg_ready, i + 1)
                lg = rt[:, 0:U * E].rearrange("p (u e) -> p u e", u=U)
                dve.tensor_reduce(m1[:, :], lg, AXX, ALU.max).then_inc(rstep, 1)
                dve.wait_ge(rstep, k + 1)
                dve.tensor_tensor(pr[:, :, :], lg, bcast(m1[:, :], 2, E), ALU.subtract).then_inc(rstep, 1)
                dve.wait_ge(ex_ready, i + 1)
                dve.tensor_reduce(sm[:, :], pr[:, :, :], AXX, ALU.add).then_inc(rstep, 1)
                dve.wait_ge(rstep, k + 3)
                dve.reciprocal(rs[:, :], sm[:, :]).then_inc(rstep, 1)
                dve.wait_ge(rstep, k + 4)
                dve.tensor_tensor(pr[:, :, :], pr[:, :, :], bcast(rs[:, :], 2, E), ALU.mult).then_inc(rstep, 1)
                dve.wait_ge(rstep, k + 5)
                top_one(dve, None, rstep, k + 5, pr[:, :, :], v[:, :, 0], eq[:, :, :], cum[:, :, :], reset,
                        oh[:, :, 0, :])
                dve.scalar_tensor_tensor(p2[:, :, :], oh[:, :, 0, :], -2.0, pr[:, :, :], ALU.mult, ALU.add
                                         ).then_inc(rstep, 1)
                dve.wait_ge(rstep, k + 10)
                top_one(dve, None, rstep, k + 10, p2[:, :, :], v[:, :, 1], eq[:, :, :], cum[:, :, :], reset,
                        oh[:, :, 1, :])
                dve.sem_inc(oh_ready, 1)
                dve.tensor_tensor(ss[:, :], v[:, :, 0], v[:, :, 1], ALU.add).then_inc(rstep, 1)
                dve.wait_ge(rstep, k + 15)
                dve.reciprocal(rss[:, :], ss[:, :]).then_inc(rstep, 1)
                dve.wait_ge(rstep, k + 16)
                dve.tensor_tensor(gate[:, :, :], v[:, :, :], bcast(rss[:, :], 2, 2), ALU.mult).then_inc(rstep, 1)
                src = oh
                if capacity:
                    src = kept
                    dve.wait_ge(pos_ready, i + 1)
                    dve.scalar_tensor_tensor(kept[:, :, :, :].rearrange("p u k e -> p (u k e)"),
                                             rt[:, 64:64 + U * 2 * E], float(capacity),
                                             oh[:, :, :, :].rearrange("p u k e -> p (u k e)"),
                                             ALU.is_le, ALU.mult).then_inc(cw_ready, 1)
                    for u in range(U):
                        dve.tensor_tensor(run[:, :, :], run[:, :, :], oh[:, u, :, :], ALU.add).then_inc(run_ready, 1)
                        dve.wait_ge(run_ready, i * U + u + 2)
                    dve.wait_ge(cw_ready, i + 1)
                dve.wait_ge(rstep, k + 17)
                for q in range(2):
                    dve.tensor_tensor(part[:, :, q, :], src[:, :, q, :], bcast(gate[:, :, q], 2, E),
                                      ALU.mult).then_inc(rstep, 1)
                dve.wait_ge(rstep, k + 19)
                dve.tensor_tensor(cw[:, :, :], part[:, :, 0, :], part[:, :, 1, :], ALU.add).then_inc(cw2, 1)
                dve.wait_ge(cw2, i + 1)

                def gates(e):
                    for f in range(FC):
                        n = e * FC + f
                        dve.wait_ge(act_ready, i * E * FC + n + 1)
                        dve.wait_ge(h_ready, i * NHE + 2 * n + 2)
                        if f == 0:
                            dve.wait_ge(ye_ready, i * E + e + 1)
                        dve.tensor_tensor(G[:, e % 2, f, :], a_sb[:, n % 2, :], h_ps[0:FW, (2 * n + 1) % HR, :],
                                          ALU.mult).then_inc(g_ready, 1)

                def weigh(e):
                    dve.wait_ge(ye_ready, i * E + e + 3)
                    if e == 0:
                        prev = lambda u: x[:, bass.ds(i * U + u, 1), :].rearrange("p a d -> p (a d)")
                    else:
                        dve.wait_ge(acc_ready, i * E + e + 2)
                        prev = lambda u: nm.r[:, u, :]
                    for u in range(U):
                        last = dve.scalar_tensor_tensor(nm.r[:, u, :], ye[:, e % 2, u * D:(u + 1) * D],
                                                        cw[:, u, e:e + 1], prev(u), ALU.mult, ALU.add)
                    last.then_inc(acc_ready, 1)

                if gated:
                    gates(0)
                for e in range(1, E):
                    if gated:
                        gates(e)
                    weigh(e - 1)
                weigh(E - 1)
                dve.wait_ge(acc_ready, i * E + E + 2)
                nm.finish(dve, i)
    ph.close()


def heads_phase(nc, x, consts, blob, table):
    ph = Phase(nc, "sa0")
    LAT = 32
    w = ph.sb("w", list(blob.shape))
    xT = ph.sb("xT", [P, W])
    lat = ph.sb("latent", [LAT, W])
    RQ = 2
    qkv = ph.sb("qkv", [P, RQ, 3, H, HD])
    t1 = ph.sb("rope_cos", [P, RQ, 2, H, HD])
    t2 = ph.sb("rope_sin", [P, RQ, 2, H, HD])
    qk = ph.sb("rotated", [P, RQ, 2, H, HD])
    pq = ph.sb("products", [P, RQ, H, H, HD])
    pv = ph.sb("weighted", [P, H, HD, H])
    att = ph.sb("att", [P, RQ, H, H])
    mx, sm, rs = (ph.sb(n, [P, RQ, H]) for n in ("max", "sum", "rsum"))
    ov = ph.sb("ov", [P, RQ, H, HD])
    o = ph.sb("o", [P, U, D])
    oT = ph.sb("oT", [P, U, T])
    xt_ps, lat_ps = ph.ps("xT", [P, W]), ph.ps("latent", [LAT, W])
    qkv_ps = ph.ps("qkv", [P, 2, 512])
    y = ph.ps("y", [P, W])
    rows = Rows(ph, x)
    nm = Norm(ph, x, consts, y)
    (w_in, xt, lp, lt, qkv_in, qkv_out, cos_done, rot_done, pq_done, att_done, max_done, sub_done, exp_done, sum_done,
     pv_done, ov_done, o_done, ot_in, ot_out) = (ph.sem(n) for n in (
         "w_loaded", "xT_ready", "latent_in_psum", "latent_ready", "qkv_in_psum", "qkv_ready", "roped_parts",
         "rotated_ready", "products_ready", "att_ready", "max_ready", "shifted_ready", "exp_ready", "sum_ready",
         "weighted_ready", "ov_ready", "o_ready", "ot_in_psum", "ot_ready"))
    pw = lambda n: pick(w, table, n)
    yo = lambda u: y[:, u * D:(u + 1) * D]

    with nc.Block() as block:
        @block.sync
        def _(sp):
            sp.dma_start(w[:, :], blob).then_inc(w_in, 16)

        @block.gpsimd
        def _(pool):
            pool.wait_ge(w_in, 16)
            pool.sem_inc(pq_done, RQ)
            rows.gpsimd(pool, 0, first=True)

            def rotate(i):
                for u in range(U):
                    s = u % RQ
                    n = i * U + u
                    pool.wait_ge(qkv_out, n + 1 + 2)
                    src = qkv[:, s, 0:2, :, :].rearrange("p a h e -> p (a h) e")
                    ca = t1[:, s, :, :, :].rearrange("p a h e -> p (a h) e")
                    si = t2[:, s, :, :, :].rearrange("p a h e -> p (a h) e")
                    pool.tensor_tensor(ca, src, bcast(pw("cos"), 1, 2 * H), ALU.mult).then_inc(cos_done, 1)
                    pool.tensor_tensor(si[:, :, 0:HD // 2], src[:, :, HD // 2:HD],
                                       bcast(pw("sin")[:, 0:HD // 2], 1, 2 * H), ALU.mult).then_inc(cos_done, 1)
                    pool.tensor_tensor(si[:, :, HD // 2:HD], src[:, :, 0:HD // 2],
                                       bcast(pw("sin")[:, HD // 2:HD], 1, 2 * H), ALU.mult).then_inc(cos_done, 1)
                    pool.wait_ge(cos_done, n * 3 + 3)
                    pool.tensor_tensor(qk[:, s, :, :, :].rearrange("p a h e -> p (a h) e"), ca, si,
                                       ALU.add).then_inc(rot_done, 1)
                    pool.wait_ge(rot_done, n + 1)
                    pool.wait_ge(att_done, n + 1)
                    pool.tensor_tensor(pq[:, s, :, :, :], bcast(qk[:, s, 0, :, :], 2, H),
                                       bcast(qk[:, s, 1, :, :], 1, H), ALU.mult).then_inc(pq_done, 1)

            with pool.Fori(0, NIT - 1) as i:
                rows.gpsimd(pool, i + 1)
                rotate(i)
                nm.gpsimd(pool, i)
            rotate(NIT - 1)
            nm.gpsimd(pool, NIT - 1)

        def out_row(pe, i, v):
            pe.wait_ge(o_done, i * U + v + 1)
            if v == 0:
                pe.wait_ge(nm.r_ready, i + 1)
            pe.transpose(yo(v), o[:, v, :], consts["ident"][:, :]).then_inc(ot_in, 1)
            pe.wait_ge(ot_out, i * U + v + 1)
            pe.matmul(yo(v), consts["ones"][0:1, 0:P], pw("bout"), start=True, stop=False)
            mm = pe.matmul(yo(v), oT[:, v, :], pw("wout"), start=False, stop=True)
            if v == U - 1:
                mm.then_inc(nm.y_ready, 1)

        @block.tensor
        def _(pe):
            pe.wait_ge(w_in, 16)
            with pe.Fori(0, NIT) as i:
                rows.tensor(pe, i, xt_ps, consts["ident"][:, :])
                pe.wait_ge(xt, i + 1)
                pe.matmul(lat_ps[:, :], pw("wdown"), xT[:, :], start=True, stop=True).then_inc(lp, 1)
                pe.wait_ge(lt, i + 1)
                for u in range(U + 2):
                    if u < U:
                        bank = qkv_ps[:, u % 2, :]
                        pe.wait_ge(qkv_out, i * U + u + 1)
                        pe.matmul(bank[:, 0:D], consts["ones"][0:1, 0:P], pw("bq"), start=True, stop=False)
                        pe.matmul(bank[:, 0:D], xT[:, u * T:(u + 1) * T], pw("wq"), start=False, stop=True)
                        pe.matmul(bank[:, D:3 * D], consts["ones"][0:1, 0:P], pw("bup"), start=True, stop=False)
                        pe.matmul(bank[:, D:3 * D], lat[:, u * T:(u + 1) * T], pw("wup"), start=False,
                                  stop=True).then_inc(qkv_in, 1)
                    v = u - 2
                    if v >= 0:
                        out_row(pe, i, v)

        @block.scalar
        def _(act):
            act.sem_inc(qkv_out, 2)
            act.wait_ge(w_in, 16)
            with act.Fori(0, NIT) as i:
                act.wait_ge(rows.free, i + 1)
                act.activation(xT[:, :], xt_ps[:, :], ACT.Copy).then_inc(xt, 1)
                act.wait_ge(lp, i + 1)
                act.activation(lat[:, :], lat_ps[:, :], ACT.Identity, bias=pw("bdown")[:, 0:1]).then_inc(lt, 1)
                for u in range(U + 2):
                    if u < U:
                        n = i * U + u
                        act.wait_ge(qkv_in, n + 1)
                        act.wait_ge(pv_done, n + 1)
                        act.activation(qkv[:, u % RQ, :, :, :],
                                       qkv_ps[:, u % 2, 0:3 * D].rearrange("p (a h e) -> p a h e", a=3, h=H),
                                       ACT.Copy).then_inc(qkv_out, 1)
                    v = u - 1
                    if 0 <= v < U:
                        act.wait_ge(sub_done, i * U + v + 1)
                        act.activation(att[:, v % RQ, :, :], att[:, v % RQ, :, :], ACT.Exp,
                                       scale=HD ** -0.5).then_inc(exp_done, 1)
                    v = u - 2
                    if v >= 0:
                        act.wait_ge(ot_in, i * U + v + 1)
                        act.activation(oT[:, v, :], yo(v), ACT.Copy).then_inc(ot_out, 1)

        @block.vector
        def _(dve):
            dve.sem_inc(nm.r_ready, 1)
            dve.sem_inc(att_done, RQ)
            dve.sem_inc(pv_done, RQ)
            with dve.Fori(0, NIT) as i:
                for u in range(U + 1):
                    if u < U:
                        n, s = i * U + u, u % RQ
                        dve.wait_ge(pq_done, n + 1 + RQ)
                        dve.tensor_reduce(att[:, s, :, :], pq[:, s, :, :, :], AXX, ALU.add).then_inc(att_done, 1)
                        dve.wait_ge(att_done, n + 1 + RQ)
                        dve.tensor_reduce(mx[:, s, :], att[:, s, :, :], AXX, ALU.max).then_inc(max_done, 1)
                        dve.wait_ge(max_done, n + 1)
                        dve.tensor_tensor(att[:, s, :, :], att[:, s, :, :], bcast(mx[:, s, :], 2, H),
                                          ALU.subtract).then_inc(sub_done, 1)
                    v = u - 1
                    if v >= 0:
                        n, s = i * U + v, v % RQ
                        dve.wait_ge(exp_done, n + 1)
                        dve.tensor_reduce(sm[:, s, :], att[:, s, :, :], AXX, ALU.add).then_inc(sum_done, 1)
                        dve.tensor_tensor(pv[:, :, :, :], bcast(att[:, s, :, :], 2, HD),
                                          bcast(qkv[:, s, 2, :, :].rearrange("p g e -> p e g"), 1, H),
                                          ALU.mult).then_inc(pv_done, 1)
                        dve.wait_ge(sum_done, 2 * n + 1)
                        dve.reciprocal(rs[:, s, :], sm[:, s, :]).then_inc(sum_done, 1)
                        dve.wait_ge(pv_done, n + 1 + RQ)
                        dve.tensor_reduce(ov[:, s, :, :], pv[:, :, :, :], AXX, ALU.add).then_inc(ov_done, 1)
                        dve.wait_ge(ov_done, n + 1)
                        dve.wait_ge(sum_done, 2 * n + 2)
                        dve.tensor_tensor(o[:, v, :].rearrange("p (h e) -> p h e", h=H), ov[:, s, :, :],
                                          bcast(rs[:, s, :], 2, HD), ALU.mult).then_inc(o_done, 1)
                nm.vector(dve, i)
    ph.close()


HQ = 4
QW = D // HQ
RW = 4 * QW + HQ


def delta_phase(nc, x, consts, blob, table, rec, outs):
    ph = Phase(nc, "sa1")
    PC = 3 * D + 2 * H
    w = ph.sb("w", list(blob.shape))
    pw = lambda n: pick(w, table, n)
    w_in = ph.sem("w_loaded")
    if True:
        xT = ph.sb("xT", [P, W])
        sg = ph.sb("sigmoid", [P, 2, PC])
        qkv = ph.sb("qkv", [P, 2, 3, H, HD])
        sq = ph.sb("ksquare", [P, 2, H, HD])
        ss, nr, co, c2 = (ph.sb(n, [P, 2, H]) for n in ("ksum", "knorm", "coef", "coef_raw"))
        rc = ph.sb("records", [P, 2, HQ, RW])
        xt_ps = ph.ps("xT", [P, W])
        pj = ph.ps("pj", [P, 2, 512])
        rows = Rows(ph, x)
        (xt, pj_in, sg_out, qkv_done, sq_done, ss_done, nr_done, co_done, rc_done) = (ph.sem(n) for n in (
            "xT_ready", "pj_ready", "sigmoid_ready", "qkv_ready", "ksquare_ready", "ksum_ready", "knorm_ready",
            "coef_ready", "record_parts"))
        stored = [ph.sem(f"record_stored{r}") for r in range(2)]
        half = ph.sb("half", [P, H])
        half_set = ph.sem("half_set")
        nr2 = ph.sem("rnorm_ready")

        with nc.Block() as block:
            @block.sync
            def _(sp):
                sp.dma_start(w[:, :], blob).then_inc(w_in, 16)
                with sp.Fori(0, NIT) as i:
                    for u in range(U):
                        sp.wait_ge(rc_done, (i * U + u + 1) * 5 + 10)
                        sp.dma_start(rec[bass.ds(i * U + u, 1)].rearrange("a h t w -> t (a h) w"), rc[:, u % 2, :, :]
                                     ).then_inc(stored[u % 2], 16)
                for s in stored:
                    sp.wait_ge(s, B // 2 * 16 + 16)

            @block.gpsimd
            def _(pool):
                pool.memset(half[:, :], 0.5).then_inc(half_set, 1)
                rows.gpsimd(pool, 0, first=True)
                pool.wait_ge(half_set, 1)

                def knorm(i):
                    for u in range(U):
                        pool.wait_ge(ss_done, i * U + u + 1)
                        pool.tensor_tensor(nr[:, u % 2, :], ss[:, u % 2, :], half[:, :], ALU.pow
                                           ).then_inc(nr_done, 1)

                with pool.Fori(0, NIT - 1) as i:
                    rows.gpsimd(pool, i + 1)
                    knorm(i)
                knorm(NIT - 1)

            @block.tensor
            def _(pe):
                pe.wait_ge(w_in, 16)
                with pe.Fori(0, NIT) as i:
                    rows.tensor(pe, i, xt_ps, consts["ident"][:, :])
                    pe.wait_ge(xt, i + 1)
                    for u in range(U):
                        pe.wait_ge(qkv_done, (i * U + u) * 1 + 1)
                        pe.matmul(pj[:, u % 2, 0:PC], xT[:, u * T:(u + 1) * T], pw("wproj"), start=True,
                                  stop=True).then_inc(pj_in, 1)

            @block.scalar
            def _(act):
                with act.Fori(0, NIT) as i:
                    act.wait_ge(rows.free, i + 1)
                    act.activation(xT[:, :], xt_ps[:, :], ACT.Copy).then_inc(xt, 1)
                    for u in range(U):
                        act.wait_ge(pj_in, i * U + u + 1)
                        act.wait_ge(rc_done, (i * U + u + 1) * 5)
                        act.activation(sg[:, u % 2, :], pj[:, u % 2, 0:PC], ACT.Sigmoid).then_inc(sg_out, 1)

            @block.vector
            def _(dve):
                dve.sem_inc(qkv_done, 2)
                dve.sem_inc(rc_done, 10)
                dve.sem_inc(stored[0], 16)
                dve.sem_inc(stored[1], 16)
                with dve.Fori(0, NIT) as i:
                    for u in range(U):
                        n, s = i * U + u, u % 2
                        quarter = lambda k, a: rc[:, s, :, k * QW:(k + 1) * QW].rearrange("p q (h e) -> p q h e", e=HD)
                        heads = lambda t: t.rearrange("p (q h) e -> p q h e", q=HQ)
                        dve.wait_ge(sg_out, n + 1)
                        dve.tensor_tensor(qkv[:, s, :, :, :].rearrange("p a h e -> p (a h e)"), sg[:, s, 0:3 * D],
                                          pj[:, s, 0:3 * D], ALU.mult).then_inc(qkv_done, 1)
                        dve.tensor_tensor(c2[:, s, :], sg[:, s, 3 * D:3 * D + H], sg[:, s, 3 * D + H:PC],
                                          ALU.mult).then_inc(co_done, 1)
                        dve.wait_ge(qkv_done, n + 3)
                        dve.tensor_tensor(sq[:, s, :, :], qkv[:, s, 1, :, :], qkv[:, s, 1, :, :],
                                          ALU.mult).then_inc(sq_done, 1)
                        dve.wait_ge(co_done, 2 * n + 1)
                        dve.scalar_tensor_tensor(co[:, s, :], c2[:, s, :], -1.0, sg[:, s, 3 * D + H:PC], ALU.mult,
                                                 ALU.mult).then_inc(co_done, 1)
                        dve.wait_ge(sq_done, n + 1)
                        dve.tensor_reduce(ss[:, s, :], sq[:, s, :, :], AXX, ALU.add).then_inc(ss_done, 1)
                        dve.wait_ge(stored[s], (i * 2 + u // 2 + 1) * 16)
                        rq = lambda k: rc[:, s, :, k * QW:(k + 1) * QW]
                        flat = lambda k: qkv[:, s, k, :, :].rearrange("p (q h) e -> p q (h e)", q=HQ)
                        dve.tensor_copy(rq(0), flat(0)).then_inc(rc_done, 1)
                        dve.tensor_copy(rq(2), flat(2)).then_inc(rc_done, 1)
                        dve.tensor_copy(rc[:, s, :, 4 * QW:RW],
                                        sg[:, s, 3 * D + H:PC].rearrange("p (q h) -> p q h", q=HQ)).then_inc(rc_done, 1)
                        dve.wait_ge(nr_done, n * 1 + 1)
                        dve.tensor_scalar(nr[:, s, :], nr[:, s, :], 1e-12, None, ALU.max).then_inc(nr2, 1)
                        dve.wait_ge(nr2, 2 * n + 1)
                        dve.reciprocal(nr[:, s, :], nr[:, s, :]).then_inc(nr2, 1)
                        dve.wait_ge(nr2, 2 * n + 2)
                        dve.tensor_tensor(rc[:, s, :, QW:2 * QW].rearrange("p q (h e) -> p q h e", e=HD),
                                          heads(qkv[:, s, 1, :, :]),
                                          bcast(nr[:, s, :].rearrange("p (q h) -> p q h", q=HQ), 3, HD),
                                          ALU.mult).then_inc(rc_done, 1)
                        dve.wait_ge(rc_done, n * 5 + 14)
                        dve.tensor_tensor(rc[:, s, :, 3 * QW:4 * QW].rearrange("p q (h e) -> p q h e", e=HD),
                                          rc[:, s, :, QW:2 * QW].rearrange("p q (h e) -> p q h e", e=HD),
                                          bcast(co[:, s, :].rearrange("p (q h) -> p q h", q=HQ), 3, HD),
                                          ALU.mult).then_inc(rc_done, 1)
    ph.close()

    ph = Phase(nc, "scan")
    TC, HH = 16, H // HQ
    NC = T // TC
    rb = ph.sb("records", [P, 2, TC, RW])
    SH = ph.sb("states", [P, TC + 1, HH, HD, HD])
    tmp, kU = ph.sb("aS", [P, HH, HD, HD]), ph.sb("kU", [P, HH, HD, HD])
    Sd = ph.sb("decayed", [P, 2, HH, HD, HD])
    ra, uu = ph.sb("aS_sum", [P, HH, HD]), ph.sb("u", [P, HH, HD])
    qS = ph.sb("qS", [P, TC, HH, HD, HD])
    ob = ph.sb("out", [P, 2, TC, HH, HD])
    (tmp_done, ra_done, u_done, ku_done, s_done, sd_done, qs_done, o_done) = (ph.sem(n) for n in (
        "aS_ready", "aS_sum_ready", "u_ready", "kU_ready", "state_ready", "decayed_ready", "qS_ready", "out_ready"))
    rb_in = [ph.sem(f"records_loaded{r}") for r in range(2)]
    o_out = [ph.sem(f"out_stored{r}") for r in range(2)]
    recp = rec.rearrange("b q t w -> (b q) (t w)")
    outp = outs.rearrange("b q t w -> (b q) (t w)")
    with nc.Block() as block:
        @block.sync
        def _(sp):
            for k in range(2):
                sp.dma_start(rb[:, k, :, :].rearrange("p t w -> p (t w)"), recp[:, k * TC * RW:(k + 1) * TC * RW]
                             ).then_inc(rb_in[k], 16)
            for c in range(NC):
                sp.wait_ge(o_done, c + 1 + 1)
                sp.dma_start(outp[:, c * TC * QW:(c + 1) * TC * QW],
                             ob[:, c % 2, :, :, :].rearrange("p t h e -> p (t h e)")).then_inc(o_out[c % 2], 16)
                if c + 2 < NC:
                    k = c + 2
                    sp.dma_start(rb[:, k % 2, :, :].rearrange("p t w -> p (t w)"),
                                 recp[:, k * TC * RW:(k + 1) * TC * RW]).then_inc(rb_in[k % 2], 16)
            for s in o_out:
                sp.wait_ge(s, NC // 2 * 16 + 16)

        def field(c2, t, k):
            return rb[:, c2, t, k * QW:(k + 1) * QW].rearrange("p (h e) -> p h e", h=HH)

        def read_out(pool, c, c2, t):
            if t == 1:
                pool.wait_ge(o_done, c + 1)
            pool.tensor_tensor(qS[:, t - 1, :, :, :], SH[:, t, :, :, :], bcast(field(c2, t - 1, 0), 2, HD),
                               ALU.mult).then_inc(qs_done, 1)

        @block.gpsimd
        def _(pool):
            with pool.Fori(0, NC // 2) as cc:
                for c2 in range(2):
                    c = cc * 2 + c2
                    pool.wait_ge(rb_in[c2], cc * 16 + 16)
                    for t in range(TC):
                        f = rb[:, c2, t, 4 * QW:RW]
                        pool.wait_ge(s_done, c * (TC + 1) + t + 1)
                        pool.tensor_tensor(Sd[:, t % 2, :, :, :].rearrange("p h a b -> p h (a b)"),
                                           SH[:, t, :, :, :].rearrange("p h a b -> p h (a b)"),
                                           bcast(f, 2, HD * HD), ALU.mult).then_inc(sd_done, 1)
                        if t > 0:
                            read_out(pool, c, c2, t)
                    pool.wait_ge(s_done, c * (TC + 1) + TC + 1)
                    read_out(pool, c, c2, TC)

        @block.vector
        def _(dve):
            dve.sem_inc(o_done, 1)
            dve.memset(SH[:, 0, :, :, :], 0.0).then_inc(s_done, 1)
            dve.wait_ge(s_done, 1)
            for k in range(2):
                dve.sem_inc(o_out[k], 16)
            with dve.Fori(0, NC // 2) as cc:
                for c2 in range(2):
                    c = cc * 2 + c2
                    dve.wait_ge(rb_in[c2], cc * 16 + 16)
                    for t in range(TC):
                        n = c * TC + t
                        dve.tensor_tensor(tmp[:, :, :, :], SH[:, t, :, :, :], bcast(field(c2, t, 3), 2, HD),
                                          ALU.mult).then_inc(tmp_done, 1)
                        dve.wait_ge(tmp_done, n + 1)
                        dve.tensor_reduce(ra[:, :, :], tmp[:, :, :, :], AXX, ALU.add).then_inc(ra_done, 1)
                        dve.wait_ge(ra_done, n + 1)
                        dve.tensor_tensor(uu[:, :, :], ra[:, :, :], field(c2, t, 2), ALU.add).then_inc(u_done, 1)
                        dve.wait_ge(u_done, n + 1)
                        dve.tensor_tensor(kU[:, :, :, :], bcast(uu[:, :, :], 3, HD), bcast(field(c2, t, 1), 2, HD),
                                          ALU.mult).then_inc(ku_done, 1)
                        dve.wait_ge(ku_done, n + 1)
                        dve.wait_ge(sd_done, n + 1)
                        dve.tensor_tensor(SH[:, t + 1, :, :, :], Sd[:, t % 2, :, :, :], kU[:, :, :, :],
                                          ALU.add).then_inc(s_done, 1)
                        dve.wait_ge(s_done, c * (TC + 1) + t + 2)
                    dve.wait_ge(qs_done, c * TC + TC)
                    dve.wait_ge(o_out[c2], cc * 16 + 16)
                    dve.tensor_reduce(ob[:, c2, :, :, :], qS[:, :, :, :, :], AXX, ALU.add).then_inc(o_done, 1)
                    dve.tensor_copy(SH[:, 0, :, :, :], SH[:, TC, :, :, :]).then_inc(s_done, 1)
                    dve.wait_ge(s_done, (c + 1) * (TC + 1) + 1)
    ph.close()

    ph = Phase(nc, "gate")
    w = ph.sb("w", list(blob.shape))
    xT = ph.sb("xT", [P, W])
    g1 = ph.sb("g1", [HD, W])
    gt, ol, og, z, zn, zT = (ph.sb(n, [P, U, D]) for n in ("gate", "o", "gated", "z", "zn", "zT"))
    xt_ps, g1_ps, gt_ps, z_ps, y = (ph.ps(n, [P, W]) for n in ("xT", "g1", "gate", "zT", "y"))
    rows = Rows(ph, x)
    nm = Norm(ph, x, consts, y)
    inner = Stats(ph, consts, "inner_")
    (w_in, ol_in, xt, g1_in, g1_out, gt_in, gt_out, og_done, z_done, zn_done, zt_in, zt_out) = (ph.sem(n) for n in (
        "w_loaded", "o_loaded", "xT_ready", "g1_in_psum", "g1_ready", "gate_in_psum", "gate_ready", "gated_ready",
        "z_ready", "zn_ready", "zT_in_psum", "zT_ready"))
    flat = lambda a: a[:, :, :].rearrange("p u d -> p (u d)")
    with nc.Block() as block:
        @block.sync
        def _(sp):
            sp.dma_start(w[:, :], blob).then_inc(w_in, 16)
            with sp.Fori(0, NIT) as i:
                sp.wait_ge(og_done, i + 1)
                for u in range(U):
                    sp.dma_start(ol[:, u, :].rearrange("p (q e) -> p q e", q=HQ),
                                 outs[bass.ds(i * U + u, 1)].rearrange("a q t e -> t (a q) e")).then_inc(ol_in, 16)

        @block.gpsimd
        def _(pool):
            rows.gpsimd(pool, 0, first=True)
            with pool.Fori(0, NIT - 1) as i:
                rows.gpsimd(pool, i + 1)
                inner.gpsimd(pool, i)
                nm.gpsimd(pool, i)
            inner.gpsimd(pool, NIT - 1)
            nm.gpsimd(pool, NIT - 1)

        @block.tensor
        def _(pe):
            pe.wait_ge(w_in, 16)
            with pe.Fori(0, NIT) as i:
                rows.tensor(pe, i, xt_ps, consts["ident"][:, :])
                pe.wait_ge(xt, i + 1)
                pe.matmul(g1_ps[0:HD, :], pw("wg1"), xT[:, :], start=True, stop=True).then_inc(g1_in, 1)
                pe.wait_ge(g1_out, i + 1)
                for u in range(U):
                    mm = pe.matmul(gt_ps[:, u * D:(u + 1) * D], g1[:, u * T:(u + 1) * T], pw("wg2"), start=True,
                                   stop=True)
                mm.then_inc(gt_in, 1)
                pe.wait_ge(zn_done, i + 1)
                for u in range(U):
                    mm = pe.transpose(z_ps[:, u * T:(u + 1) * T], zn[:, u, :], consts["ident"][:, :])
                mm.then_inc(zt_in, 1)
                pe.wait_ge(zt_out, i + 1)
                pe.wait_ge(nm.r_ready, i + 1)
                for u in range(U):
                    mm = pe.matmul(y[:, u * D:(u + 1) * D], zT[:, u, :], pw("wo"), start=True, stop=True)
                mm.then_inc(nm.y_ready, 1)

        @block.scalar
        def _(act):
            with act.Fori(0, NIT) as i:
                act.wait_ge(rows.free, i + 1)
                act.activation(xT[:, :], xt_ps[:, :], ACT.Copy).then_inc(xt, 1)
                act.wait_ge(g1_in, i + 1)
                act.activation(g1[:, :], g1_ps[0:HD, :], ACT.Copy).then_inc(g1_out, 1)
                act.wait_ge(gt_in, i + 1)
                act.activation(flat(gt), gt_ps[:, :], ACT.Sigmoid).then_inc(gt_out, 1)
                act.wait_ge(zt_in, i + 1)
                act.activation(flat(zT), z_ps[:, :], ACT.Copy).then_inc(zt_out, 1)

        @block.vector
        def _(dve):
            dve.sem_inc(nm.r_ready, 1)
            dve.sem_inc(og_done, 1)
            dve.wait_ge(w_in, 16)
            with dve.Fori(0, NIT) as i:
                dve.wait_ge(gt_out, i + 1)
                dve.wait_ge(ol_in, (i + 1) * 16 * U)
                dve.tensor_tensor(flat(og), flat(ol), flat(gt), ALU.mult).then_inc(og_done, 1)
                dve.wait_ge(og_done, i + 2)
                inner.vector(dve, i, og)
                dve.wait_ge(inner.rstd_ready, i + 1)
                for u in range(U):
                    dve.tensor_scalar(z[:, u, :], og[:, u, :], inner.mv[:, u, 0:1], inner.rstd[:, u:u + 1],
                                      ALU.subtract, ALU.mult).then_inc(z_done, 1)
                dve.wait_ge(z_done, i * U + U)
                dve.tensor_tensor(zn[:, :, :], z[:, :, :], bcast(pw("norm_w"), 1, U), ALU.mult).then_inc(zn_done, 1)
                nm.vector(dve, i)
    ph.close()


def ssm_phase(nc, x, consts, blob, table):
    ph = Phase(nc, "ssm")
    NCH, NS, KC = 2, 16, 4
    NB = P // NS
    NR = NCH * P // NB
    PAD = KC - 1
    w = ph.sb("w", list(blob.shape))
    pw = lambda n: pick(w, table, n)
    xn = ph.sb("xn", [P, U, D])
    xT = ph.sb("xnT", [P, W])
    xp = ph.sb("xp", [P, NCH, U, T + PAD])
    sgate = ph.sb("silu_gate", [P, NCH, W])
    cv = ph.sb("conv", [P, NCH, U, T])
    xc = ph.sb("xc", [P, NCH, W])
    BC = ph.sb("BC", [P, 2, W])
    sig_a = ph.sb("decay", [P, NR])
    UR = 4
    uu, hh, hc = (ph.sb(n, [P, UR, W]) for n in ("u", "h", "hC"))
    yg, yd = ph.sb("y_gated", [P, NCH, W]), ph.sb("y_skip", [P, NCH, W])
    pj = ph.ps("pj", [P, 2, W])
    xr_ps = ph.ps("xr", [P, 2, W])
    ya = ph.ps("ya", [P, NCH, W])
    y = ph.ps("y", [P, W])
    nm = Norm(ph, x, consts, y, x_times=2.0)
    pre = Stats(ph, consts, "pre_")
    (w_in, dec_done, pad_done, xn_done, pj_in, pj_out, cv_done, xc_done, xr_in, u_done, h_done, hc_done,
     ya_in, yd_done, yg_done, row_in) = (ph.sem(n) for n in (
         "w_loaded", "decay_ready", "pads_ready", "xn_ready", "pj_ready", "pj_done", "conv_ready", "xc_ready",
         "xr_ready", "u_ready", "h_ready", "hC_ready", "ya_ready", "skip_ready", "gated_ready", "rows_ready"))
    NJ = 1 + 4 + 2
    flat = lambda a: a.rearrange("p a b -> p (a b)")
    row = lambda i, u: x[:, bass.ds(i * U + u, 1), :].rearrange("p a d -> p (a d)")

    with nc.Block() as block:
        @block.sync
        def _(sp):
            sp.dma_start(w[:, :], blob).then_inc(w_in, 16)

        @block.gpsimd
        def _(pool):
            pool.memset(xp[:, :, :, :], 0.0).then_inc(pad_done, 1)
            pool.wait_ge(pad_done, 1)
            pool.sem_inc(hc_done, UR)

            def weigh(i):
                for r in range(NR):
                    n = i * NR + r
                    pool.wait_ge(h_done, (n + 1 + UR) * U)
                    pool.wait_ge(ya_in, n + 1)
                    pool.tensor_tensor(hc[:, r % UR, :], hh[:, r % UR, :], BC[:, 1, :], ALU.mult).then_inc(hc_done, 1)

            pre.gpsimd(pool, 0)
            with pool.Fori(0, NIT - 1) as i:
                weigh(i)
                nm.gpsimd(pool, i)
                pre.gpsimd(pool, i + 1)
            weigh(NIT - 1)
            nm.gpsimd(pool, NIT - 1)

        @block.tensor
        def _(pe):
            pe.sem_inc(ya_in, UR)
            pe.wait_ge(w_in, 16)
            with pe.Fori(0, NIT) as i:
                pe.wait_ge(xn_done, (i + 1) * U)
                for u in range(U):
                    mm = pe.transpose(pj[:, 0, u * T:(u + 1) * T], xn[:, u, :], consts["ident"][:, :])
                mm.then_inc(pj_in, 1)
                pe.wait_ge(pj_out, i * NJ + 1)
                for j in range(1, 5):
                    if j > 1:
                        pe.wait_ge(pj_out, i * NJ + j - 1)
                    pe.matmul(pj[:, j % 2, :], pw("w_in")[:, (j - 1) * P:j * P], xT[:, :], start=True,
                              stop=True).then_inc(pj_in, 1)
                pe.wait_ge(xc_done, (i + 1) * NCH)
                pe.wait_ge(pj_out, i * NJ + 5)
                for k in range(2):
                    bank = pj[:, (5 + k) % 2, :]
                    for c in range(NCH):
                        mm = pe.matmul(bank, pw("w_bc")[:, (k * NCH + c) * P:(k * NCH + c + 1) * P], xc[:, c, :],
                                       start=(c == 0), stop=(c == NCH - 1))
                    mm.then_inc(pj_in, 1)
                for r in range(NR + 2):
                    if r < NR:
                        c, q = r // NS, r % NS
                        pe.wait_ge(u_done, i * NR + r + 1)
                        pe.matmul(xr_ps[:, r % 2, :], pw("spread")[:, q * P:(q + 1) * P], xc[:, c, :], start=True,
                                  stop=True).then_inc(xr_in, 1)
                    m = r - 2
                    if m >= 0:
                        c, q = m // NS, m % NS
                        pe.wait_ge(hc_done, i * NR + m + 1 + UR)
                        if m == 0:
                            pe.wait_ge(yd_done, i * NCH + NCH)
                        pe.matmul(ya[:, c, :], pw("gather")[:, q * P:(q + 1) * P], hc[:, m % UR, :], start=(q == 0),
                                  stop=(q == NS - 1)).then_inc(ya_in, 1)
                pe.wait_ge(yg_done, (i + 1) * NCH)
                pe.wait_ge(nm.r_ready, i + 1)
                for u in range(U):
                    yu = y[:, u * D:(u + 1) * D]
                    pe.matmul(yu, consts["ones"][0:1, 0:P], pw("b_out"), start=True, stop=False)
                    for c in range(NCH):
                        mm = pe.matmul(yu, yg[:, c, u * T:(u + 1) * T], pw("w_out")[:, c * D:(c + 1) * D],
                                       start=False, stop=(c == NCH - 1))
                mm.then_inc(nm.y_ready, 1)

        @block.scalar
        def _(act):
            act.wait_ge(w_in, 16)
            act.wait_ge(pad_done, 1)
            act.activation(sig_a[:, :], pw("a"), ACT.Sigmoid).then_inc(dec_done, 1)
            with act.Fori(0, NIT) as i:
                act.wait_ge(pj_in, i * NJ + 1)
                act.activation(xT[:, :], pj[:, 0, :], ACT.Identity, scale=pw("ln_g")[:, 0:1],
                               bias=pw("ln_b")[:, 0:1]).then_inc(pj_out, 1)
                for j in range(1, 5):
                    act.wait_ge(pj_in, i * NJ + j + 1)
                    c, b = (j - 1) % 2, pw("b_in")[:, j - 1:j]
                    if j < 3:
                        act.activation(xp[:, c, :, PAD:], pj[:, j % 2, :].rearrange("p (u t) -> p u t", u=U),
                                       ACT.Identity, bias=b).then_inc(pj_out, 1)
                    else:
                        act.activation(sgate[:, c, :], pj[:, j % 2, :], ACT.Silu, bias=b).then_inc(pj_out, 1)
                for c in range(NCH):
                    act.wait_ge(cv_done, (i * NCH + c + 1) * KC)
                    act.activation(xc[:, c, :], flat(cv[:, c, :, :]), ACT.Silu).then_inc(xc_done, 1)
                for k in range(2):
                    act.wait_ge(pj_in, i * NJ + 6 + k)
                    act.activation(BC[:, k, :], pj[:, (5 + k) % 2, :], ACT.Identity, bias=pw("b_bc")[:, k:k + 1]
                                   ).then_inc(pj_out, 1)

        @block.vector
        def _(dve):
            dve.sem_inc(nm.r_ready, 1)
            dve.sem_inc(u_done, 2)
            dve.sem_inc(h_done, UR * U)
            dve.sem_inc(yd_done, NCH)
            dve.wait_ge(w_in, 16)
            dve.wait_ge(dec_done, 1)

            def prenorm(i):
                pre.vector(dve, i, x[:, bass.ds(i * U, U), :])
                dve.wait_ge(pre.rstd_ready, i + 1)
                for u in range(U):
                    dve.tensor_scalar(xn[:, u, :], row(i, u), pre.mv[:, u, 0:1], pre.rstd[:, u:u + 1],
                                      ALU.subtract, ALU.mult).then_inc(xn_done, 1)

            prenorm(0)

            def body(i):
                for c in range(NCH):
                    dve.wait_ge(pj_out, i * NJ + 2 + c)
                    for k in range(KC):
                        taps = xp[:, c, :, k:k + T]
                        wk = pw("conv_w")[:, c * KC + k:c * KC + k + 1]
                        n = (i * NCH + c) * KC + k
                        if k == 0:
                            dve.tensor_scalar(cv[:, c, :, :], taps, wk, pw("conv_b")[:, c:c + 1], ALU.mult,
                                              ALU.add).then_inc(cv_done, 1)
                        else:
                            dve.wait_ge(cv_done, n)
                            dve.scalar_tensor_tensor(cv[:, c, :, :], taps, wk, cv[:, c, :, :], ALU.mult,
                                                     ALU.add).then_inc(cv_done, 1)
                for r in range(NR):
                    n = i * NR + r
                    dve.wait_ge(xr_in, n + 1)
                    if r == 0:
                        dve.wait_ge(pj_out, i * NJ + NJ)
                    dve.wait_ge(h_done, (n + 1) * U)
                    dve.tensor_tensor(uu[:, r % UR, :], xr_ps[:, r % 2, :], BC[:, 0, :], ALU.mult).then_inc(u_done, 1)
                    if r >= 1:
                        scan(i, r - 1)
                scan(i, NR - 1)
                for c in range(NCH):
                    dve.wait_ge(ya_in, i * NR + NS * (c + 1) + UR)
                    dve.scalar_tensor_tensor(yd[:, c, :], xc[:, c, :], pw("d")[:, c:c + 1], ya[:, c, :],
                                             ALU.mult, ALU.add).then_inc(yd_done, 1)
                for c in range(NCH):
                    dve.wait_ge(yd_done, (i + 1) * NCH + c + 1)
                    dve.tensor_tensor(yg[:, c, :], yd[:, c, :], sgate[:, c, :], ALU.mult).then_inc(yg_done, 1)
                nm.vector(dve, i)

            def scan(i, r):
                n = i * NR + r
                dve.wait_ge(u_done, n + 3)
                dve.wait_ge(hc_done, n + 1)
                for u in range(U):
                    dve.tensor_tensor_scan(hh[:, r % UR, u * T:(u + 1) * T],
                                           sig_a[:, r:r + 1].broadcast_to([P, T]),
                                           uu[:, r % UR, u * T:(u + 1) * T], 0.0, ALU.mult, ALU.add
                                           ).then_inc(h_done, 1)

            with dve.Fori(0, NIT - 1) as i:
                body(i)
                prenorm(i + 1)
            body(NIT - 1)
    ph.close()


def wide_moe_phase(nc, x, consts, blob, table):
    ph = Phase(nc, "ff3")
    E, K, EH = 64, 8, 32
    NR = E * EH // P
    NSH = 4
    NCK = NR + NSH
    w = ph.sb("w", list(blob.shape))
    pw = lambda n: pick(w, table, n)
    xT = ph.sb("xT", [P, W])
    big = lambda n: ph.sb(n, [P, U, E])
    pr, gt, eq, cum, le, sel, cw = (big(n) for n in ("probs", "above", "equal", "cumul", "fits", "chosen", "share"))
    m1, sm, rs, cnt, need, s8, rs8 = (ph.sb(n, [P, U]) for n in ("lmax", "lsum", "rlsum", "above_n", "need", "sum8",
                                                                  "rsum8"))
    top = ph.sb("top8", [P, U, 8])
    cwT = ph.sb("shareT", [E, W])
    act_sb = ph.sb("silu", [P, 3, W])
    hid = ph.sb("hidden", [P, NCK, W])
    xt_ps = ph.ps("xT", [P, W])
    h_ps = ph.ps("h", [P, 3, W])
    cb_ps = ph.ps("share", [P, 2, W])
    y = ph.ps("y", [P, W])
    rows = Rows(ph, x)
    nm = Norm(ph, x, consts, y)
    (w_in, xt, lg, st, ex, cw_done, ct_in, ct_out, h_in, a_done, cb_in, hid_done, sh_done) = (ph.sem(n) for n in (
        "w_loaded", "xT_ready", "logits_ready", "router_step", "exp_ready", "share_ready", "shareT_in_psum",
        "shareT_ready", "h_ready", "silu_ready", "share_spread", "hidden_ready", "shared_ready"))
    NSTEP = 18

    with nc.Block() as block:
        @block.sync
        def _(sp):
            sp.dma_start(w[:, :], blob).then_inc(w_in, 16)

        @block.gpsimd
        def _(pool):
            rows.gpsimd(pool, 0, first=True)
            with pool.Fori(0, NIT - 1) as i:
                rows.gpsimd(pool, i + 1)
                nm.gpsimd(pool, i)
            nm.gpsimd(pool, NIT - 1)

        @block.tensor
        def _(pe):
            pe.wait_ge(w_in, 16)
            with pe.Fori(0, NIT) as i:
                rows.tensor(pe, i, xt_ps, consts["ident"][:, :])
                pe.wait_ge(xt, i + 1)
                for u in range(U):
                    o = xt_ps[:, u * E:(u + 1) * E]
                    pe.matmul(o, consts["ones"][0:1, 0:P], pw("router_b"), start=True, stop=False)
                    mm = pe.matmul(o, xT[:, u * T:(u + 1) * T], pw("router"), start=False, stop=True)
                mm.then_inc(lg, 1)

                def hidden(j):
                    pe.wait_ge(a_done, i * NCK + j + 1)
                    pe.matmul(h_ps[:, j % 3, :], pw("w1")[:, j * P:(j + 1) * P], xT[:, :], start=True,
                              stop=True).then_inc(h_in, 1)

                for j in range(NSH):
                    hidden(j)
                pe.wait_ge(cw_done, i + 1)
                hidden(NSH)
                for u in range(U):
                    mm = pe.transpose(xt_ps[0:E, u * T:(u + 1) * T], cw[:, u, :], consts["ident"][:, :])
                mm.then_inc(ct_in, 1)
                pe.wait_ge(ct_out, i + 1)
                for r in range(NR):
                    if r > 0:
                        hidden(NSH + r)
                    pe.wait_ge(hid_done, i * NR + r + 1)
                    pe.matmul(cb_ps[:, r % 2, :], pw("spread")[:, r * P:(r + 1) * P], cwT[:, :], start=True,
                              stop=True).then_inc(cb_in, 1)
                pe.wait_ge(nm.r_ready, i + 1)
                for u in range(U):
                    yu = y[:, u * D:(u + 1) * D]
                    for k in range(2):
                        pe.matmul(yu, consts["ones"][0:1, 0:P], pw(f"sb2_{k}"), start=(k == 0), stop=False)
                    pe.matmul(yu, cwT[:, u * T:(u + 1) * T], pw("b2"), start=False, stop=False)
                    for j in range(NCK):
                        if u == 0 and j >= NSH:
                            pe.wait_ge(hid_done, i * NR + (j - NSH) + 1 + 2)
                        if u == 0 and j == 0:
                            pe.wait_ge(sh_done, (i + 1) * NSH)
                        mm = pe.matmul(yu, hid[:, j, u * T:(u + 1) * T], pw("w2")[:, j * D:(j + 1) * D],
                                       start=False, stop=(j == NCK - 1))
                mm.then_inc(nm.y_ready, 1)

        @block.scalar
        def _(act):
            act.sem_inc(a_done, 3)
            act.wait_ge(w_in, 16)
            with act.Fori(0, NIT) as i:
                act.wait_ge(rows.free, i + 1)
                act.activation(xT[:, :], xt_ps[:, :], ACT.Copy).then_inc(xt, 1)
                act.wait_ge(st, i * NSTEP + 2)
                act.activation(pr[:, :, :], pr[:, :, :], ACT.Exp).then_inc(ex, 1)
                for j in range(NCK):
                    n = i * NCK + j
                    if j == NSH:
                        act.wait_ge(ct_in, i + 1)
                        act.activation(cwT[:, :], xt_ps[0:E, :], ACT.Copy).then_inc(ct_out, 1)
                    act.wait_ge(h_in, n + 1)
                    b = pw("b1")[:, j:j + 1]
                    if j < NSH:
                        act.activation(hid[:, j, :], h_ps[:, j % 3, :], ACT.Silu, bias=b).then_inc(a_done, 1)
                        act.wait_ge(a_done, n + 4)
                        act.sem_inc(sh_done, 1)
                    else:
                        if j >= NSH + 3:
                            act.wait_ge(hid_done, i * NR + (j - NSH) + 1 - 3 + 2)
                        act.activation(act_sb[:, j % 3, :], h_ps[:, j % 3, :], ACT.Silu, bias=b).then_inc(a_done, 1)

        @block.vector
        def _(dve):
            dve.sem_inc(nm.r_ready, 1)
            dve.sem_inc(hid_done, 2)
            dve.wait_ge(w_in, 16)
            with dve.Fori(0, NIT) as i:
                k0 = i * NSTEP
                dve.wait_ge(lg, i + 1)
                l = xt_ps[:, 0:U * E].rearrange("p (u e) -> p u e", u=U)
                step = [0]

                def done(ins, hold=True):
                    ins.then_inc(st, 1)
                    step[0] += 1
                    if hold:
                        dve.wait_ge(st, k0 + step[0])

                done(dve.tensor_reduce(m1[:, :], l, AXX, ALU.max))
                done(dve.tensor_tensor(pr[:, :, :], l, bcast(m1[:, :], 2, E), ALU.subtract), hold=False)
                dve.wait_ge(ex, i + 1)
                done(dve.tensor_reduce(sm[:, :], pr[:, :, :], AXX, ALU.add))
                done(dve.reciprocal(rs[:, :], sm[:, :]))
                done(dve.tensor_tensor(pr[:, :, :], pr[:, :, :], bcast(rs[:, :], 2, E), ALU.mult))
                dve.memset(cnt[:, :], 0.0)
                for u in range(U):
                    ins = dve.max(top[:, u, :], pr[:, u, :])
                done(ins)
                done(dve.tensor_tensor(gt[:, :, :], pr[:, :, :], bcast(top[:, :, 7], 2, E), ALU.is_gt), hold=False)
                done(dve.tensor_tensor(eq[:, :, :], pr[:, :, :], bcast(top[:, :, 7], 2, E), ALU.is_equal))
                done(dve.tensor_reduce(cnt[:, :], gt[:, :, :], AXX, ALU.add), hold=False)
                done(dve.tensor_tensor_scan(flat3(cum), pw("reset"), flat3(eq), 0.0, ALU.mult, ALU.add))
                done(dve.tensor_scalar(need[:, :], cnt[:, :], -1.0, float(K), ALU.mult, ALU.add))
                done(dve.tensor_tensor(le[:, :, :], cum[:, :, :], bcast(need[:, :], 2, E), ALU.is_le))
                done(dve.tensor_tensor(sel[:, :, :], le[:, :, :], eq[:, :, :], ALU.mult))
                done(dve.tensor_tensor(sel[:, :, :], sel[:, :, :], gt[:, :, :], ALU.add), hold=False)
                done(dve.tensor_reduce(s8[:, :], top[:, :, :], AXX, ALU.add))
                done(dve.reciprocal(rs8[:, :], s8[:, :]), hold=False)
                done(dve.tensor_tensor(sel[:, :, :], sel[:, :, :], pr[:, :, :], ALU.mult))
                assert step[0] == NSTEP - 1
                done(dve.tensor_tensor(cw[:, :, :], sel[:, :, :], bcast(rs8[:, :], 2, E), ALU.mult))
                dve.sem_inc(cw_done, 1)
                for r in range(NR):
                    j = NSH + r
                    dve.wait_ge(a_done, i * NCK + j + 4)
                    dve.wait_ge(cb_in, i * NR + r + 1)
                    dve.tensor_tensor(hid[:, j, :], act_sb[:, j % 3, :], cb_ps[:, r % 2, :], ALU.mult
                                      ).then_inc(hid_done, 1)
                nm.vector(dve, i)
    ph.close()


def flat3(a):
    return a[:, :, :].rearrange("p u e -> p (u e)")


def build(nc, t, tables, out, stages):
    ctx = ExitStack()
    with ctx:
        sb = lambda n, s, d=F32: ctx.enter_context(nc.sbuf_tensor(n, s, d))
        x = sb("x", [P, B, D])
        consts = {"ident": sb("ident", [P, P]), "ones": sb("ones", [P, 512]), "neghalf": sb("neghalf", [P, 16])}
        x_in = ctx.enter_context(nc.semaphore("x_loaded"))
        const_ready = ctx.enter_context(nc.semaphore("const_ready"))
        stored = ctx.enter_context(nc.semaphore("stored"))
        consts["ready"] = const_ready
        with nc.Block() as block:
            @block.sync
            def _(sp):
                sp.dma_start(x[:, :, :], t["x"].rearrange("b t d -> t b d")).then_inc(x_in, 16)
                sp.wait_ge(x_in, 16)

            @block.gpsimd
            def _(pool):
                pool.memset(consts["ident"][:, :], 0.0).then_inc(const_ready, 1)
                pool.memset(consts["ones"][:, :], 1.0).then_inc(const_ready, 1)
                pool.memset(consts["neghalf"][:, :], -0.5).then_inc(const_ready, 1)
                pool.wait_ge(const_ready, 3)
                pool.affine_select(out=consts["ident"][:, :], in_=consts["ident"][:, :],
                                   compare_op=ALU.not_equal, fill=1.0, base=0, pattern=[[-1, P]],
                                   channel_multiplier=1).then_inc(const_ready, 1)
                pool.wait_ge(const_ready, 4)
        for s in stages:
            PHASES[s](nc, x, consts, t, tables)
        with nc.Block() as block:
            @block.sync
            def _(sp):
                sp.dma_start(out.rearrange("b t d -> t b d"), x[:, :, :]).then_inc(stored, 16)
                sp.wait_ge(stored, 16)


PHASES = {
    0: lambda nc, x, c, t, tb: heads_phase(nc, x, c, t["sa0"], tb["sa0"]),
    3: lambda nc, x, c, t, tb: delta_phase(nc, x, c, t["sa1"], tb["sa1"],
                                           nc.dram_tensor("records", (B, HQ, T, RW), F32, kind="Internal").ap(),
                                           nc.dram_tensor("recurrence", (B, HQ, T, QW), F32, kind="Internal").ap()),
    9: lambda nc, x, c, t, tb: ssm_phase(nc, x, c, t["ssm"], tb["ssm"]),
    11: lambda nc, x, c, t, tb: wide_moe_phase(nc, x, c, t["ff3"], tb["ff3"]),
    2: lambda nc, x, c, t, tb: moe_phase(nc, "ff0", x, c, t["ff0"], tb["ff0"], F=512, gated=False,
                                         capacity=max(1, int(1.25 * (B * T) / 8 * 2))),
    5: lambda nc, x, c, t, tb: moe_phase(nc, "ff1", x, c, t["ff1"], tb["ff1"], F=448, gated=True),
    1: lambda nc, x, c, t, tb: attention_phase(nc, "xa0", x, c, t, t["xa0"], tb["xa0"], scale=HD ** -0.5, bias="causal"),
    4: lambda nc, x, c, t, tb: attention_phase(nc, "xa1", x, c, t, t["xa1"], tb["xa1"], scale=HD ** -0.5, bias="rows"),
    6: lambda nc, x, c, t, tb: attention_phase(nc, "sa2", x, c, t, t["sa2"], tb["sa2"], scale=0.25, bias="causal",
                                               lut=True),
    7: lambda nc, x, c, t, tb: attention_phase(nc, "xa2", x, c, t, t["xa2"], tb["xa2"], scale=HD ** -0.5),
    10: lambda nc, x, c, t, tb: attention_phase(nc, "xa3", x, c, t, t["xa3"], tb["xa3"], scale=HD ** -0.5,
                                                bias="heads"),
    8: lambda nc, x, c, t, tb: piecewise_phase(nc, x, c, t["pw"], tb["pw"]),
}


STAGES = list(range(12))


def _pack(np, parts):
    table, cols = {}, 0
    for name, a in parts:
        table[name] = (a.shape[0], cols, a.shape[1])
        cols += a.shape[1]
    out = np.zeros((P, cols), np.float32)
    for name, a in parts:
        r, o, c = table[name]
        out[0:r, o:o + c] = a
    return out, table


def _layouts(np, g):
    packs = {}
    W1, b1, W2 = (g("L2_ffn_" + n).reshape(64, 8, 2) for n in ("W1", "b1", "W2"))
    pair = lambda a: np.concatenate([a[:, :, 0], a[:, :, 1]], 0)
    dup = lambda a: np.concatenate([a, a], -1)
    Wout = g("L2_ffn_Wout")
    packs["pw"] = [("Win", dup(g("L2_ffn_Win"))), ("bin", dup(g("L2_ffn_bin_"))[:, None]),
                   ("W1", pair(W1)), ("b1", pair(b1)), ("W2", pair(W2)),
                   ("Wout", Wout), ("Wout2", np.concatenate([Wout, Wout], 0)),
                   ("b2", np.repeat(g("L2_ffn_b2")[:, None], P, 1)),
                   ("bout", g("L2_ffn_bout")[None, :])]

    def head_cols(a):
        out = np.zeros((P, CH, 4, 32), np.float32)
        out[..., :HD] = a.reshape(P, CH, 4, HD)
        return out.reshape(P, CH * P)

    def head_bias(b):
        out = np.zeros((CH, 4, 32), np.float32)
        out[..., :HD] = b.reshape(CH, 4, HD)
        return out.reshape(CH, P).T

    def causal(nk):
        return np.where(np.arange(nk)[None, :] <= np.arange(T)[:, None], 0.0, MASKED).astype(np.float32)

    def attn(wq, bq, wk, bk, wv, bv, wo, bo):
        parts = [("wq", head_cols(wq)), ("wk", head_cols(wk)), ("wv", wv), ("wo", wo)]
        if bq is not None:
            parts += [("bq", head_bias(bq)), ("bk", head_bias(bk))]
        parts += [("bv", np.zeros((1, D), np.float32) if bv is None else bv[None, :])]
        return parts + [("bo", bo[None, :])]

    packs["xa0"] = attn(*(g("L0_xattn_" + n) for n in ("q_w", "q_b", "k_w", "k_b", "v_w", "v_b", "o_w", "o_b")))
    packs["xa0"] += [("causal", causal(S2))]
    L1 = lambda n: g("L1_xattn_" + n)
    packs["xa1"] = attn(L1("Wq").T, L1("bq"), L1("Wk").T, L1("bk"), L1("Wv").T, L1("bv"), L1("Wo").T, L1("bo"))
    kv = g("L2_xattn_Wkv")
    packs["xa2"] = attn(g("L2_xattn_Wq").T, None, kv[:D].T, None, kv[D:].T, None, g("L2_xattn_Wproj").T,
                        g("L2_xattn_bproj"))
    packs["xa3"] = attn(*(g("L3_xattn_" + n) for n in ("Wq", "bq", "Wk", "bk", "Wv", "bv", "Wo", "bo")))
    eye = np.eye(P, dtype=np.float32)
    L2 = lambda n: g("L2_attn_" + n)
    cols = lambda a, b: np.stack([a.reshape(-1), b.reshape(-1)], 1)
    packs["sa2"] = [("wid", cols(L2("w_q"), L2("w_k"))), ("shift", cols(L2("b_q"), L2("b_k"))),
                    ("cos_sel", head_cols(eye)), ("sin_sel", np.roll(head_cols(eye), HD, 1)),
                    ("wv", L2("v_w").T), ("wo", L2("out_w").T), ("causal", causal(T))]

    reset = np.tile((np.arange(U * 8) % 8 != 0).astype(np.float32)[None, :], (P, 1))
    upto = np.triu(np.ones((T, T), np.float32))
    packs["ff0"] = [("router", g("L0_ffn_router_w").T), ("reset", reset), ("upto", upto),
                    ("w1", g("L0_ffn_w1").transpose(1, 0, 2).reshape(D, -1)),
                    ("w2", g("L0_ffn_w2").reshape(8, 4, 128, D).transpose(2, 0, 1, 3).reshape(128, -1))]
    packs["ff1"] = [("router", g("L1_ffn_gate_w").T), ("reset", reset),
                    ("w1", g("L1_ffn_w1").transpose(2, 0, 1).reshape(D, -1)),
                    ("w3", g("L1_ffn_w3").transpose(2, 0, 1).reshape(D, -1)),
                    ("w2", g("L1_ffn_w2").transpose(0, 2, 1).reshape(8, 4, 112, D).transpose(2, 0, 1, 3)
                     .reshape(112, -1))]

    A0 = lambda n: g("L0_attn_" + n)
    up = A0("Wup").reshape(32, H, 2, HD).transpose(0, 2, 1, 3).reshape(32, 2 * D)
    bup = A0("bup").reshape(H, 2, HD).transpose(1, 0, 2).reshape(1, 2 * D)
    freq = 1.0 / 10000.0 ** (np.arange(0, HD, 2, dtype=np.float32) / HD)
    angle = np.arange(T, dtype=np.float32)[:, None] * freq[None, :].astype(np.float32)
    cos, sin = np.cos(angle).astype(np.float32), np.sin(angle).astype(np.float32)
    packs["sa0"] = [("wq", A0("Wq")), ("bq", A0("bq")[None, :]), ("wdown", A0("Wdown")), ("bdown", A0("bdown")[:, None]),
                    ("wup", up), ("bup", bup), ("wout", A0("Wout")), ("bout", A0("bout")[None, :]),
                    ("cos", np.concatenate([cos, cos], 1)), ("sin", np.concatenate([-sin, sin], 1))]

    A1 = lambda n: g("L1_attn_" + n)
    packs["sa1"] = [("wproj", np.concatenate([A1(n) for n in ("Wq", "Wk", "Wv", "Wgamma", "Wf")], 1)),
                    ("wg1", A1("Wg1")), ("wg2", A1("Wg2")), ("wo", A1("Wo")),
                    ("norm_w", np.tile(A1("norm_w")[None, :], (P, 1)))]

    A3 = lambda n: g("L3_attn_" + n)
    by_chunk = lambda a: a.reshape(-1, P).T
    wb, wc = (np.tile(A3(n).reshape(2, P, 1, 16), (1, 1, 8, 1)).reshape(2, P, P) for n in ("W_B", "W_C"))
    block = np.arange(16)[:, None, None] * 8 + np.arange(P)[None, None, :] // 16
    spread = (np.arange(P)[None, :, None] == block).astype(np.float32)
    packs["ssm"] = [("ln_g", A3("ln_g")[:, None]), ("ln_b", A3("ln_b")[:, None]), ("w_in", A3("W_in")),
                    ("b_in", by_chunk(A3("b_in"))),
                    ("conv_w", A3("conv_w").reshape(2, P, 4).transpose(1, 0, 2).reshape(P, 8)),
                    ("conv_b", by_chunk(A3("conv_b"))),
                    ("w_bc", np.concatenate([wb[0], wb[1], wc[0], wc[1]], 1)),
                    ("b_bc", np.stack([np.tile(A3("b_B"), 8), np.tile(A3("b_C"), 8)], 1)),
                    ("a", A3("A").reshape(32, P).T), ("d", by_chunk(A3("D"))),
                    ("spread", spread.transpose(1, 0, 2).reshape(P, -1)),
                    ("gather", spread.transpose(2, 0, 1).reshape(P, -1)),
                    ("w_out", A3("W_out").reshape(2, P, D).transpose(1, 0, 2).reshape(P, -1)),
                    ("b_out", A3("b_out")[None, :])]

    F3 = lambda n: g("L3_ffn_" + n)
    w1 = np.concatenate([F3("sw1").transpose(1, 0, 2).reshape(D, 512), F3("w1").transpose(1, 0, 2).reshape(D, 2048)], 1)
    w2 = np.concatenate([F3("sw2").reshape(512, D), F3("w2").reshape(2048, D)], 0)
    b1 = np.concatenate([F3("sb1").reshape(-1), F3("b1").reshape(-1)])
    ex = np.arange(2048)[None, :] // 32 == np.arange(64)[:, None]
    packs["ff3"] = [("router", F3("router_w")), ("router_b", F3("router_b")[None, :]),
                    ("reset", np.tile((np.arange(U * 64) % 64 != 0).astype(np.float32)[None, :], (P, 1))),
                    ("w1", w1), ("b1", by_chunk(b1)), ("w2", w2.reshape(20, P, D).transpose(1, 0, 2).reshape(P, -1)),
                    ("b2", F3("b2")), ("sb2_0", F3("sb2")[0:1]), ("sb2_1", F3("sb2")[1:2]),
                    ("spread", ex.astype(np.float32))]
    return packs


def kernel(**inputs):
    import numpy as np
    import concourse.bacc as bacc
    from concourse.bass_utils import run_bass_kernel_spmd

    nc = bacc.Bacc("TRN2", target_bir_lowering=False, num_devices=1)
    g = lambda n: np.asarray(inputs[n])
    arrays, tables = {}, {}
    for name, parts in _layouts(np, g).items():
        arrays[name], tables[name] = _pack(np, parts)
    arrays["x"] = g("x")
    arrays["ctxT"] = g("ctx_1024").reshape(B * S2, D).T
    arrays["fside"] = g("fside_Bx16xSxS2_0")
    arrays["xa1_mask"] = g("mask_BxSxS2_bf1").view(np.uint8)
    arrays["xa3_mask"] = g("mask_Bx1xSxS2_ik1").reshape(B, T, S2)
    t = {}
    for name, a in arrays.items():
        t[name] = nc.dram_tensor(f"in_{name}", a.shape, mybir.dt.from_np(a.dtype), kind="ExternalInput").ap()
    out = nc.dram_tensor("out_x", (B, T, D), F32, kind="ExternalOutput").ap()
    build(nc, t, tables, out, STAGES)
    feed = {f"in_{n}": np.ascontiguousarray(a) for n, a in arrays.items()}
    r = run_bass_kernel_spmd(nc, [feed], core_ids=[0])
    return r.results[0]["out_x"]
```

```python
from contextlib import ExitStack

import concourse.bass as bass
from concourse import mybir

F32 = mybir.dt.float32
BF16 = mybir.dt.bfloat16
I32 = mybir.dt.int32
U8 = mybir.dt.uint8
ALU = mybir.AluOpType
ACT = mybir.ActivationFunctionType
AXX = mybir.AxisListType.X

P = 128
B = 32
T = 128
D = 128
H = 16
HD = 8
S2 = 120
U = 4
NIT = B // U
W = U * T
CH = 4
EPS = 1e-5
MASKED = -1.0e30


class Phase:

    def __init__(self, nc, name):
        self.nc, self.name, self.ctx, self.sems = nc, name, ExitStack(), []

    def sb(self, name, shape, dt=F32):
        return self.ctx.enter_context(self.nc.sbuf_tensor(f"{self.name}_{name}", shape, dt))

    def ps(self, name, shape, dt=F32):
        return self.ctx.enter_context(self.nc.psum_tensor(f"{self.name}_ps_{name}", shape, dt))

    def sem(self, name):
        s = self.ctx.enter_context(self.nc.semaphore(f"{self.name}_{name}"))
        self.sems.append(s)
        return s

    def close(self):
        for s in self.sems:
            self.nc.sync.sem_clear(s)
        self.nc.all_engine_barrier()
        self.ctx.close()


def bcast(ap, axis, n):
    a = ap.unsqueeze(axis)
    shape = list(a.shape)
    shape[axis] = n
    return a.broadcast_to(shape)


class Rows:

    def __init__(self, ph, x):
        self.x = x
        self.xs = ph.sb("x_rows", [P, U, D])
        self.ready = ph.sem("rows_ready")
        self.free = ph.sem("rows_free")

    def gpsimd(self, pool, i, first=False):
        if not first:
            pool.wait_ge(self.free, i)
        pool.tensor_copy(self.xs[:, :, :], self.x[:, bass.ds(i * U, U), :]).then_inc(self.ready, 1)

    def tensor(self, pe, i, out, ident):
        pe.wait_ge(self.ready, i + 1)
        for u in range(U):
            mm = pe.transpose(out[:, u * T:(u + 1) * T], self.xs[:, u, :], ident)
        mm.then_inc(self.free, 1)


class Stats:

    def __init__(self, ph, consts, tag=""):
        self.c = consts
        self.st = ph.sb(tag + "bnst", [P, U, 6])
        self.mv = ph.sb(tag + "meanvar", [P, U, 2])
        self.ve = ph.sb(tag + "vareps", [P, U])
        self.rstd = ph.sb(tag + "rstd", [P, U])
        self.st_ready = ph.sem(tag + "bnst_ready")
        self.mv_ready = ph.sem(tag + "meanvar_ready")
        self.ve_ready = ph.sem(tag + "vareps_ready")
        self.rstd_ready = ph.sem(tag + "rstd_ready")

    def vector(self, dve, i, r):
        for u in range(U):
            dve.bn_stats(self.st[:, u, :], r[:, u, :]).then_inc(self.st_ready, 1)
        dve.wait_ge(self.st_ready, i * U + U)
        dve.memset(self.ve[:, :], EPS)
        for u in range(U):
            dve.bn_aggr(self.mv[:, u, :], self.st[:, u, :]).then_inc(self.mv_ready, 1)
        dve.wait_ge(self.mv_ready, i * U + U)
        dve.tensor_scalar(self.ve[:, :], self.mv[:, :, 1], EPS, None, ALU.add).then_inc(self.ve_ready, 1)

    def gpsimd(self, pool, i):
        pool.wait_ge(self.ve_ready, i + 1)
        pool.tensor_tensor(self.rstd[:, :], self.ve[:, :], self.c["neghalf"][:, 0:U],
                           ALU.pow).then_inc(self.rstd_ready, 1)


class Norm:

    def __init__(self, ph, x, consts, y, x_times=1.0):
        self.x, self.y, self.x_times = x, y, x_times
        self.r = ph.sb("resid", [P, U, D])
        self.stats = Stats(ph, consts)
        self.y_ready = ph.sem("y_ready")
        self.r_ready = ph.sem("resid_ready")
        self.x_done = ph.sem("x_done")

    def begin(self, dve, i):
        n = self
        dve.wait_ge(n.y_ready, i + 1)
        dve.scalar_tensor_tensor(n.r[:, :, :].rearrange("p u d -> p (u d)"),
                                 n.x[:, bass.ds(i * U, U), :].rearrange("p u d -> p (u d)"), n.x_times,
                                 n.y[:, :], ALU.mult, ALU.add).then_inc(n.r_ready, 1)
        dve.wait_ge(n.r_ready, i + 2)
        n.stats.vector(dve, i, n.r)

    def vector(self, dve, i):
        self.begin(dve, i)
        self.finish(dve, i)

    def finish(self, dve, i):
        n = self
        dve.wait_ge(n.stats.rstd_ready, i + 1)
        for u in range(U):
            dve.tensor_scalar(n.x[:, bass.ds(i * U + u, 1), :].rearrange("p a d -> p (a d)"), n.r[:, u, :],
                              n.stats.mv[:, u, 0:1], n.stats.rstd[:, u:u + 1],
                              ALU.subtract, ALU.mult).then_inc(n.x_done, 1)
        dve.wait_ge(n.x_done, i * U + U)

    def gpsimd(self, pool, i):
        self.stats.gpsimd(pool, i)


def pick(w, table, name):
    rows, off, cols = table[name]
    return w[0:rows, off:off + cols]


def piecewise_phase(nc, x, consts, blob, table):
    ph = Phase(nc, "pw")
    NJ = 8
    w = ph.sb("w", list(blob.shape))
    xT = ph.sb("xT", [P, W])
    s = ph.sb("s", [P, W])
    h = ph.sb("h", [P, NJ, W])
    wc = ph.sb("wc", [P, NJ, D])
    pj = ph.ps("pj", [P, 2, W])
    y = ph.ps("y", [P, W])
    nm = Norm(ph, x, consts, y)
    rows = Rows(ph, x)
    w_in, xt, s_ps, s_sb, h_sb, wc_sb = (ph.sem(n) for n in (
        "w_loaded", "xT_ready", "s_in_psum", "s_ready", "h_ready", "outweights_ready"))
    Win, bin_ = pick(w, table, "Win"), pick(w, table, "bin")
    W1, b1, W2 = pick(w, table, "W1"), pick(w, table, "b1"), pick(w, table, "W2")
    Wout, b2, bout = pick(w, table, "Wout"), pick(w, table, "b2"), pick(w, table, "bout")

    with nc.Block() as block:
        @block.sync
        def _(sp):
            sp.dma_start(w[:, :], blob).then_inc(w_in, 16)

        @block.gpsimd
        def _(pool):
            rows.gpsimd(pool, 0, first=True)
            with pool.Fori(0, NIT - 1) as i:
                rows.gpsimd(pool, i + 1)
                nm.gpsimd(pool, i)
            nm.gpsimd(pool, NIT - 1)

        @block.tensor
        def _(pe):
            pe.wait_ge(w_in, 16)
            with pe.Fori(0, NIT) as i:
                rows.tensor(pe, i, pj[:, 0, :], consts["ident"][:, :])
                pe.wait_ge(xt, i + 1)
                pe.matmul(pj[:, 1, :], Win, xT[:, :], start=True, stop=True).then_inc(s_ps, 1)
                pe.wait_ge(nm.r_ready, i + 1)
                pe.wait_ge(wc_sb, NJ + 1)
                for u in range(U):
                    yu = y[:, u * D:(u + 1) * D]
                    pe.matmul(yu, consts["ones"][0:1, 0:P], bout, start=True, stop=False)
                    pe.matmul(yu, b2, Wout, start=False, stop=False)
                    for j in range(NJ):
                        if u == 0:
                            pe.wait_ge(h_sb, i * NJ + j + 1)
                        mm = pe.matmul(yu, h[:, j, u * T:(u + 1) * T], wc[:, j, :],
                                       start=False, stop=(j == NJ - 1))
                mm.then_inc(nm.y_ready, 1)

        @block.scalar
        def _(act):
            act.wait_ge(w_in, 16)
            with act.Fori(0, NIT) as i:
                act.wait_ge(rows.free, i + 1)
                act.activation(xT[:, :], pj[:, 0, :], ACT.Copy).then_inc(xt, 1)
                act.wait_ge(s_ps, i + 1)
                act.activation(s[:, :], pj[:, 1, :], ACT.Identity, bias=bin_).then_inc(s_sb, 1)
                act.wait_ge(s_sb, i + 1)
                for j in range(NJ):
                    act.activation(h[:, j, :], s[:, :], ACT.Relu, scale=W1[:, j:j + 1],
                                   bias=b1[:, j:j + 1]).then_inc(h_sb, 1)

        @block.vector
        def _(dve):
            dve.sem_inc(nm.r_ready, 1)
            dve.wait_ge(w_in, 16)
            for j in range(NJ):
                dve.tensor_scalar(wc[:, j, :], pick(w, table, "Wout2"), W2[:, j:j + 1], None,
                                  ALU.mult).then_inc(wc_sb, 1)
            dve.sem_inc(wc_sb, 1)
            with dve.Fori(0, NIT) as i:
                nm.vector(dve, i)
    ph.close()


def attention_phase(nc, name, x, consts, t, blob, table, *, scale, bias=None, lut=False):
    ph = Phase(nc, name)
    NK = T if lut else S2
    KW = U * NK
    HF = 2 * HD if lut else HD
    NF = H * HF // P
    HT = H // NF
    G4 = 4
    NU = U * G4
    NS, TR = 2, 8
    w = ph.sb("w", list(blob.shape))
    xT = ph.sb("xT", [P, W])
    q = ph.sb("q", [P, NF, W])
    kT = ph.sb("kT", [P, NF, KW])
    kS = ph.sb("kspread", [P, U, H, NK])
    VP = 32 + HD
    V = ph.sb("v", [NK, U * G4, G4 * VP])
    E = ph.sb("exps", [P, TR, G4 * NK])
    mx = ph.sb("negmax", [P, TR, G4])
    ET = ph.sb("expsT", [NK, TR, G4, T])
    den = ph.sb("sums", [P, U, H])
    rd = ph.sb("rsum", [P, U, H])
    rb = ph.sb("rsums", [P, H, HD])
    rT = ph.sb("rsumsT", [P, 2, T])
    oT = ph.sb("oT", [P, U, T])
    s_ps = ph.ps("s", [P, NS, 512])
    t_ps = ph.ps("t", [P, 2, G4, T])
    o_ps = ph.ps("o", [P, 2, 512])
    y = ph.ps("y", [P, W])
    pj = ph.ps("pj", [P, 512])
    rows = Rows(ph, x)
    nm = Norm(ph, x, consts, y)
    ident = consts["ident"][:, :]
    (w_in, zeroed, pj_ready, pj_done, k_spread, s_ready, b_ready, m_ready, e_ready, sum_ready, t_ready,
     et_ready, pv_ready, rd_ready, rb_ready, o_ready, rt_ready, on_ready) = (ph.sem(n) for n in (
         "w_loaded", "zeroed", "pj_ready", "pj_done", "keys_spread", "s_ready", "biased_ready", "max_ready",
         "exp_ready", "sum_ready", "t_ready", "expT_ready", "pv_ready", "rsum_single", "rsum_ready", "o_ready",
         "rsumT_ready", "oT_ready"))
    s_done = b_ready if bias else e_ready
    S0 = 4
    E0 = 0 if bias else S0
    pw = lambda n: pick(w, table, n)
    if not lut:
        ctx = ph.sb("ctx", [P, KW])
        ctx_in = ph.sem("ctx_loaded")
    masks = bias in ("rows", "heads")
    if masks:
        m_raw = ph.sb("mask_raw", [P, U, NK], t[name + "_mask"].dtype)
        m_bias = ph.sb("mask_bias", [P, U, NK])
        m_in, mb_ready = ph.sem("mask_loaded"), ph.sem("maskbias_ready")
    if bias == "heads":
        FR = 4
        fb = ph.sb("headbias", [P, FR, G4, NK])
        fb_in = [ph.sem(f"headbias_loaded{r}") for r in range(FR)]
        fb_sum = ph.sem("headbias_masked")
    if lut:
        TWO_PI_INV = 512.0 / 6.283185307179586
        ANG = 6.283185307179586 / 512.0
        MAGIC = 12582912.0
        ang = ph.sb("angle", [P, 2, W])
        kk = ph.sb("index", [P, 2, 2, W])
        rr = ph.sb("turns", [P, 2, 2, W])
        sc = ph.sb("cossin", [P, 2, 2, W])
        (a_ready, k_ready, r1_ready, r2_ready, i_ready, cs_ready, den_ready) = (ph.sem(n) for n in (
            "angle_ready", "index_ready", "turns_raw", "turns_ready", "wrapped_ready", "cossin_ready", "rwidth_ready"))
        rw = ph.sb("rwidth", [P, 2])

    J0 = 1 + 2 * NF
    NJ = J0 + 1
    V_AT, X_AT, K_AT, Q_AT = 4, 5, (13 if lut else 8), NU - 1
    SIN_AT = 12
    MASK_AT = (8, 9, 11, 15)
    CTX_AT = 6
    SUM_LAG, T_LAG, PV_LAG, R_LAG, MUL_LAG, Y_LAG = 2, 3, 5, 6, 7, 9
    NORM_AT = 9
    TAIL = NORM_AT + 2

    def unit(n, lag, first, tail):
        m = n - lag
        return None if (m < 0 and first) or (m >= 0 and tail) else m

    def job(i, k):
        return J0 + i * NJ + k

    with nc.Block() as block:
        @block.sync
        def _(sp):
            def load_ctx(i):
                if not lut:
                    sp.dma_start(ctx[:, :], t["ctxT"][:, bass.ds(i * KW, KW)]).then_inc(ctx_in, 16)

            def load_mask(i):
                if masks:
                    src = t[name + "_mask"][bass.ds(i * U, U)].rearrange("u q k -> q u k")
                    sp.dma_start(m_raw[:, :, :], src).then_inc(m_in, 16)

            def load_bias(i, n):
                if bias == "heads":
                    sp.wait_ge(b_ready, i * NU + n - FR + 1 + S0)
                    sp.dma_start(fb[:, n % FR, :, :],
                                 t["fside"][bass.ds(i * U + n // 4, 1), G4 * (n % 4):G4 * (n % 4) + G4]
                                 .rearrange("a h q k -> q (a h) k")).then_inc(fb_in[n % FR], 16)

            def trip(k, last=False):
                for n in range(NU):
                    load_bias(k - 1, n)
                    if n == CTX_AT and not last:
                        if not lut:
                            sp.wait_ge(pj_done, job(k - 1, 0) + 1)
                        load_ctx(k)
                        load_mask(k)

            sp.dma_start(w[:, :], blob).then_inc(w_in, 16)
            load_ctx(0)
            load_mask(0)
            with sp.Fori(1, NIT) as k:
                trip(k)
            trip(NIT, last=True)

        @block.gpsimd
        def _(pool):
            def masked_bias(i, n):
                if bias == "heads":
                    pool.wait_ge(mb_ready, i * U + n // 4 + 1)
                    pool.wait_ge(fb_in[n % FR], (i * (NU // FR) + n // FR + 1) * 16)
                    pool.tensor_tensor(fb[:, n % FR, :, :], fb[:, n % FR, :, :],
                                       bcast(m_bias[:, n // 4, :], 1, G4), ALU.add).then_inc(fb_sum, 1)

            def spread(i, u, first=False):
                pool.wait_ge(pj_done, job(i - 1, 2 + NF))
                if not first:
                    pool.wait_ge(s_ready, (i - 1) * NU + 4 * u + 4)
                for f in range(NF):
                    kp = pool.tensor_tensor(kS[:, u, f * HT:(f + 1) * HT, :],
                                            bcast(kT[:, f, u * NK:(u + 1) * NK], 1, HT),
                                            bcast(pw("own"), 2, NK), ALU.mult)
                kp.then_inc(k_spread, 1)

            def trip(i, first=False, last=False, tail=False):
                for n in range(TAIL if tail else NU):
                    if n == 0 and not (last or tail):
                        rows.gpsimd(pool, i + 1)
                    if not tail and not (last and n + 2 >= NU):
                        masked_bias(i + (n + 2) // NU, (n + 2) % NU)
                    if n == NORM_AT and not first:
                        nm.gpsimd(pool, i - 1)
                    if n in (9, 11, 13, 15) and not (last or tail):
                        spread(i + 1, (n - 9) // 2)

            pool.memset(V[:, :, :], 0.0).then_inc(zeroed, 1)
            rows.gpsimd(pool, 0, first=True)
            for n in range(2):
                masked_bias(0, n)
            pool.wait_ge(w_in, 16)
            for u in range(U):
                spread(0, u, first=True)
            trip(0, first=True)
            with pool.Fori(1, NIT - 1) as i:
                trip(i)
            trip(NIT - 1, last=True)
            trip(NIT, tail=True)

        @block.tensor
        def _(pe):
            def bank(i, k):
                n = job(i, k)
                if not (isinstance(n, int) and n == 0):
                    pe.wait_ge(pj_done, n)
                return pj

            def transpose_x(i):
                rows.tensor(pe, i, bank(i - 1, 1), ident)

            def project(i, a):
                if a == 1 and not lut:
                    pe.wait_ge(ctx_in, (i + 1) * 16)
                if lut:
                    pe.wait_ge(cs_ready, (i + 1) * 2)
                for f in range(NF):
                    out = bank(i - 1, 2 + (1 - a) * NF + f)
                    if lut:
                        for k in range(2):
                            mm = pe.matmul(out[:, :], pw(f"sel{f}{k}"), sc[:, a, k, :], start=(k == 0), stop=(k == 1))
                    elif a == 0:
                        mm = pe.matmul(out[:, :], pw("wq"), xT[:, :], start=True, stop=True)
                    else:
                        mm = pe.matmul(out[:, 0:KW], pw("wk"), ctx[:, :], start=True, stop=True)
                    mm.then_inc(pj_ready, 1)

            def project_values(i):
                out = bank(i, 0)
                for u in range(U):
                    src = xT[:, u * T:(u + 1) * T] if lut else ctx[:, u * NK:(u + 1) * NK]
                    vu = out[0:NK, u * D:(u + 1) * D]
                    if not lut:
                        pe.matmul(vu, consts["ones"][0:1, 0:NK], pw("bv"), start=True, stop=False)
                    mm = pe.matmul(vu, src, pw("wv"), start=lut, stop=True)
                mm.then_inc(pj_ready, 1)

            def trip(i, first=False, last=False, tail=False):
                for n in range(TAIL if tail else NU):
                    if not tail:
                        u, g = n // 4, n % 4
                        if n == 0:
                            pe.wait_ge(pj_done, job(i, 0))
                        if g == 0:
                            pe.wait_ge(k_spread, i * U + u + 1)
                        pe.wait_ge(s_done, i * NU + n - NS + 1 + S0)
                        pe.matmul(s_ps[:, n % NS, 0:G4 * NK], q[:, g * G4 // HT, u * T:(u + 1) * T],
                                  kS[:, u, g * G4:(g + 1) * G4, :].rearrange("p h k -> p (h k)"),
                                  start=True, stop=True).then_inc(s_ready, 1)
                    if n == Q_AT and not (last or tail):
                        project(i + 1, 0)
                    m = unit(n, T_LAG, first, tail)
                    if m is not None:
                        pe.wait_ge(e_ready, i * NU + m + 1 + E0)
                        pe.wait_ge(et_ready, i * NU + m + 1)
                        for j in range(G4):
                            mm = pe.transpose(t_ps[0:NK, m % 2, j, :], E[:, m % TR, j * NK:(j + 1) * NK], ident)
                        mm.then_inc(t_ready, 1)
                    m = unit(n, PV_LAG, first, tail)
                    if m is not None:
                        u, g = m % NU // 4, m % 4
                        pe.wait_ge(et_ready, i * NU + m + 3)
                        if m == 0:
                            pe.wait_ge(pj_done, job(i, 1))
                        if g == 0:
                            pe.wait_ge(on_ready, i * U + m // 4 + 1)
                        for j in range(G4):
                            mm = pe.matmul(o_ps[32 * g:32 * g + 32, u % 2, 0:T], V[:, u * G4 + g, 32 * j:32 * j + 32],
                                           ET[:, m % TR, j, :], start=(j == 0), stop=(j == G4 - 1))
                        mm.then_inc(pv_ready, 1)
                    if n == V_AT and not tail:
                        project_values(i)
                    m = unit(n, R_LAG, first, tail)
                    if m is not None and m % 4 == 3:
                        u = m % NU // 4
                        pe.wait_ge(rb_ready, i * U + m // 4 + 1 + U)
                        pe.transpose(o_ps[:, u % 2, T:2 * T], rb[:, :, :].rearrange("p h e -> p (h e)"), ident
                                     ).then_inc(o_ready, 1)
                    m = unit(n, Y_LAG, first, tail)
                    if m is not None and m % 4 == 3:
                        u = m % NU // 4
                        pe.wait_ge(on_ready, i * U + m // 4 + 1 + 2)
                        if u == 0:
                            pe.wait_ge(nm.r_ready, i + 1)
                        yu = y[:, u * D:(u + 1) * D]
                        if "bo" in table:
                            pe.matmul(yu, consts["ones"][0:1, 0:P], pw("bo"), start=True, stop=False)
                        mm = pe.matmul(yu, oT[:, u, :], pw("wo"), start="bo" not in table, stop=True)
                        if u == U - 1:
                            mm.then_inc(nm.y_ready, 1)
                    if n == X_AT and not (last or tail):
                        transpose_x(i + 1)
                    if n == K_AT and not (last or tail):
                        project(i + 1, 1)

            pe.sem_inc(t_ready, TR)
            pe.wait_ge(w_in, 16)
            transpose_x(0)
            project(0, 1)
            project(0, 0)
            pe.wait_ge(zeroed, 1)
            trip(0, first=True)
            with pe.Fori(1, NIT - 1) as i:
                trip(i)
            trip(NIT - 1, last=True)
            trip(NIT, tail=True)

        @block.scalar
        def _(act):
            def copy_x(i):
                act.wait_ge(rows.free, i + 1)
                act.activation(xT[:, :], pj[:, :], ACT.Copy).then_inc(pj_done, 1)

            def cos_sin(i):
                for a in range(2):
                    act.wait_ge(i_ready, i * 2 + a + 1)
                    act.activation(sc[:, a, :, :], kk[:, a, :, :], ACT.Sin, scale=ANG).then_inc(cs_ready, 1)

            def copy_features(i, a):
                for f in range(NF):
                    act.wait_ge(pj_ready, i * (NJ - 1) + (1 - a) * NF + f + 1)
                    dst, src = (q[:, f, :], pj[:, :]) if a == 0 else (kT[:, f, :], pj[:, 0:KW])
                    b = "bk" if a else "bq"
                    if b in table:
                        act.activation(dst, src, ACT.Identity, bias=pw(b)).then_inc(pj_done, 1)
                    elif a == 0:
                        act.activation(dst, src, ACT.Copy, scale=scale if not bias else 1.0).then_inc(pj_done, 1)
                    else:
                        act.activation(dst, src, ACT.Copy).then_inc(pj_done, 1)

            def trip(i, first=False, last=False, tail=False):
                for n in range(TAIL if tail else NU):
                    if not tail:
                        src = E[:, n % TR, :] if bias else s_ps[:, n % NS, 0:G4 * NK]
                        act.wait_ge(m_ready, i * NU + n + 1)
                        if not bias:
                            act.wait_ge(sum_ready, i * NU + n + 1)
                        for j in range(G4):
                            cut = slice(j * NK, (j + 1) * NK)
                            ex = act.activation(E[:, n % TR, cut], src[:, cut], ACT.Exp, bias=mx[:, n % TR, j:j + 1])
                        ex.then_inc(e_ready, 1)
                    if n == Q_AT and not (last or tail):
                        act.wait_ge(s_ready, (i + 1) * NU)
                        copy_features(i + 1, 0)
                    m = unit(n, T_LAG, first, tail)
                    if m is not None:
                        act.wait_ge(t_ready, i * NU + m + 1 + TR)
                        if not (first and m < TR):
                            act.wait_ge(pv_ready, i * NU + m - TR + 1)
                        act.activation(ET[:, m % TR, :, :], t_ps[0:NK, m % 2, :, :], ACT.Copy
                                       ).then_inc(et_ready, 1)
                    if n == V_AT and not tail:
                        act.wait_ge(pj_ready, J0 - 1 + i * (NJ - 1) + 1)
                        if not first:
                            act.wait_ge(pv_ready, i * NU)
                        act.activation(V[:, :, :].rearrange("k n (j e) -> k n j e", e=VP)[:, :, :, 0:HD],
                                       pj[0:NK, :].rearrange("k (n j e) -> k n j e", j=G4, e=HD),
                                       ACT.Copy).then_inc(pj_done, 1)
                    m = unit(n, R_LAG, first, tail)
                    if m is not None and m % 4 == 3:
                        u = m % NU // 4
                        act.wait_ge(o_ready, i * U + m // 4 + 1)
                        act.wait_ge(on_ready, i * U + m // 4 + 1)
                        act.activation(rT[:, u % 2, :], o_ps[:, u % 2, T:2 * T], ACT.Copy).then_inc(rt_ready, 1)
                    if n == X_AT and not (last or tail):
                        copy_x(i + 1)
                    if lut and n == SIN_AT and not (last or tail):
                        cos_sin(i + 1)
                    if n == K_AT and not (last or tail):
                        act.wait_ge(k_spread, (i + 1) * U)
                        copy_features(i + 1, 1)

            act.sem_inc(et_ready, 2)
            act.wait_ge(w_in, 16)
            act.wait_ge(zeroed, 1)
            copy_x(0)
            if lut:
                cos_sin(0)
            copy_features(0, 1)
            copy_features(0, 0)
            trip(0, first=True)
            with act.Fori(1, NIT - 1) as i:
                trip(i)
            trip(NIT - 1, last=True)
            trip(NIT, tail=True)

        @block.vector
        def _(dve):
            def angle_steps(i, k):
                for a in range(2):
                    if k == 0:
                        dve.tensor_scalar(ang[:, a, :], xT[:, :], rw[:, a:a + 1], pw("shift")[:, a:a + 1],
                                          ALU.mult, ALU.add).then_inc(a_ready, 1)
                    if k == 1:
                        dve.wait_ge(a_ready, i * 2 + a + 1)
                        for f in range(2):
                            dve.tensor_scalar(rr[:, a, f, :], ang[:, a, :], TWO_PI_INV, MAGIC, ALU.mult,
                                              ALU.add).then_inc(k_ready, 1)
                    if k == 2:
                        dve.wait_ge(k_ready, i * 4 + 2 * a + 2)
                        for f in range(2):
                            dve.tensor_scalar(kk[:, a, f, :], rr[:, a, f, :], -MAGIC, 128.0 * (1 - f), ALU.add,
                                              ALU.add).then_inc(r1_ready, 1)
                    if k == 3:
                        dve.wait_ge(r1_ready, i * 4 + 2 * a + 2)
                        dve.tensor_scalar(rr[:, a, :, :], kk[:, a, :, :], 1.0 / 512, MAGIC, ALU.mult,
                                          ALU.add).then_inc(r2_ready, 1)
                    if k == 4:
                        dve.wait_ge(r2_ready, i * 4 + a + 1)
                        dve.tensor_scalar(rr[:, a, :, :], rr[:, a, :, :], -MAGIC, -512.0, ALU.add,
                                          ALU.mult).then_inc(r2_ready, 1)
                    if k == 5:
                        dve.wait_ge(r2_ready, i * 4 + 2 + a + 1)
                        dve.tensor_tensor(kk[:, a, :, :], kk[:, a, :, :], rr[:, a, :, :],
                                          ALU.add).then_inc(i_ready, 1)

            def mask_bias(i, u):
                dve.wait_ge(m_in, i * 16 + 16)
                dve.tensor_scalar(m_bias[:, u, :], m_raw[:, u, :], 0.0, MASKED, ALU.is_equal,
                                  ALU.mult).then_inc(mb_ready, 1)

            def trip(i, first=False, last=False, tail=False):
                for n in range(TAIL if tail else NU):
                    if not tail:
                        u, g = n // 4, n % 4
                        src = s_ps[:, n % NS, 0:G4 * NK]
                        heads = lambda a: a.rearrange("p (h k) -> p h k", h=G4)
                        dve.wait_ge(s_ready, i * NU + n + 1)
                        dve.wait_ge(t_ready, i * NU + n + 1)
                        if bias:
                            dve.wait_ge(sum_ready, i * NU + n + 1)
                            if bias == "causal":
                                add = bcast(pw("causal"), 1, G4)
                            elif bias == "rows":
                                if g == 0:
                                    dve.wait_ge(mb_ready, i * U + u + 1)
                                add = bcast(m_bias[:, u, :], 1, G4)
                            else:
                                dve.wait_ge(fb_sum, i * NU + n + 1)
                                add = fb[:, n % FR, :, :]
                            dve.scalar_tensor_tensor(heads(E[:, n % TR, :]), heads(src), scale, add, ALU.mult,
                                                     ALU.add).then_inc(b_ready, 1)
                            dve.wait_ge(b_ready, i * NU + n + 1 + S0)
                            src = E[:, n % TR, :]
                        dve.tensor_reduce(mx[:, n % TR, :], heads(src), AXX, ALU.max, negate=True).then_inc(m_ready, 1)
                        if masks and n in MASK_AT and not last:
                            mask_bias(i + 1, MASK_AT.index(n))
                    m = unit(n, SUM_LAG, first, tail)
                    if m is not None:
                        u, g = m % NU // 4, m % 4
                        if g == 0:
                            dve.wait_ge(rb_ready, i * U + m // 4 + 1)
                        dve.wait_ge(e_ready, i * NU + m + 1 + E0)
                        dve.tensor_reduce(den[:, u, g * G4:(g + 1) * G4],
                                          E[:, m % TR, :].rearrange("p (h k) -> p h k", h=G4), AXX, ALU.add
                                          ).then_inc(sum_ready, 1)
                        if g == 3:
                            dve.wait_ge(sum_ready, i * NU + m + 1 + TR)
                            if not (first and u == 0):
                                dve.wait_ge(o_ready, i * U + m // 4)
                            dve.reciprocal(rd[:, u, :], den[:, u, :]).then_inc(rd_ready, 1)
                            dve.wait_ge(rd_ready, i * U + m // 4 + 1)
                            dve.tensor_copy(rb[:, :, :], bcast(rd[:, u, :], 2, HD)).then_inc(rb_ready, 1)
                    m = unit(n, MUL_LAG, first, tail)
                    if m is not None and m % 4 == 3:
                        u = m % NU // 4
                        dve.wait_ge(rt_ready, i * U + m // 4 + 1)
                        dve.tensor_tensor(oT[:, u, :], o_ps[:, u % 2, 0:T], rT[:, u % 2, :], ALU.mult
                                          ).then_inc(on_ready, 1)
                    if n == NORM_AT and not first:
                        nm.begin(dve, i - 1)
                    if n == NORM_AT + 1 and not first:
                        nm.finish(dve, i - 1)
                    if lut and 6 <= n < 12 and not (last or tail):
                        if n == 6:
                            dve.wait_ge(pj_done, job(i, 2))
                        angle_steps(i + 1, n - 6)

            dve.sem_inc(nm.r_ready, 1)
            dve.sem_inc(sum_ready, TR)
            dve.sem_inc(on_ready, 2)
            dve.sem_inc(rb_ready, U)
            dve.sem_inc(s_done, S0)
            dve.wait_ge(w_in, 16)
            if masks:
                for u in range(U):
                    mask_bias(0, u)
            if lut:
                dve.tensor_scalar(rw[:, :], pw("wid"), -1.0, None, ALU.mult).then_inc(den_ready, 1)
                dve.wait_ge(den_ready, 1)
                dve.tensor_tensor(rw[:, :], rw[:, :], pw("wid"), ALU.max).then_inc(den_ready, 1)
                dve.wait_ge(den_ready, 2)
                dve.tensor_scalar(rw[:, :], rw[:, :], 1.0, None, ALU.add).then_inc(den_ready, 1)
                dve.wait_ge(den_ready, 3)
                dve.reciprocal(rw[:, :], rw[:, :]).then_inc(den_ready, 1)
                dve.wait_ge(den_ready, 4)
                dve.wait_ge(pj_done, 1)
                for k in range(6):
                    angle_steps(0, k)
            trip(0, first=True)
            with dve.Fori(1, NIT - 1) as i:
                trip(i)
            trip(NIT - 1, last=True)
            trip(NIT, tail=True)
    ph.close()


def top_one(dve, wait, ready, base, pr, best, eq, cum, reset, onehot):
    E = pr.shape[2]
    dve.tensor_reduce(best, pr, AXX, ALU.max).then_inc(ready, 1)
    dve.wait_ge(ready, base + 1)
    dve.tensor_tensor(eq, pr, bcast(best, 2, E), ALU.is_equal).then_inc(ready, 1)
    dve.wait_ge(ready, base + 2)
    dve.tensor_tensor_scan(cum.rearrange("p u e -> p (u e)"), reset, eq.rearrange("p u e -> p (u e)"), 0.0,
                           ALU.mult, ALU.add).then_inc(ready, 1)
    dve.wait_ge(ready, base + 3)
    dve.scalar_tensor_tensor(onehot, cum, 1.0, eq, ALU.is_equal, ALU.mult).then_inc(ready, 1)
    dve.wait_ge(ready, base + 4)


def moe_phase(nc, name, x, consts, blob, table, *, F, gated, capacity=None):
    ph = Phase(nc, name)
    E, FC = 8, 4
    FW = F // FC
    HR = 4
    w = ph.sb("w", list(blob.shape))
    xT = ph.sb("xT", [P, W])
    G = ph.sb("hidden", [FW, 2, FC, W])
    small = lambda n, shape=(P, U, E): ph.sb(n, list(shape))
    pr, p2, eq, cum, cw = (small(n) for n in ("probs", "rest", "equal", "cumul", "share"))
    oh, kept, part = (small(n, (P, U, 2, E)) for n in ("onehot", "kept", "gated"))
    v = small("best", (P, U, 2))
    gate = small("gate", (P, U, 2))
    m1, sm, rs, ss, rss = (small(n, (P, U)) for n in ("lmax", "lsum", "rlsum", "vsum", "rvsum"))
    run = small("run", (P, 2, E))
    misc = ph.ps("misc", [P, 512])
    rt = ph.ps("router", [P, 512])
    h_ps = ph.ps("h", [P, HR, W])
    ye = ph.ps("ye", [P, 2, W])
    rows = Rows(ph, x)
    nm = Norm(ph, x, consts, None)
    (w_in, xt, lg_ready, rstep, ex_ready, oh_ready, pos_ready, run_ready, h_ready, act_ready, g_ready, ye_ready,
     acc_ready, cw_ready) = (ph.sem(n) for n in (
         "w_loaded", "xT_ready", "logits_ready", "router_step", "exp_ready", "onehot_ready", "pos_ready", "run_ready",
         "h_ready", "act_ready", "hidden_ready", "ye_ready", "acc_ready", "share_ready"))
    pw = lambda n: pick(w, table, n)
    RS = 19
    NH = 2 if gated else 1
    NHE = E * FC * NH
    cw2 = ph.sem("weights_ready")
    if gated:
        a_sb = ph.sb("silu", [FW, 2, W])

    def w1(e, f, k):
        o = (e * FC + f) * FW
        return pw("w1" if k == 0 else "w3")[:, o:o + FW]

    with nc.Block() as block:
        @block.sync
        def _(sp):
            sp.dma_start(w[:, :], blob).then_inc(w_in, 16)

        @block.gpsimd
        def _(pool):
            rows.gpsimd(pool, 0, first=True)
            with pool.Fori(0, NIT - 1) as i:
                rows.gpsimd(pool, i + 1)
                nm.gpsimd(pool, i)
            nm.gpsimd(pool, NIT - 1)

        @block.tensor
        def _(pe):
            pe.wait_ge(w_in, 16)
            with pe.Fori(0, NIT) as i:
                rows.tensor(pe, i, misc, consts["ident"][:, :])
                pe.wait_ge(xt, i + 1)
                for u in range(U):
                    mm = pe.matmul(rt[:, u * E:(u + 1) * E], xT[:, u * T:(u + 1) * T], pw("router"), start=True,
                                   stop=True)
                mm.then_inc(lg_ready, 1)

                def hidden(e):
                    for f in range(FC):
                        for k in range(NH):
                            n = (e * FC + f) * NH + k
                            if gated:
                                pe.wait_ge(g_ready, i * E * FC + (e * FC + f) + 1)
                            else:
                                pe.wait_ge(g_ready, i * NHE + n + 1)
                            pe.matmul(h_ps[0:FW, n % HR, :], w1(e, f, k), xT[:, :], start=True,
                                      stop=True).then_inc(h_ready, 1)

                def down(e):
                    pe.wait_ge(acc_ready, i * E + e + 1)
                    for u in range(U):
                        for f in range(FC):
                            if u == 0:
                                pe.wait_ge(g_ready, i * E * FC + e * FC + f + 1 + HR // NH)
                            mm = pe.matmul(ye[:, e % 2, u * D:(u + 1) * D], G[:, e % 2, f, u * T:(u + 1) * T],
                                           pw("w2")[0:FW, (e * FC + f) * D:(e * FC + f + 1) * D],
                                           start=(f == 0), stop=(f == FC - 1))
                    mm.then_inc(ye_ready, 1)

                hidden(0)
                if capacity:
                    pe.wait_ge(oh_ready, i + 1)
                    pe.wait_ge(run_ready, i * U + 1)
                    for u in range(U):
                        out = rt[:, 64 + u * 2 * E:64 + (u + 1) * 2 * E]
                        flat = lambda q: oh[:, q, :, :].rearrange("p k e -> p (k e)")
                        pe.matmul(out, pw("upto"), flat(u), start=True, stop=False)
                        for q in range(u):
                            pe.matmul(out, consts["ones"][:, 0:P], flat(q), start=False, stop=False)
                        mm = pe.matmul(out, consts["ones"][:, 0:P], run[:, :, :].rearrange("p k e -> p (k e)"),
                                       start=False, stop=True)
                    mm.then_inc(pos_ready, 1)
                for e in range(1, E):
                    hidden(e)
                    down(e - 1)
                down(E - 1)

        @block.scalar
        def _(act):
            with act.Fori(0, NIT) as i:
                act.wait_ge(rows.free, i + 1)
                act.activation(xT[:, :], misc[:, :], ACT.Copy).then_inc(xt, 1)
                act.wait_ge(rstep, i * RS + 2)
                act.activation(pr[:, :, :], pr[:, :, :], ACT.Exp).then_inc(ex_ready, 1)
                for n in range(E * FC):
                    e, f = n // FC, n % FC
                    act.wait_ge(h_ready, i * NHE + NH * n + 1)
                    if f == 0:
                        act.wait_ge(ye_ready, i * E + e + 1)
                    if gated:
                        act.wait_ge(g_ready, i * E * FC + n + 1)
                        act.activation(a_sb[:, n % 2, :], h_ps[0:FW, (2 * n) % HR, :], ACT.Silu
                                       ).then_inc(act_ready, 1)
                    else:
                        act.activation(G[:, e % 2, f, :], h_ps[0:FW, n % HR, :], ACT.Gelu).then_inc(g_ready, 1)

        @block.vector
        def _(dve):
            dve.sem_inc(acc_ready, 2)
            dve.sem_inc(g_ready, HR // NH)
            dve.sem_inc(ye_ready, 2)
            dve.memset(run[:, :, :], 0.0).then_inc(run_ready, 1)
            dve.wait_ge(run_ready, 1)
            dve.wait_ge(w_in, 16)
            with dve.Fori(0, NIT) as i:
                k = i * RS
                reset = pw("reset")
                dve.wait_ge(lg_ready, i + 1)
                lg = rt[:, 0:U * E].rearrange("p (u e) -> p u e", u=U)
                dve.tensor_reduce(m1[:, :], lg, AXX, ALU.max).then_inc(rstep, 1)
                dve.wait_ge(rstep, k + 1)
                dve.tensor_tensor(pr[:, :, :], lg, bcast(m1[:, :], 2, E), ALU.subtract).then_inc(rstep, 1)
                dve.wait_ge(ex_ready, i + 1)
                dve.tensor_reduce(sm[:, :], pr[:, :, :], AXX, ALU.add).then_inc(rstep, 1)
                dve.wait_ge(rstep, k + 3)
                dve.reciprocal(rs[:, :], sm[:, :]).then_inc(rstep, 1)
                dve.wait_ge(rstep, k + 4)
                dve.tensor_tensor(pr[:, :, :], pr[:, :, :], bcast(rs[:, :], 2, E), ALU.mult).then_inc(rstep, 1)
                dve.wait_ge(rstep, k + 5)
                top_one(dve, None, rstep, k + 5, pr[:, :, :], v[:, :, 0], eq[:, :, :], cum[:, :, :], reset,
                        oh[:, :, 0, :])
                dve.scalar_tensor_tensor(p2[:, :, :], oh[:, :, 0, :], -2.0, pr[:, :, :], ALU.mult, ALU.add
                                         ).then_inc(rstep, 1)
                dve.wait_ge(rstep, k + 10)
                top_one(dve, None, rstep, k + 10, p2[:, :, :], v[:, :, 1], eq[:, :, :], cum[:, :, :], reset,
                        oh[:, :, 1, :])
                dve.sem_inc(oh_ready, 1)
                dve.tensor_tensor(ss[:, :], v[:, :, 0], v[:, :, 1], ALU.add).then_inc(rstep, 1)
                dve.wait_ge(rstep, k + 15)
                dve.reciprocal(rss[:, :], ss[:, :]).then_inc(rstep, 1)
                dve.wait_ge(rstep, k + 16)
                dve.tensor_tensor(gate[:, :, :], v[:, :, :], bcast(rss[:, :], 2, 2), ALU.mult).then_inc(rstep, 1)
                src = oh
                if capacity:
                    src = kept
                    dve.wait_ge(pos_ready, i + 1)
                    dve.scalar_tensor_tensor(kept[:, :, :, :].rearrange("p u k e -> p (u k e)"),
                                             rt[:, 64:64 + U * 2 * E], float(capacity),
                                             oh[:, :, :, :].rearrange("p u k e -> p (u k e)"),
                                             ALU.is_le, ALU.mult).then_inc(cw_ready, 1)
                    for u in range(U):
                        dve.tensor_tensor(run[:, :, :], run[:, :, :], oh[:, u, :, :], ALU.add).then_inc(run_ready, 1)
                        dve.wait_ge(run_ready, i * U + u + 2)
                    dve.wait_ge(cw_ready, i + 1)
                dve.wait_ge(rstep, k + 17)
                for q in range(2):
                    dve.tensor_tensor(part[:, :, q, :], src[:, :, q, :], bcast(gate[:, :, q], 2, E),
                                      ALU.mult).then_inc(rstep, 1)
                dve.wait_ge(rstep, k + 19)
                dve.tensor_tensor(cw[:, :, :], part[:, :, 0, :], part[:, :, 1, :], ALU.add).then_inc(cw2, 1)
                dve.wait_ge(cw2, i + 1)

                def gates(e):
                    for f in range(FC):
                        n = e * FC + f
                        dve.wait_ge(act_ready, i * E * FC + n + 1)
                        dve.wait_ge(h_ready, i * NHE + 2 * n + 2)
                        if f == 0:
                            dve.wait_ge(ye_ready, i * E + e + 1)
                        dve.tensor_tensor(G[:, e % 2, f, :], a_sb[:, n % 2, :], h_ps[0:FW, (2 * n + 1) % HR, :],
                                          ALU.mult).then_inc(g_ready, 1)

                def weigh(e):
                    dve.wait_ge(ye_ready, i * E + e + 3)
                    if e == 0:
                        prev = lambda u: x[:, bass.ds(i * U + u, 1), :].rearrange("p a d -> p (a d)")
                    else:
                        dve.wait_ge(acc_ready, i * E + e + 2)
                        prev = lambda u: nm.r[:, u, :]
                    for u in range(U):
                        last = dve.scalar_tensor_tensor(nm.r[:, u, :], ye[:, e % 2, u * D:(u + 1) * D],
                                                        cw[:, u, e:e + 1], prev(u), ALU.mult, ALU.add)
                    last.then_inc(acc_ready, 1)

                if gated:
                    gates(0)
                for e in range(1, E):
                    if gated:
                        gates(e)
                    weigh(e - 1)
                weigh(E - 1)
                dve.wait_ge(acc_ready, i * E + E + 2)
                nm.stats.vector(dve, i, nm.r)
                nm.finish(dve, i)
    ph.close()


def heads_phase(nc, x, consts, blob, table):
    ph = Phase(nc, "sa0")
    LAT = 32
    w = ph.sb("w", list(blob.shape))
    xT = ph.sb("xT", [P, W])
    lat = ph.sb("latent", [LAT, W])
    RQ = 2
    qkv = ph.sb("qkv", [P, RQ, 3, H, HD])
    t1 = ph.sb("rope_cos", [P, RQ, 2, H, HD])
    t2 = ph.sb("rope_sin", [P, RQ, 2, H, HD])
    qk = ph.sb("rotated", [P, RQ, 2, H, HD])
    pq = ph.sb("products", [P, RQ, H, H, HD])
    pv = ph.sb("weighted", [P, H, HD, H])
    att = ph.sb("att", [P, RQ, H, H])
    mx, sm, rs = (ph.sb(n, [P, RQ, H]) for n in ("max", "sum", "rsum"))
    ov = ph.sb("ov", [P, RQ, H, HD])
    o = ph.sb("o", [P, U, D])
    oT = ph.sb("oT", [P, U, T])
    xt_ps, lat_ps = ph.ps("xT", [P, W]), ph.ps("latent", [LAT, W])
    qkv_ps = ph.ps("qkv", [P, 2, 512])
    y = ph.ps("y", [P, W])
    rows = Rows(ph, x)
    nm = Norm(ph, x, consts, y)
    (w_in, xt, lp, lt, qkv_in, qkv_out, cos_done, rot_done, pq_done, att_done, max_done, sub_done, exp_done, sum_done,
     pv_done, ov_done, o_done, ot_in, ot_out) = (ph.sem(n) for n in (
         "w_loaded", "xT_ready", "latent_in_psum", "latent_ready", "qkv_in_psum", "qkv_ready", "roped_parts",
         "rotated_ready", "products_ready", "att_ready", "max_ready", "shifted_ready", "exp_ready", "sum_ready",
         "weighted_ready", "ov_ready", "o_ready", "ot_in_psum", "ot_ready"))
    pw = lambda n: pick(w, table, n)
    yo = lambda u: y[:, u * D:(u + 1) * D]

    with nc.Block() as block:
        @block.sync
        def _(sp):
            sp.dma_start(w[:, :], blob).then_inc(w_in, 16)

        @block.gpsimd
        def _(pool):
            pool.wait_ge(w_in, 16)
            pool.sem_inc(pq_done, RQ)
            rows.gpsimd(pool, 0, first=True)

            def rotate(i):
                for u in range(U):
                    s = u % RQ
                    n = i * U + u
                    pool.wait_ge(qkv_out, n + 1 + 2)
                    src = qkv[:, s, 0:2, :, :].rearrange("p a h e -> p (a h) e")
                    ca = t1[:, s, :, :, :].rearrange("p a h e -> p (a h) e")
                    si = t2[:, s, :, :, :].rearrange("p a h e -> p (a h) e")
                    pool.tensor_tensor(ca, src, bcast(pw("cos"), 1, 2 * H), ALU.mult).then_inc(cos_done, 1)
                    pool.tensor_tensor(si[:, :, 0:HD // 2], src[:, :, HD // 2:HD],
                                       bcast(pw("sin")[:, 0:HD // 2], 1, 2 * H), ALU.mult).then_inc(cos_done, 1)
                    pool.tensor_tensor(si[:, :, HD // 2:HD], src[:, :, 0:HD // 2],
                                       bcast(pw("sin")[:, HD // 2:HD], 1, 2 * H), ALU.mult).then_inc(cos_done, 1)
                    pool.wait_ge(cos_done, n * 3 + 3)
                    pool.tensor_tensor(qk[:, s, :, :, :].rearrange("p a h e -> p (a h) e"), ca, si,
                                       ALU.add).then_inc(rot_done, 1)
                    pool.wait_ge(rot_done, n + 1)
                    pool.wait_ge(att_done, n + 1)
                    pool.tensor_tensor(pq[:, s, :, :, :], bcast(qk[:, s, 0, :, :], 2, H),
                                       bcast(qk[:, s, 1, :, :], 1, H), ALU.mult).then_inc(pq_done, 1)

            with pool.Fori(0, NIT - 1) as i:
                rows.gpsimd(pool, i + 1)
                rotate(i)
                nm.gpsimd(pool, i)
            rotate(NIT - 1)
            nm.gpsimd(pool, NIT - 1)

        def out_row(pe, i, v):
            pe.wait_ge(o_done, i * U + v + 1)
            if v == 0:
                pe.wait_ge(nm.r_ready, i + 1)
            pe.transpose(yo(v), o[:, v, :], consts["ident"][:, :]).then_inc(ot_in, 1)
            pe.wait_ge(ot_out, i * U + v + 1)
            pe.matmul(yo(v), consts["ones"][0:1, 0:P], pw("bout"), start=True, stop=False)
            mm = pe.matmul(yo(v), oT[:, v, :], pw("wout"), start=False, stop=True)
            if v == U - 1:
                mm.then_inc(nm.y_ready, 1)

        @block.tensor
        def _(pe):
            pe.wait_ge(w_in, 16)
            with pe.Fori(0, NIT) as i:
                rows.tensor(pe, i, xt_ps, consts["ident"][:, :])
                pe.wait_ge(xt, i + 1)
                pe.matmul(lat_ps[:, :], pw("wdown"), xT[:, :], start=True, stop=True).then_inc(lp, 1)
                pe.wait_ge(lt, i + 1)
                for u in range(U + 2):
                    if u < U:
                        bank = qkv_ps[:, u % 2, :]
                        pe.wait_ge(qkv_out, i * U + u + 1)
                        pe.matmul(bank[:, 0:D], consts["ones"][0:1, 0:P], pw("bq"), start=True, stop=False)
                        pe.matmul(bank[:, 0:D], xT[:, u * T:(u + 1) * T], pw("wq"), start=False, stop=True)
                        pe.matmul(bank[:, D:3 * D], consts["ones"][0:1, 0:P], pw("bup"), start=True, stop=False)
                        pe.matmul(bank[:, D:3 * D], lat[:, u * T:(u + 1) * T], pw("wup"), start=False,
                                  stop=True).then_inc(qkv_in, 1)
                    v = u - 2
                    if v >= 0:
                        out_row(pe, i, v)

        @block.scalar
        def _(act):
            act.sem_inc(qkv_out, 2)
            act.wait_ge(w_in, 16)
            with act.Fori(0, NIT) as i:
                act.wait_ge(rows.free, i + 1)
                act.activation(xT[:, :], xt_ps[:, :], ACT.Copy).then_inc(xt, 1)
                act.wait_ge(lp, i + 1)
                act.activation(lat[:, :], lat_ps[:, :], ACT.Identity, bias=pw("bdown")[:, 0:1]).then_inc(lt, 1)
                for u in range(U + 2):
                    if u < U:
                        n = i * U + u
                        act.wait_ge(qkv_in, n + 1)
                        act.wait_ge(pv_done, n + 1)
                        act.activation(qkv[:, u % RQ, :, :, :],
                                       qkv_ps[:, u % 2, 0:3 * D].rearrange("p (a h e) -> p a h e", a=3, h=H),
                                       ACT.Copy).then_inc(qkv_out, 1)
                    v = u - 1
                    if 0 <= v < U:
                        act.wait_ge(sub_done, i * U + v + 1)
                        act.activation(att[:, v % RQ, :, :], att[:, v % RQ, :, :], ACT.Exp,
                                       scale=HD ** -0.5).then_inc(exp_done, 1)
                    v = u - 2
                    if v >= 0:
                        act.wait_ge(ot_in, i * U + v + 1)
                        act.activation(oT[:, v, :], yo(v), ACT.Copy).then_inc(ot_out, 1)

        @block.vector
        def _(dve):
            dve.sem_inc(nm.r_ready, 1)
            dve.sem_inc(att_done, RQ)
            dve.sem_inc(pv_done, RQ)
            with dve.Fori(0, NIT) as i:
                for u in range(U + 1):
                    if u < U:
                        n, s = i * U + u, u % RQ
                        dve.wait_ge(pq_done, n + 1 + RQ)
                        dve.tensor_reduce(att[:, s, :, :], pq[:, s, :, :, :], AXX, ALU.add).then_inc(att_done, 1)
                        dve.wait_ge(att_done, n + 1 + RQ)
                        dve.tensor_reduce(mx[:, s, :], att[:, s, :, :], AXX, ALU.max).then_inc(max_done, 1)
                        dve.wait_ge(max_done, n + 1)
                        dve.tensor_tensor(att[:, s, :, :], att[:, s, :, :], bcast(mx[:, s, :], 2, H),
                                          ALU.subtract).then_inc(sub_done, 1)
                    v = u - 1
                    if v >= 0:
                        n, s = i * U + v, v % RQ
                        dve.wait_ge(exp_done, n + 1)
                        dve.tensor_reduce(sm[:, s, :], att[:, s, :, :], AXX, ALU.add).then_inc(sum_done, 1)
                        dve.tensor_tensor(pv[:, :, :, :], bcast(att[:, s, :, :], 2, HD),
                                          bcast(qkv[:, s, 2, :, :].rearrange("p g e -> p e g"), 1, H),
                                          ALU.mult).then_inc(pv_done, 1)
                        dve.wait_ge(sum_done, 2 * n + 1)
                        dve.reciprocal(rs[:, s, :], sm[:, s, :]).then_inc(sum_done, 1)
                        dve.wait_ge(pv_done, n + 1 + RQ)
                        dve.tensor_reduce(ov[:, s, :, :], pv[:, :, :, :], AXX, ALU.add).then_inc(ov_done, 1)
                        dve.wait_ge(ov_done, n + 1)
                        dve.wait_ge(sum_done, 2 * n + 2)
                        dve.tensor_tensor(o[:, v, :].rearrange("p (h e) -> p h e", h=H), ov[:, s, :, :],
                                          bcast(rs[:, s, :], 2, HD), ALU.mult).then_inc(o_done, 1)
                nm.vector(dve, i)
    ph.close()


HQ = 4
QW = D // HQ
RW = 4 * QW + HQ


def delta_phase(nc, x, consts, blob, table, rec, outs):
    ph = Phase(nc, "sa1")
    PC = 3 * D + 2 * H
    w = ph.sb("w", list(blob.shape))
    pw = lambda n: pick(w, table, n)
    w_in = ph.sem("w_loaded")
    if True:
        xT = ph.sb("xT", [P, W])
        sg = ph.sb("sigmoid", [P, 2, PC])
        qkv = ph.sb("qkv", [P, 2, 3, H, HD])
        sq = ph.sb("ksquare", [P, 2, H, HD])
        ss, nr, co, c2 = (ph.sb(n, [P, 2, H]) for n in ("ksum", "knorm", "coef", "coef_raw"))
        rc = ph.sb("records", [P, 2, HQ, RW])
        xt_ps = ph.ps("xT", [P, W])
        pj = ph.ps("pj", [P, 2, 512])
        rows = Rows(ph, x)
        (xt, pj_in, sg_out, qkv_done, sq_done, ss_done, nr_done, co_done, rc_done) = (ph.sem(n) for n in (
            "xT_ready", "pj_ready", "sigmoid_ready", "qkv_ready", "ksquare_ready", "ksum_ready", "knorm_ready",
            "coef_ready", "record_parts"))
        stored = [ph.sem(f"record_stored{r}") for r in range(2)]
        half = ph.sb("half", [P, H])
        half_set = ph.sem("half_set")
        nr2 = ph.sem("rnorm_ready")

        with nc.Block() as block:
            @block.sync
            def _(sp):
                sp.dma_start(w[:, :], blob).then_inc(w_in, 16)
                with sp.Fori(0, NIT) as i:
                    for u in range(U):
                        sp.wait_ge(rc_done, (i * U + u + 1) * 5 + 10)
                        sp.dma_start(rec[bass.ds(i * U + u, 1)].rearrange("a h t w -> t (a h) w"), rc[:, u % 2, :, :]
                                     ).then_inc(stored[u % 2], 16)
                for s in stored:
                    sp.wait_ge(s, B // 2 * 16 + 16)

            @block.gpsimd
            def _(pool):
                pool.memset(half[:, :], 0.5).then_inc(half_set, 1)
                rows.gpsimd(pool, 0, first=True)
                pool.wait_ge(half_set, 1)

                def knorm(i):
                    for u in range(U):
                        pool.wait_ge(ss_done, i * U + u + 1)
                        pool.tensor_tensor(nr[:, u % 2, :], ss[:, u % 2, :], half[:, :], ALU.pow
                                           ).then_inc(nr_done, 1)

                with pool.Fori(0, NIT - 1) as i:
                    rows.gpsimd(pool, i + 1)
                    knorm(i)
                knorm(NIT - 1)

            @block.tensor
            def _(pe):
                pe.wait_ge(w_in, 16)
                with pe.Fori(0, NIT) as i:
                    rows.tensor(pe, i, xt_ps, consts["ident"][:, :])
                    pe.wait_ge(xt, i + 1)
                    for u in range(U):
                        pe.wait_ge(qkv_done, (i * U + u) * 1 + 1)
                        pe.matmul(pj[:, u % 2, 0:PC], xT[:, u * T:(u + 1) * T], pw("wproj"), start=True,
                                  stop=True).then_inc(pj_in, 1)

            @block.scalar
            def _(act):
                with act.Fori(0, NIT) as i:
                    act.wait_ge(rows.free, i + 1)
                    act.activation(xT[:, :], xt_ps[:, :], ACT.Copy).then_inc(xt, 1)
                    for u in range(U):
                        act.wait_ge(pj_in, i * U + u + 1)
                        act.wait_ge(rc_done, (i * U + u + 1) * 5)
                        act.activation(sg[:, u % 2, :], pj[:, u % 2, 0:PC], ACT.Sigmoid).then_inc(sg_out, 1)

            @block.vector
            def _(dve):
                dve.sem_inc(qkv_done, 2)
                dve.sem_inc(rc_done, 10)
                dve.sem_inc(stored[0], 16)
                dve.sem_inc(stored[1], 16)
                with dve.Fori(0, NIT) as i:
                    for u in range(U):
                        n, s = i * U + u, u % 2
                        quarter = lambda k, a: rc[:, s, :, k * QW:(k + 1) * QW].rearrange("p q (h e) -> p q h e", e=HD)
                        heads = lambda t: t.rearrange("p (q h) e -> p q h e", q=HQ)
                        dve.wait_ge(sg_out, n + 1)
                        dve.tensor_tensor(qkv[:, s, :, :, :].rearrange("p a h e -> p (a h e)"), sg[:, s, 0:3 * D],
                                          pj[:, s, 0:3 * D], ALU.mult).then_inc(qkv_done, 1)
                        dve.tensor_tensor(c2[:, s, :], sg[:, s, 3 * D:3 * D + H], sg[:, s, 3 * D + H:PC],
                                          ALU.mult).then_inc(co_done, 1)
                        dve.wait_ge(qkv_done, n + 3)
                        dve.tensor_tensor(sq[:, s, :, :], qkv[:, s, 1, :, :], qkv[:, s, 1, :, :],
                                          ALU.mult).then_inc(sq_done, 1)
                        dve.wait_ge(co_done, 2 * n + 1)
                        dve.scalar_tensor_tensor(co[:, s, :], c2[:, s, :], -1.0, sg[:, s, 3 * D + H:PC], ALU.mult,
                                                 ALU.mult).then_inc(co_done, 1)
                        dve.wait_ge(sq_done, n + 1)
                        dve.tensor_reduce(ss[:, s, :], sq[:, s, :, :], AXX, ALU.add).then_inc(ss_done, 1)
                        dve.wait_ge(stored[s], (i * 2 + u // 2 + 1) * 16)
                        rq = lambda k: rc[:, s, :, k * QW:(k + 1) * QW]
                        flat = lambda k: qkv[:, s, k, :, :].rearrange("p (q h) e -> p q (h e)", q=HQ)
                        dve.tensor_copy(rq(0), flat(0)).then_inc(rc_done, 1)
                        dve.tensor_copy(rq(2), flat(2)).then_inc(rc_done, 1)
                        dve.tensor_copy(rc[:, s, :, 4 * QW:RW],
                                        sg[:, s, 3 * D + H:PC].rearrange("p (q h) -> p q h", q=HQ)).then_inc(rc_done, 1)
                        dve.wait_ge(nr_done, n * 1 + 1)
                        dve.tensor_scalar(nr[:, s, :], nr[:, s, :], 1e-12, None, ALU.max).then_inc(nr2, 1)
                        dve.wait_ge(nr2, 2 * n + 1)
                        dve.reciprocal(nr[:, s, :], nr[:, s, :]).then_inc(nr2, 1)
                        dve.wait_ge(nr2, 2 * n + 2)
                        dve.tensor_tensor(rc[:, s, :, QW:2 * QW].rearrange("p q (h e) -> p q h e", e=HD),
                                          heads(qkv[:, s, 1, :, :]),
                                          bcast(nr[:, s, :].rearrange("p (q h) -> p q h", q=HQ), 3, HD),
                                          ALU.mult).then_inc(rc_done, 1)
                        dve.wait_ge(rc_done, n * 5 + 14)
                        dve.tensor_tensor(rc[:, s, :, 3 * QW:4 * QW].rearrange("p q (h e) -> p q h e", e=HD),
                                          rc[:, s, :, QW:2 * QW].rearrange("p q (h e) -> p q h e", e=HD),
                                          bcast(co[:, s, :].rearrange("p (q h) -> p q h", q=HQ), 3, HD),
                                          ALU.mult).then_inc(rc_done, 1)
    ph.close()

    ph = Phase(nc, "scan")
    TC, HH = 16, H // HQ
    NC = T // TC
    rb = ph.sb("records", [P, 2, TC, RW])
    SH = ph.sb("states", [P, TC + 1, HH, HD, HD])
    tmp, kU = ph.sb("aS", [P, HH, HD, HD]), ph.sb("kU", [P, HH, HD, HD])
    Sd = ph.sb("decayed", [P, 2, HH, HD, HD])
    ra, uu = ph.sb("aS_sum", [P, HH, HD]), ph.sb("u", [P, HH, HD])
    qS = ph.sb("qS", [P, TC, HH, HD, HD])
    ob = ph.sb("out", [P, 2, TC, HH, HD])
    (tmp_done, ra_done, u_done, ku_done, s_done, sd_done, qs_done, o_done) = (ph.sem(n) for n in (
        "aS_ready", "aS_sum_ready", "u_ready", "kU_ready", "state_ready", "decayed_ready", "qS_ready", "out_ready"))
    rb_in = [ph.sem(f"records_loaded{r}") for r in range(2)]
    o_out = [ph.sem(f"out_stored{r}") for r in range(2)]
    recp = rec.rearrange("b q t w -> (b q) (t w)")
    outp = outs.rearrange("b q t w -> (b q) (t w)")
    with nc.Block() as block:
        @block.sync
        def _(sp):
            for k in range(2):
                sp.dma_start(rb[:, k, :, :].rearrange("p t w -> p (t w)"), recp[:, k * TC * RW:(k + 1) * TC * RW]
                             ).then_inc(rb_in[k], 16)
            for c in range(NC):
                sp.wait_ge(o_done, c + 1 + 1)
                sp.dma_start(outp[:, c * TC * QW:(c + 1) * TC * QW],
                             ob[:, c % 2, :, :, :].rearrange("p t h e -> p (t h e)")).then_inc(o_out[c % 2], 16)
                if c + 2 < NC:
                    k = c + 2
                    sp.dma_start(rb[:, k % 2, :, :].rearrange("p t w -> p (t w)"),
                                 recp[:, k * TC * RW:(k + 1) * TC * RW]).then_inc(rb_in[k % 2], 16)
            for s in o_out:
                sp.wait_ge(s, NC // 2 * 16 + 16)

        def field(c2, t, k):
            return rb[:, c2, t, k * QW:(k + 1) * QW].rearrange("p (h e) -> p h e", h=HH)

        def read_out(pool, c, c2, t):
            if t == 1:
                pool.wait_ge(o_done, c + 1)
            pool.tensor_tensor(qS[:, t - 1, :, :, :], SH[:, t, :, :, :], bcast(field(c2, t - 1, 0), 2, HD),
                               ALU.mult).then_inc(qs_done, 1)

        @block.gpsimd
        def _(pool):
            with pool.Fori(0, NC // 2) as cc:
                for c2 in range(2):
                    c = cc * 2 + c2
                    pool.wait_ge(rb_in[c2], cc * 16 + 16)
                    for t in range(TC):
                        f = rb[:, c2, t, 4 * QW:RW]
                        pool.wait_ge(s_done, c * (TC + 1) + t + 1)
                        pool.tensor_tensor(Sd[:, t % 2, :, :, :].rearrange("p h a b -> p h (a b)"),
                                           SH[:, t, :, :, :].rearrange("p h a b -> p h (a b)"),
                                           bcast(f, 2, HD * HD), ALU.mult).then_inc(sd_done, 1)
                        if t > 0:
                            read_out(pool, c, c2, t)
                    pool.wait_ge(s_done, c * (TC + 1) + TC + 1)
                    read_out(pool, c, c2, TC)

        @block.vector
        def _(dve):
            dve.sem_inc(o_done, 1)
            dve.memset(SH[:, 0, :, :, :], 0.0).then_inc(s_done, 1)
            dve.wait_ge(s_done, 1)
            for k in range(2):
                dve.sem_inc(o_out[k], 16)
            with dve.Fori(0, NC // 2) as cc:
                for c2 in range(2):
                    c = cc * 2 + c2
                    dve.wait_ge(rb_in[c2], cc * 16 + 16)
                    for t in range(TC):
                        n = c * TC + t
                        dve.tensor_tensor(tmp[:, :, :, :], SH[:, t, :, :, :], bcast(field(c2, t, 3), 2, HD),
                                          ALU.mult).then_inc(tmp_done, 1)
                        dve.wait_ge(tmp_done, n + 1)
                        dve.tensor_reduce(ra[:, :, :], tmp[:, :, :, :], AXX, ALU.add).then_inc(ra_done, 1)
                        dve.wait_ge(ra_done, n + 1)
                        dve.tensor_tensor(uu[:, :, :], ra[:, :, :], field(c2, t, 2), ALU.add).then_inc(u_done, 1)
                        dve.wait_ge(u_done, n + 1)
                        dve.tensor_tensor(kU[:, :, :, :], bcast(uu[:, :, :], 3, HD), bcast(field(c2, t, 1), 2, HD),
                                          ALU.mult).then_inc(ku_done, 1)
                        dve.wait_ge(ku_done, n + 1)
                        dve.wait_ge(sd_done, n + 1)
                        dve.tensor_tensor(SH[:, t + 1, :, :, :], Sd[:, t % 2, :, :, :], kU[:, :, :, :],
                                          ALU.add).then_inc(s_done, 1)
                        dve.wait_ge(s_done, c * (TC + 1) + t + 2)
                    dve.wait_ge(qs_done, c * TC + TC)
                    dve.wait_ge(o_out[c2], cc * 16 + 16)
                    dve.tensor_reduce(ob[:, c2, :, :, :], qS[:, :, :, :, :], AXX, ALU.add).then_inc(o_done, 1)
                    dve.tensor_copy(SH[:, 0, :, :, :], SH[:, TC, :, :, :]).then_inc(s_done, 1)
                    dve.wait_ge(s_done, (c + 1) * (TC + 1) + 1)
    ph.close()

    ph = Phase(nc, "gate")
    w = ph.sb("w", list(blob.shape))
    xT = ph.sb("xT", [P, W])
    g1 = ph.sb("g1", [HD, W])
    gt, ol, og, z, zn, zT = (ph.sb(n, [P, U, D]) for n in ("gate", "o", "gated", "z", "zn", "zT"))
    xt_ps, g1_ps, gt_ps, z_ps, y = (ph.ps(n, [P, W]) for n in ("xT", "g1", "gate", "zT", "y"))
    rows = Rows(ph, x)
    nm = Norm(ph, x, consts, y)
    inner = Stats(ph, consts, "inner_")
    (w_in, ol_in, xt, g1_in, g1_out, gt_in, gt_out, og_done, z_done, zn_done, zt_in, zt_out) = (ph.sem(n) for n in (
        "w_loaded", "o_loaded", "xT_ready", "g1_in_psum", "g1_ready", "gate_in_psum", "gate_ready", "gated_ready",
        "z_ready", "zn_ready", "zT_in_psum", "zT_ready"))
    flat = lambda a: a[:, :, :].rearrange("p u d -> p (u d)")
    with nc.Block() as block:
        @block.sync
        def _(sp):
            sp.dma_start(w[:, :], blob).then_inc(w_in, 16)
            with sp.Fori(0, NIT) as i:
                sp.wait_ge(og_done, i + 1)
                for u in range(U):
                    sp.dma_start(ol[:, u, :].rearrange("p (q e) -> p q e", q=HQ),
                                 outs[bass.ds(i * U + u, 1)].rearrange("a q t e -> t (a q) e")).then_inc(ol_in, 16)

        @block.gpsimd
        def _(pool):
            rows.gpsimd(pool, 0, first=True)
            with pool.Fori(0, NIT - 1) as i:
                rows.gpsimd(pool, i + 1)
                inner.gpsimd(pool, i)
                nm.gpsimd(pool, i)
            inner.gpsimd(pool, NIT - 1)
            nm.gpsimd(pool, NIT - 1)

        @block.tensor
        def _(pe):
            pe.wait_ge(w_in, 16)
            with pe.Fori(0, NIT) as i:
                rows.tensor(pe, i, xt_ps, consts["ident"][:, :])
                pe.wait_ge(xt, i + 1)
                pe.matmul(g1_ps[0:HD, :], pw("wg1"), xT[:, :], start=True, stop=True).then_inc(g1_in, 1)
                pe.wait_ge(g1_out, i + 1)
                for u in range(U):
                    mm = pe.matmul(gt_ps[:, u * D:(u + 1) * D], g1[:, u * T:(u + 1) * T], pw("wg2"), start=True,
                                   stop=True)
                mm.then_inc(gt_in, 1)
                pe.wait_ge(zn_done, i + 1)
                for u in range(U):
                    mm = pe.transpose(z_ps[:, u * T:(u + 1) * T], zn[:, u, :], consts["ident"][:, :])
                mm.then_inc(zt_in, 1)
                pe.wait_ge(zt_out, i + 1)
                pe.wait_ge(nm.r_ready, i + 1)
                for u in range(U):
                    mm = pe.matmul(y[:, u * D:(u + 1) * D], zT[:, u, :], pw("wo"), start=True, stop=True)
                mm.then_inc(nm.y_ready, 1)

        @block.scalar
        def _(act):
            with act.Fori(0, NIT) as i:
                act.wait_ge(rows.free, i + 1)
                act.activation(xT[:, :], xt_ps[:, :], ACT.Copy).then_inc(xt, 1)
                act.wait_ge(g1_in, i + 1)
                act.activation(g1[:, :], g1_ps[0:HD, :], ACT.Copy).then_inc(g1_out, 1)
                act.wait_ge(gt_in, i + 1)
                act.activation(flat(gt), gt_ps[:, :], ACT.Sigmoid).then_inc(gt_out, 1)
                act.wait_ge(zt_in, i + 1)
                act.activation(flat(zT), z_ps[:, :], ACT.Copy).then_inc(zt_out, 1)

        @block.vector
        def _(dve):
            dve.sem_inc(nm.r_ready, 1)
            dve.sem_inc(og_done, 1)
            dve.wait_ge(w_in, 16)
            with dve.Fori(0, NIT) as i:
                dve.wait_ge(gt_out, i + 1)
                dve.wait_ge(ol_in, (i + 1) * 16 * U)
                dve.tensor_tensor(flat(og), flat(ol), flat(gt), ALU.mult).then_inc(og_done, 1)
                dve.wait_ge(og_done, i + 2)
                inner.vector(dve, i, og)
                dve.wait_ge(inner.rstd_ready, i + 1)
                for u in range(U):
                    dve.tensor_scalar(z[:, u, :], og[:, u, :], inner.mv[:, u, 0:1], inner.rstd[:, u:u + 1],
                                      ALU.subtract, ALU.mult).then_inc(z_done, 1)
                dve.wait_ge(z_done, i * U + U)
                dve.tensor_tensor(zn[:, :, :], z[:, :, :], bcast(pw("norm_w"), 1, U), ALU.mult).then_inc(zn_done, 1)
                nm.vector(dve, i)
    ph.close()


def ssm_phase(nc, x, consts, blob, table):
    ph = Phase(nc, "ssm")
    NCH, NS, KC = 2, 16, 4
    NB = P // NS
    NR = NCH * P // NB
    PAD = KC - 1
    w = ph.sb("w", list(blob.shape))
    pw = lambda n: pick(w, table, n)
    xn = ph.sb("xn", [P, U, D])
    xT = ph.sb("xnT", [P, W])
    xp = ph.sb("xp", [P, NCH, U, T + PAD])
    sgate = ph.sb("silu_gate", [P, NCH, W])
    cv = ph.sb("conv", [P, NCH, U, T])
    xc = ph.sb("xc", [P, NCH, W])
    BC = ph.sb("BC", [P, 2, W])
    sig_a = ph.sb("decay", [P, NR])
    UR = 4
    uu, hh, hc = (ph.sb(n, [P, UR, W]) for n in ("u", "h", "hC"))
    yg, yd = ph.sb("y_gated", [P, NCH, W]), ph.sb("y_skip", [P, NCH, W])
    pj = ph.ps("pj", [P, 2, W])
    xr_ps = ph.ps("xr", [P, 2, W])
    ya = ph.ps("ya", [P, NCH, W])
    y = ph.ps("y", [P, W])
    nm = Norm(ph, x, consts, y, x_times=2.0)
    pre = Stats(ph, consts, "pre_")
    (w_in, dec_done, pad_done, xn_done, pj_in, pj_out, cv_done, xc_done, xr_in, u_done, h_done, hc_done,
     ya_in, yd_done, yg_done, row_in) = (ph.sem(n) for n in (
         "w_loaded", "decay_ready", "pads_ready", "xn_ready", "pj_ready", "pj_done", "conv_ready", "xc_ready",
         "xr_ready", "u_ready", "h_ready", "hC_ready", "ya_ready", "skip_ready", "gated_ready", "rows_ready"))
    NJ = 1 + 4 + 2
    flat = lambda a: a.rearrange("p a b -> p (a b)")
    row = lambda i, u: x[:, bass.ds(i * U + u, 1), :].rearrange("p a d -> p (a d)")

    with nc.Block() as block:
        @block.sync
        def _(sp):
            sp.dma_start(w[:, :], blob).then_inc(w_in, 16)

        @block.gpsimd
        def _(pool):
            pool.memset(xp[:, :, :, :], 0.0).then_inc(pad_done, 1)
            pool.wait_ge(pad_done, 1)
            pool.sem_inc(hc_done, UR)

            def weigh(i):
                for r in range(NR):
                    n = i * NR + r
                    pool.wait_ge(h_done, (n + 1 + UR) * U)
                    pool.wait_ge(ya_in, n + 1)
                    pool.tensor_tensor(hc[:, r % UR, :], hh[:, r % UR, :], BC[:, 1, :], ALU.mult).then_inc(hc_done, 1)

            pre.gpsimd(pool, 0)
            with pool.Fori(0, NIT - 1) as i:
                weigh(i)
                nm.gpsimd(pool, i)
                pre.gpsimd(pool, i + 1)
            weigh(NIT - 1)
            nm.gpsimd(pool, NIT - 1)

        @block.tensor
        def _(pe):
            pe.sem_inc(ya_in, UR)
            pe.wait_ge(w_in, 16)
            with pe.Fori(0, NIT) as i:
                pe.wait_ge(xn_done, (i + 1) * U)
                for u in range(U):
                    mm = pe.transpose(pj[:, 0, u * T:(u + 1) * T], xn[:, u, :], consts["ident"][:, :])
                mm.then_inc(pj_in, 1)
                pe.wait_ge(pj_out, i * NJ + 1)
                for j in range(1, 5):
                    if j > 1:
                        pe.wait_ge(pj_out, i * NJ + j - 1)
                    pe.matmul(pj[:, j % 2, :], pw("w_in")[:, (j - 1) * P:j * P], xT[:, :], start=True,
                              stop=True).then_inc(pj_in, 1)
                pe.wait_ge(xc_done, (i + 1) * NCH)
                pe.wait_ge(pj_out, i * NJ + 5)
                for k in range(2):
                    bank = pj[:, (5 + k) % 2, :]
                    for c in range(NCH):
                        mm = pe.matmul(bank, pw("w_bc")[:, (k * NCH + c) * P:(k * NCH + c + 1) * P], xc[:, c, :],
                                       start=(c == 0), stop=(c == NCH - 1))
                    mm.then_inc(pj_in, 1)
                for r in range(NR + 2):
                    if r < NR:
                        c, q = r // NS, r % NS
                        pe.wait_ge(u_done, i * NR + r + 1)
                        pe.matmul(xr_ps[:, r % 2, :], pw("spread")[:, q * P:(q + 1) * P], xc[:, c, :], start=True,
                                  stop=True).then_inc(xr_in, 1)
                    m = r - 2
                    if m >= 0:
                        c, q = m // NS, m % NS
                        pe.wait_ge(hc_done, i * NR + m + 1 + UR)
                        if m == 0:
                            pe.wait_ge(yd_done, i * NCH + NCH)
                        pe.matmul(ya[:, c, :], pw("gather")[:, q * P:(q + 1) * P], hc[:, m % UR, :], start=(q == 0),
                                  stop=(q == NS - 1)).then_inc(ya_in, 1)
                pe.wait_ge(yg_done, (i + 1) * NCH)
                pe.wait_ge(nm.r_ready, i + 1)
                for u in range(U):
                    yu = y[:, u * D:(u + 1) * D]
                    pe.matmul(yu, consts["ones"][0:1, 0:P], pw("b_out"), start=True, stop=False)
                    for c in range(NCH):
                        mm = pe.matmul(yu, yg[:, c, u * T:(u + 1) * T], pw("w_out")[:, c * D:(c + 1) * D],
                                       start=False, stop=(c == NCH - 1))
                mm.then_inc(nm.y_ready, 1)

        @block.scalar
        def _(act):
            act.wait_ge(w_in, 16)
            act.wait_ge(pad_done, 1)
            act.activation(sig_a[:, :], pw("a"), ACT.Sigmoid).then_inc(dec_done, 1)
            with act.Fori(0, NIT) as i:
                act.wait_ge(pj_in, i * NJ + 1)
                act.activation(xT[:, :], pj[:, 0, :], ACT.Identity, scale=pw("ln_g")[:, 0:1],
                               bias=pw("ln_b")[:, 0:1]).then_inc(pj_out, 1)
                for j in range(1, 5):
                    act.wait_ge(pj_in, i * NJ + j + 1)
                    c, b = (j - 1) % 2, pw("b_in")[:, j - 1:j]
                    if j < 3:
                        act.activation(xp[:, c, :, PAD:], pj[:, j % 2, :].rearrange("p (u t) -> p u t", u=U),
                                       ACT.Identity, bias=b).then_inc(pj_out, 1)
                    else:
                        act.activation(sgate[:, c, :], pj[:, j % 2, :], ACT.Silu, bias=b).then_inc(pj_out, 1)
                for c in range(NCH):
                    act.wait_ge(cv_done, (i * NCH + c + 1) * KC)
                    act.activation(xc[:, c, :], flat(cv[:, c, :, :]), ACT.Silu).then_inc(xc_done, 1)
                for k in range(2):
                    act.wait_ge(pj_in, i * NJ + 6 + k)
                    act.activation(BC[:, k, :], pj[:, (5 + k) % 2, :], ACT.Identity, bias=pw("b_bc")[:, k:k + 1]
                                   ).then_inc(pj_out, 1)

        @block.vector
        def _(dve):
            dve.sem_inc(nm.r_ready, 1)
            dve.sem_inc(u_done, 2)
            dve.sem_inc(h_done, UR * U)
            dve.sem_inc(yd_done, NCH)
            dve.wait_ge(w_in, 16)
            dve.wait_ge(dec_done, 1)

            def prenorm(i):
                pre.vector(dve, i, x[:, bass.ds(i * U, U), :])
                dve.wait_ge(pre.rstd_ready, i + 1)
                for u in range(U):
                    dve.tensor_scalar(xn[:, u, :], row(i, u), pre.mv[:, u, 0:1], pre.rstd[:, u:u + 1],
                                      ALU.subtract, ALU.mult).then_inc(xn_done, 1)

            prenorm(0)

            def body(i):
                for c in range(NCH):
                    dve.wait_ge(pj_out, i * NJ + 2 + c)
                    for k in range(KC):
                        taps = xp[:, c, :, k:k + T]
                        wk = pw("conv_w")[:, c * KC + k:c * KC + k + 1]
                        n = (i * NCH + c) * KC + k
                        if k == 0:
                            dve.tensor_scalar(cv[:, c, :, :], taps, wk, pw("conv_b")[:, c:c + 1], ALU.mult,
                                              ALU.add).then_inc(cv_done, 1)
                        else:
                            dve.wait_ge(cv_done, n)
                            dve.scalar_tensor_tensor(cv[:, c, :, :], taps, wk, cv[:, c, :, :], ALU.mult,
                                                     ALU.add).then_inc(cv_done, 1)
                for r in range(NR):
                    n = i * NR + r
                    dve.wait_ge(xr_in, n + 1)
                    if r == 0:
                        dve.wait_ge(pj_out, i * NJ + NJ)
                    dve.wait_ge(h_done, (n + 1) * U)
                    dve.tensor_tensor(uu[:, r % UR, :], xr_ps[:, r % 2, :], BC[:, 0, :], ALU.mult).then_inc(u_done, 1)
                    if r >= 1:
                        scan(i, r - 1)
                scan(i, NR - 1)
                for c in range(NCH):
                    dve.wait_ge(ya_in, i * NR + NS * (c + 1) + UR)
                    dve.scalar_tensor_tensor(yd[:, c, :], xc[:, c, :], pw("d")[:, c:c + 1], ya[:, c, :],
                                             ALU.mult, ALU.add).then_inc(yd_done, 1)
                for c in range(NCH):
                    dve.wait_ge(yd_done, (i + 1) * NCH + c + 1)
                    dve.tensor_tensor(yg[:, c, :], yd[:, c, :], sgate[:, c, :], ALU.mult).then_inc(yg_done, 1)
                nm.vector(dve, i)

            def scan(i, r):
                n = i * NR + r
                dve.wait_ge(u_done, n + 3)
                dve.wait_ge(hc_done, n + 1)
                for u in range(U):
                    dve.tensor_tensor_scan(hh[:, r % UR, u * T:(u + 1) * T],
                                           sig_a[:, r:r + 1].broadcast_to([P, T]),
                                           uu[:, r % UR, u * T:(u + 1) * T], 0.0, ALU.mult, ALU.add
                                           ).then_inc(h_done, 1)

            with dve.Fori(0, NIT - 1) as i:
                body(i)
                prenorm(i + 1)
            body(NIT - 1)
    ph.close()


def wide_moe_phase(nc, x, consts, blob, table):
    ph = Phase(nc, "ff3")
    E, K, EH = 64, 8, 32
    NR = E * EH // P
    NSH = 4
    NCK = NR + NSH
    w = ph.sb("w", list(blob.shape))
    pw = lambda n: pick(w, table, n)
    xT = ph.sb("xT", [P, W])
    big = lambda n: ph.sb(n, [P, U, E])
    pr, gt, eq, cum, le, sel, cw = (big(n) for n in ("probs", "above", "equal", "cumul", "fits", "chosen", "share"))
    m1, sm, rs, cnt, need, s8, rs8 = (ph.sb(n, [P, U]) for n in ("lmax", "lsum", "rlsum", "above_n", "need", "sum8",
                                                                  "rsum8"))
    top = ph.sb("top8", [P, U, 8])
    cwT = ph.sb("shareT", [E, W])
    act_sb = ph.sb("silu", [P, 3, W])
    hid = ph.sb("hidden", [P, NCK, W])
    xt_ps = ph.ps("xT", [P, W])
    h_ps = ph.ps("h", [P, 3, W])
    cb_ps = ph.ps("share", [P, 2, W])
    y = ph.ps("y", [P, W])
    rows = Rows(ph, x)
    nm = Norm(ph, x, consts, y)
    (w_in, xt, lg, st, ex, cw_done, ct_in, ct_out, h_in, a_done, cb_in, hid_done, sh_done) = (ph.sem(n) for n in (
        "w_loaded", "xT_ready", "logits_ready", "router_step", "exp_ready", "share_ready", "shareT_in_psum",
        "shareT_ready", "h_ready", "silu_ready", "share_spread", "hidden_ready", "shared_ready"))
    NSTEP = 18

    with nc.Block() as block:
        @block.sync
        def _(sp):
            sp.dma_start(w[:, :], blob).then_inc(w_in, 16)

        @block.gpsimd
        def _(pool):
            rows.gpsimd(pool, 0, first=True)
            with pool.Fori(0, NIT - 1) as i:
                rows.gpsimd(pool, i + 1)
                nm.gpsimd(pool, i)
            nm.gpsimd(pool, NIT - 1)

        @block.tensor
        def _(pe):
            pe.wait_ge(w_in, 16)
            with pe.Fori(0, NIT) as i:
                rows.tensor(pe, i, xt_ps, consts["ident"][:, :])
                pe.wait_ge(xt, i + 1)
                for u in range(U):
                    o = xt_ps[:, u * E:(u + 1) * E]
                    pe.matmul(o, consts["ones"][0:1, 0:P], pw("router_b"), start=True, stop=False)
                    mm = pe.matmul(o, xT[:, u * T:(u + 1) * T], pw("router"), start=False, stop=True)
                mm.then_inc(lg, 1)

                def hidden(j):
                    pe.wait_ge(a_done, i * NCK + j + 1)
                    pe.matmul(h_ps[:, j % 3, :], pw("w1")[:, j * P:(j + 1) * P], xT[:, :], start=True,
                              stop=True).then_inc(h_in, 1)

                for j in range(NSH):
                    hidden(j)
                pe.wait_ge(cw_done, i + 1)
                hidden(NSH)
                for u in range(U):
                    mm = pe.transpose(xt_ps[0:E, u * T:(u + 1) * T], cw[:, u, :], consts["ident"][:, :])
                mm.then_inc(ct_in, 1)
                pe.wait_ge(ct_out, i + 1)
                for r in range(NR):
                    if r > 0:
                        hidden(NSH + r)
                    pe.wait_ge(hid_done, i * NR + r + 1)
                    pe.matmul(cb_ps[:, r % 2, :], pw("spread")[:, r * P:(r + 1) * P], cwT[:, :], start=True,
                              stop=True).then_inc(cb_in, 1)
                pe.wait_ge(nm.r_ready, i + 1)
                for u in range(U):
                    yu = y[:, u * D:(u + 1) * D]
                    for k in range(2):
                        pe.matmul(yu, consts["ones"][0:1, 0:P], pw(f"sb2_{k}"), start=(k == 0), stop=False)
                    pe.matmul(yu, cwT[:, u * T:(u + 1) * T], pw("b2"), start=False, stop=False)
                    for j in range(NCK):
                        if u == 0 and j >= NSH:
                            pe.wait_ge(hid_done, i * NR + (j - NSH) + 1 + 2)
                        if u == 0 and j == 0:
                            pe.wait_ge(sh_done, (i + 1) * NSH)
                        mm = pe.matmul(yu, hid[:, j, u * T:(u + 1) * T], pw("w2")[:, j * D:(j + 1) * D],
                                       start=False, stop=(j == NCK - 1))
                mm.then_inc(nm.y_ready, 1)

        @block.scalar
        def _(act):
            act.sem_inc(a_done, 3)
            act.wait_ge(w_in, 16)
            with act.Fori(0, NIT) as i:
                act.wait_ge(rows.free, i + 1)
                act.activation(xT[:, :], xt_ps[:, :], ACT.Copy).then_inc(xt, 1)
                act.wait_ge(st, i * NSTEP + 2)
                act.activation(pr[:, :, :], pr[:, :, :], ACT.Exp).then_inc(ex, 1)
                for j in range(NCK):
                    n = i * NCK + j
                    if j == NSH:
                        act.wait_ge(ct_in, i + 1)
                        act.activation(cwT[:, :], xt_ps[0:E, :], ACT.Copy).then_inc(ct_out, 1)
                    act.wait_ge(h_in, n + 1)
                    b = pw("b1")[:, j:j + 1]
                    if j < NSH:
                        act.activation(hid[:, j, :], h_ps[:, j % 3, :], ACT.Silu, bias=b).then_inc(a_done, 1)
                        act.wait_ge(a_done, n + 4)
                        act.sem_inc(sh_done, 1)
                    else:
                        if j >= NSH + 3:
                            act.wait_ge(hid_done, i * NR + (j - NSH) + 1 - 3 + 2)
                        act.activation(act_sb[:, j % 3, :], h_ps[:, j % 3, :], ACT.Silu, bias=b).then_inc(a_done, 1)

        @block.vector
        def _(dve):
            dve.sem_inc(nm.r_ready, 1)
            dve.sem_inc(hid_done, 2)
            dve.wait_ge(w_in, 16)
            with dve.Fori(0, NIT) as i:
                k0 = i * NSTEP
                dve.wait_ge(lg, i + 1)
                l = xt_ps[:, 0:U * E].rearrange("p (u e) -> p u e", u=U)
                step = [0]

                def done(ins, hold=True):
                    ins.then_inc(st, 1)
                    step[0] += 1
                    if hold:
                        dve.wait_ge(st, k0 + step[0])

                done(dve.tensor_reduce(m1[:, :], l, AXX, ALU.max))
                done(dve.tensor_tensor(pr[:, :, :], l, bcast(m1[:, :], 2, E), ALU.subtract), hold=False)
                dve.wait_ge(ex, i + 1)
                done(dve.tensor_reduce(sm[:, :], pr[:, :, :], AXX, ALU.add))
                done(dve.reciprocal(rs[:, :], sm[:, :]))
                done(dve.tensor_tensor(pr[:, :, :], pr[:, :, :], bcast(rs[:, :], 2, E), ALU.mult))
                dve.memset(cnt[:, :], 0.0)
                for u in range(U):
                    ins = dve.max(top[:, u, :], pr[:, u, :])
                done(ins)
                done(dve.tensor_tensor(gt[:, :, :], pr[:, :, :], bcast(top[:, :, 7], 2, E), ALU.is_gt), hold=False)
                done(dve.tensor_tensor(eq[:, :, :], pr[:, :, :], bcast(top[:, :, 7], 2, E), ALU.is_equal))
                done(dve.tensor_reduce(cnt[:, :], gt[:, :, :], AXX, ALU.add), hold=False)
                done(dve.tensor_tensor_scan(flat3(cum), pw("reset"), flat3(eq), 0.0, ALU.mult, ALU.add))
                done(dve.tensor_scalar(need[:, :], cnt[:, :], -1.0, float(K), ALU.mult, ALU.add))
                done(dve.tensor_tensor(le[:, :, :], cum[:, :, :], bcast(need[:, :], 2, E), ALU.is_le))
                done(dve.tensor_tensor(sel[:, :, :], le[:, :, :], eq[:, :, :], ALU.mult))
                done(dve.tensor_tensor(sel[:, :, :], sel[:, :, :], gt[:, :, :], ALU.add), hold=False)
                done(dve.tensor_reduce(s8[:, :], top[:, :, :], AXX, ALU.add))
                done(dve.reciprocal(rs8[:, :], s8[:, :]), hold=False)
                done(dve.tensor_tensor(sel[:, :, :], sel[:, :, :], pr[:, :, :], ALU.mult))
                assert step[0] == NSTEP - 1
                done(dve.tensor_tensor(cw[:, :, :], sel[:, :, :], bcast(rs8[:, :], 2, E), ALU.mult))
                dve.sem_inc(cw_done, 1)
                for r in range(NR):
                    j = NSH + r
                    dve.wait_ge(a_done, i * NCK + j + 4)
                    dve.wait_ge(cb_in, i * NR + r + 1)
                    dve.tensor_tensor(hid[:, j, :], act_sb[:, j % 3, :], cb_ps[:, r % 2, :], ALU.mult
                                      ).then_inc(hid_done, 1)
                nm.vector(dve, i)
    ph.close()


def flat3(a):
    return a[:, :, :].rearrange("p u e -> p (u e)")


def build(nc, t, tables, out, stages):
    ctx = ExitStack()
    with ctx:
        sb = lambda n, s, d=F32: ctx.enter_context(nc.sbuf_tensor(n, s, d))
        x = sb("x", [P, B, D])
        consts = {"ident": sb("ident", [P, P]), "ones": sb("ones", [P, 512]), "neghalf": sb("neghalf", [P, 16])}
        x_in = ctx.enter_context(nc.semaphore("x_loaded"))
        const_ready = ctx.enter_context(nc.semaphore("const_ready"))
        stored = ctx.enter_context(nc.semaphore("stored"))
        consts["ready"] = const_ready
        with nc.Block() as block:
            @block.sync
            def _(sp):
                sp.dma_start(x[:, :, :], t["x"].rearrange("b t d -> t b d")).then_inc(x_in, 16)
                sp.wait_ge(x_in, 16)

            @block.gpsimd
            def _(pool):
                pool.memset(consts["ident"][:, :], 0.0).then_inc(const_ready, 1)
                pool.memset(consts["ones"][:, :], 1.0).then_inc(const_ready, 1)
                pool.memset(consts["neghalf"][:, :], -0.5).then_inc(const_ready, 1)
                pool.wait_ge(const_ready, 3)
                pool.affine_select(out=consts["ident"][:, :], in_=consts["ident"][:, :],
                                   compare_op=ALU.not_equal, fill=1.0, base=0, pattern=[[-1, P]],
                                   channel_multiplier=1).then_inc(const_ready, 1)
                pool.wait_ge(const_ready, 4)
        for s in stages:
            PHASES[s](nc, x, consts, t, tables)
        with nc.Block() as block:
            @block.sync
            def _(sp):
                sp.dma_start(out.rearrange("b t d -> t b d"), x[:, :, :]).then_inc(stored, 16)
                sp.wait_ge(stored, 16)


PHASES = {
    0: lambda nc, x, c, t, tb: heads_phase(nc, x, c, t["sa0"], tb["sa0"]),
    3: lambda nc, x, c, t, tb: delta_phase(nc, x, c, t["sa1"], tb["sa1"],
                                           nc.dram_tensor("records", (B, HQ, T, RW), F32, kind="Internal").ap(),
                                           nc.dram_tensor("recurrence", (B, HQ, T, QW), F32, kind="Internal").ap()),
    9: lambda nc, x, c, t, tb: ssm_phase(nc, x, c, t["ssm"], tb["ssm"]),
    11: lambda nc, x, c, t, tb: wide_moe_phase(nc, x, c, t["ff3"], tb["ff3"]),
    2: lambda nc, x, c, t, tb: moe_phase(nc, "ff0", x, c, t["ff0"], tb["ff0"], F=512, gated=False,
                                         capacity=max(1, int(1.25 * (B * T) / 8 * 2))),
    5: lambda nc, x, c, t, tb: moe_phase(nc, "ff1", x, c, t["ff1"], tb["ff1"], F=448, gated=True),
    1: lambda nc, x, c, t, tb: attention_phase(nc, "xa0", x, c, t, t["xa0"], tb["xa0"], scale=HD ** -0.5, bias="causal"),
    4: lambda nc, x, c, t, tb: attention_phase(nc, "xa1", x, c, t, t["xa1"], tb["xa1"], scale=HD ** -0.5, bias="rows"),
    6: lambda nc, x, c, t, tb: attention_phase(nc, "sa2", x, c, t, t["sa2"], tb["sa2"], scale=0.25, bias="causal",
                                               lut=True),
    7: lambda nc, x, c, t, tb: attention_phase(nc, "xa2", x, c, t, t["xa2"], tb["xa2"], scale=HD ** -0.5),
    10: lambda nc, x, c, t, tb: attention_phase(nc, "xa3", x, c, t, t["xa3"], tb["xa3"], scale=HD ** -0.5,
                                                bias="heads"),
    8: lambda nc, x, c, t, tb: piecewise_phase(nc, x, c, t["pw"], tb["pw"]),
}


STAGES = list(range(12))


def _pack(np, parts):
    table, cols = {}, 0
    for name, a in parts:
        table[name] = (a.shape[0], cols, a.shape[1])
        cols += a.shape[1]
    out = np.zeros((P, cols), np.float32)
    for name, a in parts:
        r, o, c = table[name]
        out[0:r, o:o + c] = a
    return out, table


def _layouts(np, g):
    packs = {}
    W1, b1, W2 = (g("L2_ffn_" + n).reshape(64, 8, 2) for n in ("W1", "b1", "W2"))
    pair = lambda a: np.concatenate([a[:, :, 0], a[:, :, 1]], 0)
    dup = lambda a: np.concatenate([a, a], -1)
    Wout = g("L2_ffn_Wout")
    packs["pw"] = [("Win", dup(g("L2_ffn_Win"))), ("bin", dup(g("L2_ffn_bin_"))[:, None]),
                   ("W1", pair(W1)), ("b1", pair(b1)), ("W2", pair(W2)),
                   ("Wout", Wout), ("Wout2", np.concatenate([Wout, Wout], 0)),
                   ("b2", np.repeat(g("L2_ffn_b2")[:, None], P, 1)),
                   ("bout", g("L2_ffn_bout")[None, :])]

    def own(hf):
        return (np.arange(P)[:, None] // hf == np.arange(P // hf)[None, :]).astype(np.float32)

    def causal(nk):
        return np.where(np.arange(nk)[None, :] <= np.arange(T)[:, None], 0.0, MASKED).astype(np.float32)

    def attn(wq, bq, wk, bk, wv, bv, wo, bo):
        parts = [("wq", wq), ("wk", wk), ("wv", wv), ("wo", wo), ("own", own(HD))]
        if bq is not None:
            parts += [("bq", bq[:, None]), ("bk", bk[:, None])]
        parts += [("bv", np.zeros((1, D), np.float32) if bv is None else bv[None, :])]
        return parts + [("bo", bo[None, :])]

    packs["xa0"] = attn(*(g("L0_xattn_" + n) for n in ("q_w", "q_b", "k_w", "k_b", "v_w", "v_b", "o_w", "o_b")))
    packs["xa0"] += [("causal", causal(S2))]
    L1 = lambda n: g("L1_xattn_" + n)
    packs["xa1"] = attn(L1("Wq").T, L1("bq"), L1("Wk").T, L1("bk"), L1("Wv").T, L1("bv"), L1("Wo").T, L1("bo"))
    kv = g("L2_xattn_Wkv")
    packs["xa2"] = attn(g("L2_xattn_Wq").T, None, kv[:D].T, None, kv[D:].T, None, g("L2_xattn_Wproj").T,
                        g("L2_xattn_bproj"))
    packs["xa3"] = attn(*(g("L3_xattn_" + n) for n in ("Wq", "bq", "Wk", "bk", "Wv", "bv", "Wo", "bo")))
    eye = np.eye(P, dtype=np.float32)
    L2 = lambda n: g("L2_attn_" + n)
    cols = lambda a, b: np.stack([a.reshape(-1), b.reshape(-1)], 1)
    packs["sa2"] = [("wid", cols(L2("w_q"), L2("w_k"))), ("shift", cols(L2("b_q"), L2("b_k"))),
                    ("own", own(2 * HD)),
                    ("wv", L2("v_w").T), ("wo", L2("out_w").T), ("causal", causal(T))]
    for f in range(2):
        for k in range(2):
            sel = np.zeros((P, 8, 2, HD), np.float32)
            sel[:, :, k, :] = eye[:, f * 64:(f + 1) * 64].reshape(P, 8, HD)
            packs["sa2"] += [(f"sel{f}{k}", sel.reshape(P, P))]

    reset = np.tile((np.arange(U * 8) % 8 != 0).astype(np.float32)[None, :], (P, 1))
    upto = np.triu(np.ones((T, T), np.float32))
    packs["ff0"] = [("router", g("L0_ffn_router_w").T), ("reset", reset), ("upto", upto),
                    ("w1", g("L0_ffn_w1").transpose(1, 0, 2).reshape(D, -1)),
                    ("w2", g("L0_ffn_w2").reshape(8, 4, 128, D).transpose(2, 0, 1, 3).reshape(128, -1))]
    packs["ff1"] = [("router", g("L1_ffn_gate_w").T), ("reset", reset),
                    ("w1", g("L1_ffn_w1").transpose(2, 0, 1).reshape(D, -1)),
                    ("w3", g("L1_ffn_w3").transpose(2, 0, 1).reshape(D, -1)),
                    ("w2", g("L1_ffn_w2").transpose(0, 2, 1).reshape(8, 4, 112, D).transpose(2, 0, 1, 3)
                     .reshape(112, -1))]

    A0 = lambda n: g("L0_attn_" + n)
    up = A0("Wup").reshape(32, H, 2, HD).transpose(0, 2, 1, 3).reshape(32, 2 * D)
    bup = A0("bup").reshape(H, 2, HD).transpose(1, 0, 2).reshape(1, 2 * D)
    freq = 1.0 / 10000.0 ** (np.arange(0, HD, 2, dtype=np.float32) / HD)
    angle = np.arange(T, dtype=np.float32)[:, None] * freq[None, :].astype(np.float32)
    cos, sin = np.cos(angle).astype(np.float32), np.sin(angle).astype(np.float32)
    packs["sa0"] = [("wq", A0("Wq")), ("bq", A0("bq")[None, :]), ("wdown", A0("Wdown")), ("bdown", A0("bdown")[:, None]),
                    ("wup", up), ("bup", bup), ("wout", A0("Wout")), ("bout", A0("bout")[None, :]),
                    ("cos", np.concatenate([cos, cos], 1)), ("sin", np.concatenate([-sin, sin], 1))]

    A1 = lambda n: g("L1_attn_" + n)
    packs["sa1"] = [("wproj", np.concatenate([A1(n) for n in ("Wq", "Wk", "Wv", "Wgamma", "Wf")], 1)),
                    ("wg1", A1("Wg1")), ("wg2", A1("Wg2")), ("wo", A1("Wo")),
                    ("norm_w", np.tile(A1("norm_w")[None, :], (P, 1)))]

    A3 = lambda n: g("L3_attn_" + n)
    by_chunk = lambda a: a.reshape(-1, P).T
    wb, wc = (np.tile(A3(n).reshape(2, P, 1, 16), (1, 1, 8, 1)).reshape(2, P, P) for n in ("W_B", "W_C"))
    block = np.arange(16)[:, None, None] * 8 + np.arange(P)[None, None, :] // 16
    spread = (np.arange(P)[None, :, None] == block).astype(np.float32)
    packs["ssm"] = [("ln_g", A3("ln_g")[:, None]), ("ln_b", A3("ln_b")[:, None]), ("w_in", A3("W_in")),
                    ("b_in", by_chunk(A3("b_in"))),
                    ("conv_w", A3("conv_w").reshape(2, P, 4).transpose(1, 0, 2).reshape(P, 8)),
                    ("conv_b", by_chunk(A3("conv_b"))),
                    ("w_bc", np.concatenate([wb[0], wb[1], wc[0], wc[1]], 1)),
                    ("b_bc", np.stack([np.tile(A3("b_B"), 8), np.tile(A3("b_C"), 8)], 1)),
                    ("a", A3("A").reshape(32, P).T), ("d", by_chunk(A3("D"))),
                    ("spread", spread.transpose(1, 0, 2).reshape(P, -1)),
                    ("gather", spread.transpose(2, 0, 1).reshape(P, -1)),
                    ("w_out", A3("W_out").reshape(2, P, D).transpose(1, 0, 2).reshape(P, -1)),
                    ("b_out", A3("b_out")[None, :])]

    F3 = lambda n: g("L3_ffn_" + n)
    w1 = np.concatenate([F3("sw1").transpose(1, 0, 2).reshape(D, 512), F3("w1").transpose(1, 0, 2).reshape(D, 2048)], 1)
    w2 = np.concatenate([F3("sw2").reshape(512, D), F3("w2").reshape(2048, D)], 0)
    b1 = np.concatenate([F3("sb1").reshape(-1), F3("b1").reshape(-1)])
    ex = np.arange(2048)[None, :] // 32 == np.arange(64)[:, None]
    packs["ff3"] = [("router", F3("router_w")), ("router_b", F3("router_b")[None, :]),
                    ("reset", np.tile((np.arange(U * 64) % 64 != 0).astype(np.float32)[None, :], (P, 1))),
                    ("w1", w1), ("b1", by_chunk(b1)), ("w2", w2.reshape(20, P, D).transpose(1, 0, 2).reshape(P, -1)),
                    ("b2", F3("b2")), ("sb2_0", F3("sb2")[0:1]), ("sb2_1", F3("sb2")[1:2]),
                    ("spread", ex.astype(np.float32))]
    return packs


def kernel(**inputs):
    import numpy as np
    import concourse.bacc as bacc
    from concourse.bass_utils import run_bass_kernel_spmd

    nc = bacc.Bacc("TRN2", target_bir_lowering=False, num_devices=1)
    g = lambda n: np.asarray(inputs[n])
    arrays, tables = {}, {}
    for name, parts in _layouts(np, g).items():
        arrays[name], tables[name] = _pack(np, parts)
    arrays["x"] = g("x")
    arrays["ctxT"] = g("ctx_1024").reshape(B * S2, D).T
    arrays["fside"] = g("fside_Bx16xSxS2_0")
    arrays["xa1_mask"] = g("mask_BxSxS2_bf1").view(np.uint8)
    arrays["xa3_mask"] = g("mask_Bx1xSxS2_ik1").reshape(B, T, S2)
    t = {}
    for name, a in arrays.items():
        t[name] = nc.dram_tensor(f"in_{name}", a.shape, mybir.dt.from_np(a.dtype), kind="ExternalInput").ap()
    out = nc.dram_tensor("out_x", (B, T, D), F32, kind="ExternalOutput").ap()
    build(nc, t, tables, out, STAGES)
    feed = {f"in_{n}": np.ascontiguousarray(a) for n, a in arrays.items()}
    r = run_bass_kernel_spmd(nc, [feed], core_ids=[0])
    return r.results[0]["out_x"]
```

```python
from contextlib import ExitStack

import concourse.bass as bass
from concourse import mybir

F32 = mybir.dt.float32
BF16 = mybir.dt.bfloat16
I32 = mybir.dt.int32
U8 = mybir.dt.uint8
ALU = mybir.AluOpType
ACT = mybir.ActivationFunctionType
AXX = mybir.AxisListType.X

P = 128
B = 32
T = 128
D = 128
H = 16
HD = 8
S2 = 120
U = 4
NIT = B // U
W = U * T
CH = 4
EPS = 1e-5
MASKED = -1.0e30


class Phase:

    def __init__(self, nc, name):
        self.nc, self.name, self.ctx, self.sems = nc, name, ExitStack(), []

    def sb(self, name, shape, dt=F32):
        return self.ctx.enter_context(self.nc.sbuf_tensor(f"{self.name}_{name}", shape, dt))

    def ps(self, name, shape, dt=F32):
        return self.ctx.enter_context(self.nc.psum_tensor(f"{self.name}_ps_{name}", shape, dt))

    def sem(self, name):
        s = self.ctx.enter_context(self.nc.semaphore(f"{self.name}_{name}"))
        self.sems.append(s)
        return s

    def close(self):
        for s in self.sems:
            self.nc.sync.sem_clear(s)
        self.nc.all_engine_barrier()
        self.ctx.close()


def bcast(ap, axis, n):
    a = ap.unsqueeze(axis)
    shape = list(a.shape)
    shape[axis] = n
    return a.broadcast_to(shape)


class Rows:

    def __init__(self, ph, x):
        self.x = x
        self.xs = ph.sb("x_rows", [P, U, D])
        self.ready = ph.sem("rows_ready")
        self.free = ph.sem("rows_free")

    def gpsimd(self, pool, i, first=False):
        if not first:
            pool.wait_ge(self.free, i)
        pool.tensor_copy(self.xs[:, :, :], self.x[:, bass.ds(i * U, U), :]).then_inc(self.ready, 1)

    def tensor(self, pe, i, out, ident):
        pe.wait_ge(self.ready, i + 1)
        for u in range(U):
            mm = pe.transpose(out[:, u * T:(u + 1) * T], self.xs[:, u, :], ident)
        mm.then_inc(self.free, 1)


class Stats:

    def __init__(self, ph, consts, tag=""):
        self.c = consts
        self.st = ph.sb(tag + "bnst", [P, U, 6])
        self.mv = ph.sb(tag + "meanvar", [P, U, 2])
        self.ve = ph.sb(tag + "vareps", [P, U])
        self.rstd = ph.sb(tag + "rstd", [P, U])
        self.st_ready = ph.sem(tag + "bnst_ready")
        self.mv_ready = ph.sem(tag + "meanvar_ready")
        self.ve_ready = ph.sem(tag + "vareps_ready")
        self.rstd_ready = ph.sem(tag + "rstd_ready")

    def vector(self, dve, i, r):
        for u in range(U):
            dve.bn_stats(self.st[:, u, :], r[:, u, :]).then_inc(self.st_ready, 1)
        dve.wait_ge(self.st_ready, i * U + U)
        dve.memset(self.ve[:, :], EPS)
        for u in range(U):
            dve.bn_aggr(self.mv[:, u, :], self.st[:, u, :]).then_inc(self.mv_ready, 1)
        dve.wait_ge(self.mv_ready, i * U + U)
        dve.tensor_scalar(self.ve[:, :], self.mv[:, :, 1], EPS, None, ALU.add).then_inc(self.ve_ready, 1)

    def gpsimd(self, pool, i):
        pool.wait_ge(self.ve_ready, i + 1)
        pool.tensor_tensor(self.rstd[:, :], self.ve[:, :], self.c["neghalf"][:, 0:U],
                           ALU.pow).then_inc(self.rstd_ready, 1)


class Norm:

    def __init__(self, ph, x, consts, y, x_times=1.0):
        self.x, self.y, self.x_times = x, y, x_times
        self.r = ph.sb("resid", [P, U, D])
        self.stats = Stats(ph, consts)
        self.y_ready = ph.sem("y_ready")
        self.r_ready = ph.sem("resid_ready")
        self.x_done = ph.sem("x_done")

    def begin(self, dve, i):
        n = self
        dve.wait_ge(n.y_ready, i + 1)
        dve.scalar_tensor_tensor(n.r[:, :, :].rearrange("p u d -> p (u d)"),
                                 n.x[:, bass.ds(i * U, U), :].rearrange("p u d -> p (u d)"), n.x_times,
                                 n.y[:, :], ALU.mult, ALU.add).then_inc(n.r_ready, 1)
        dve.wait_ge(n.r_ready, i + 2)
        n.stats.vector(dve, i, n.r)

    def vector(self, dve, i):
        self.begin(dve, i)
        self.finish(dve, i)

    def finish(self, dve, i):
        n = self
        dve.wait_ge(n.stats.rstd_ready, i + 1)
        for u in range(U):
            dve.tensor_scalar(n.x[:, bass.ds(i * U + u, 1), :].rearrange("p a d -> p (a d)"), n.r[:, u, :],
                              n.stats.mv[:, u, 0:1], n.stats.rstd[:, u:u + 1],
                              ALU.subtract, ALU.mult).then_inc(n.x_done, 1)
        dve.wait_ge(n.x_done, i * U + U)

    def gpsimd(self, pool, i):
        self.stats.gpsimd(pool, i)


class Weights:

    def __init__(self, tile, base, source, loaded):
        self.tile, self.base, self.source, self.loaded = tile, base, source, loaded
        self.next = None

    def load(self, sp):
        n = self.source.shape[1]
        sp.dma_start(self.tile[:, self.base:self.base + n], self.source).then_inc(self.loaded, 16)

    def load_next(self, sp):
        if self.next:
            self.next.load(sp)


def pick(w, table, name):
    rows, off, cols = table[name]
    return w.tile[0:rows, w.base + off:w.base + off + cols]


def piecewise_phase(nc, x, consts, weights, table):
    ph = Phase(nc, "pw")
    NJ = 8
    w, w_in = weights, weights.loaded
    xT = ph.sb("xT", [P, W])
    s = ph.sb("s", [P, W])
    h = ph.sb("h", [P, NJ, W])
    wc = ph.sb("wc", [P, NJ, D])
    pj = ph.ps("pj", [P, 2, W])
    y = ph.ps("y", [P, W])
    nm = Norm(ph, x, consts, y)
    rows = Rows(ph, x)
    xt, s_ps, s_sb, h_sb, wc_sb = (ph.sem(n) for n in (
        "xT_ready", "s_in_psum", "s_ready", "h_ready", "outweights_ready"))
    Win, bin_ = pick(w, table, "Win"), pick(w, table, "bin")
    W1, b1, W2 = pick(w, table, "W1"), pick(w, table, "b1"), pick(w, table, "W2")
    Wout, b2, bout = pick(w, table, "Wout"), pick(w, table, "b2"), pick(w, table, "bout")

    with nc.Block() as block:
        @block.sync
        def _(sp):
            weights.load_next(sp)

        @block.gpsimd
        def _(pool):
            rows.gpsimd(pool, 0, first=True)
            with pool.Fori(0, NIT - 1) as i:
                rows.gpsimd(pool, i + 1)
                nm.gpsimd(pool, i)
            nm.gpsimd(pool, NIT - 1)

        @block.tensor
        def _(pe):
            pe.wait_ge(w_in, 16)
            with pe.Fori(0, NIT) as i:
                rows.tensor(pe, i, pj[:, 0, :], consts["ident"][:, :])
                pe.wait_ge(xt, i + 1)
                pe.matmul(pj[:, 1, :], Win, xT[:, :], start=True, stop=True).then_inc(s_ps, 1)
                pe.wait_ge(nm.r_ready, i + 1)
                pe.wait_ge(wc_sb, NJ + 1)
                for u in range(U):
                    yu = y[:, u * D:(u + 1) * D]
                    pe.matmul(yu, consts["ones"][0:1, 0:P], bout, start=True, stop=False)
                    pe.matmul(yu, b2, Wout, start=False, stop=False)
                    for j in range(NJ):
                        if u == 0:
                            pe.wait_ge(h_sb, i * NJ + j + 1)
                        mm = pe.matmul(yu, h[:, j, u * T:(u + 1) * T], wc[:, j, :],
                                       start=False, stop=(j == NJ - 1))
                mm.then_inc(nm.y_ready, 1)

        @block.scalar
        def _(act):
            act.wait_ge(w_in, 16)
            with act.Fori(0, NIT) as i:
                act.wait_ge(rows.free, i + 1)
                act.activation(xT[:, :], pj[:, 0, :], ACT.Copy).then_inc(xt, 1)
                act.wait_ge(s_ps, i + 1)
                act.activation(s[:, :], pj[:, 1, :], ACT.Identity, bias=bin_).then_inc(s_sb, 1)
                act.wait_ge(s_sb, i + 1)
                for j in range(NJ):
                    act.activation(h[:, j, :], s[:, :], ACT.Relu, scale=W1[:, j:j + 1],
                                   bias=b1[:, j:j + 1]).then_inc(h_sb, 1)

        @block.vector
        def _(dve):
            dve.sem_inc(nm.r_ready, 1)
            dve.wait_ge(w_in, 16)
            for j in range(NJ):
                dve.tensor_scalar(wc[:, j, :], pick(w, table, "Wout2"), W2[:, j:j + 1], None,
                                  ALU.mult).then_inc(wc_sb, 1)
            dve.sem_inc(wc_sb, 1)
            with dve.Fori(0, NIT) as i:
                nm.vector(dve, i)
    ph.close()


def attention_phase(nc, name, x, consts, t, weights, table, *, scale, bias=None, lut=False):
    ph = Phase(nc, name)
    NK = T if lut else S2
    KW = U * NK
    HF = 2 * HD if lut else HD
    NF = H * HF // P
    HT = H // NF
    G4 = 4
    NU = U * G4
    NS, TR = 2, 8
    w, w_in = weights, weights.loaded
    xT = ph.sb("xT", [P, W])
    q = ph.sb("q", [P, NF, W])
    kT = ph.sb("kT", [P, NF, KW])
    kS = ph.sb("kspread", [P, U, H, NK])
    VP = 32 + HD
    V = ph.sb("v", [NK, U * G4, G4 * VP])
    E = ph.sb("exps", [P, TR, G4 * NK])
    mx = ph.sb("negmax", [P, TR, G4])
    ET = ph.sb("expsT", [NK, TR, G4, T])
    den = ph.sb("sums", [P, U, H])
    rd = ph.sb("rsum", [P, U, H])
    rb = ph.sb("rsums", [P, H, HD])
    rT = ph.sb("rsumsT", [P, 2, T])
    oT = ph.sb("oT", [P, U, T])
    s_ps = ph.ps("s", [P, NS, 512])
    t_ps = ph.ps("t", [P, 2, G4, T])
    o_ps = ph.ps("o", [P, 2, 512])
    y = ph.ps("y", [P, W])
    pj = ph.ps("pj", [P, 512])
    rows = Rows(ph, x)
    nm = Norm(ph, x, consts, y)
    ident = consts["ident"][:, :]
    (zeroed, pj_ready, pj_done, k_spread, s_ready, b_ready, m_ready, e_ready, sum_ready, t_ready,
     et_ready, pv_ready, rd_ready, rb_ready, o_ready, rt_ready, on_ready) = (ph.sem(n) for n in (
         "zeroed", "pj_ready", "pj_done", "keys_spread", "s_ready", "biased_ready", "max_ready",
         "exp_ready", "sum_ready", "t_ready", "expT_ready", "pv_ready", "rsum_single", "rsum_ready", "o_ready",
         "rsumT_ready", "oT_ready"))
    s_done = b_ready if bias else e_ready
    S0 = 4
    E0 = 0 if bias else S0
    pw = lambda n: pick(w, table, n)
    if not lut:
        ctx = ph.sb("ctx", [P, KW])
        ctx_in = ph.sem("ctx_loaded")
    masks = bias in ("rows", "heads")
    if masks:
        m_raw = ph.sb("mask_raw", [P, U, NK], t[name + "_mask"].dtype)
        m_bias = ph.sb("mask_bias", [P, U, NK])
        m_in, mb_ready = ph.sem("mask_loaded"), ph.sem("maskbias_ready")
    if bias == "heads":
        FR = 4
        fb = ph.sb("headbias", [P, FR, G4, NK])
        fb_in = [ph.sem(f"headbias_loaded{r}") for r in range(FR)]
        fb_sum = ph.sem("headbias_masked")
    if lut:
        TWO_PI_INV = 512.0 / 6.283185307179586
        ANG = 6.283185307179586 / 512.0
        MAGIC = 12582912.0
        ang = ph.sb("angle", [P, 2, W])
        kk = ph.sb("index", [P, 2, 2, W])
        rr = ph.sb("turns", [P, 2, 2, W])
        sc = ph.sb("cossin", [P, 2, 2, W])
        (a_ready, k_ready, r1_ready, r2_ready, i_ready, cs_ready, den_ready) = (ph.sem(n) for n in (
            "angle_ready", "index_ready", "turns_raw", "turns_ready", "wrapped_ready", "cossin_ready", "rwidth_ready"))
        rw = ph.sb("rwidth", [P, 2])

    J0 = 1 + 2 * NF
    NJ = J0 + 1
    V_AT, X_AT, K_AT, Q_AT = 5, 6, (13 if lut else 8), NU - 1
    ANG_AT, ANG_STEPS = 7, 6
    SIN_AT = 12
    SPREAD_AT = (12, 13, 14, 15) if lut else (9, 11, 13, 15)
    MASK_AT = (8, 9, 11, 15)
    CTX_AT = 7
    SUM_LAG, T_LAG, PV_LAG, R_LAG, MUL_LAG, Y_LAG = 3, 4, 6, 7, 8, 10
    NORM_AT = 11
    TAIL = NORM_AT + 2

    def unit(n, lag, first, tail):
        m = n - lag
        return None if (m < 0 and first) or (m >= 0 and tail) else m

    def job(i, k):
        return J0 + i * NJ + k

    with nc.Block() as block:
        @block.sync
        def _(sp):
            def load_ctx(i):
                if not lut:
                    sp.dma_start(ctx[:, :], t["ctxT"][:, bass.ds(i * KW, KW)]).then_inc(ctx_in, 16)

            def load_mask(i):
                if masks:
                    src = t[name + "_mask"][bass.ds(i * U, U)].rearrange("u q k -> q u k")
                    sp.dma_start(m_raw[:, :, :], src).then_inc(m_in, 16)

            def load_bias(i, n):
                if bias == "heads":
                    sp.wait_ge(b_ready, i * NU + n - FR + 1 + S0)
                    sp.dma_start(fb[:, n % FR, :, :],
                                 t["fside"][bass.ds(i * U + n // 4, 1), G4 * (n % 4):G4 * (n % 4) + G4]
                                 .rearrange("a h q k -> q (a h) k")).then_inc(fb_in[n % FR], 16)

            def trip(k, last=False):
                for n in range(NU):
                    load_bias(k - 1, n)
                    if n == CTX_AT and not last:
                        if not lut:
                            sp.wait_ge(pj_done, job(k - 1, 0) + 1)
                        load_ctx(k)
                        load_mask(k)

            weights.load_next(sp)
            load_ctx(0)
            load_mask(0)
            with sp.Fori(1, NIT) as k:
                trip(k)
            trip(NIT, last=True)

        @block.gpsimd
        def _(pool):
            def masked_bias(i, n):
                if bias == "heads":
                    pool.wait_ge(mb_ready, i * U + n // 4 + 1)
                    pool.wait_ge(fb_in[n % FR], (i * (NU // FR) + n // FR + 1) * 16)
                    pool.tensor_tensor(fb[:, n % FR, :, :], fb[:, n % FR, :, :],
                                       bcast(m_bias[:, n // 4, :], 1, G4), ALU.add).then_inc(fb_sum, 1)

            def spread(i, u, first=False):
                pool.wait_ge(pj_done, job(i - 1, 2 + NF))
                if not first:
                    pool.wait_ge(s_ready, (i - 1) * NU + 4 * u + 4)
                for f in range(NF):
                    kp = pool.tensor_tensor(kS[:, u, f * HT:(f + 1) * HT, :],
                                            bcast(kT[:, f, u * NK:(u + 1) * NK], 1, HT),
                                            bcast(pw("own"), 2, NK), ALU.mult)
                kp.then_inc(k_spread, 1)

            def trip(i, first=False, last=False, tail=False):
                for n in range(TAIL if tail else NU):
                    if n == 0 and not (last or tail):
                        rows.gpsimd(pool, i + 1)
                    if not tail and not (last and n + 2 >= NU):
                        masked_bias(i + (n + 2) // NU, (n + 2) % NU)
                    if n == NORM_AT and not first:
                        nm.gpsimd(pool, i - 1)
                    if n in SPREAD_AT and not (last or tail):
                        spread(i + 1, SPREAD_AT.index(n))

            pool.memset(V[:, :, :], 0.0).then_inc(zeroed, 1)
            rows.gpsimd(pool, 0, first=True)
            for n in range(2):
                masked_bias(0, n)
            pool.wait_ge(w_in, 16)
            for u in range(U):
                spread(0, u, first=True)
            trip(0, first=True)
            with pool.Fori(1, NIT - 1) as i:
                trip(i)
            trip(NIT - 1, last=True)
            trip(NIT, tail=True)

        @block.tensor
        def _(pe):
            def bank(i, k):
                n = job(i, k)
                if not (isinstance(n, int) and n == 0):
                    pe.wait_ge(pj_done, n)
                return pj

            def transpose_x(i):
                rows.tensor(pe, i, bank(i - 1, 1), ident)

            def project(i, a):
                if a == 1 and not lut:
                    pe.wait_ge(ctx_in, (i + 1) * 16)
                if lut:
                    pe.wait_ge(cs_ready, (i + 1) * 2)
                for f in range(NF):
                    out = bank(i - 1, 2 + (1 - a) * NF + f)
                    if lut:
                        for k in range(2):
                            mm = pe.matmul(out[:, :], pw(f"sel{f}{k}"), sc[:, a, k, :], start=(k == 0), stop=(k == 1))
                    elif a == 0:
                        mm = pe.matmul(out[:, :], pw("wq"), xT[:, :], start=True, stop=True)
                    else:
                        mm = pe.matmul(out[:, 0:KW], pw("wk"), ctx[:, :], start=True, stop=True)
                    mm.then_inc(pj_ready, 1)

            def project_values(i):
                out = bank(i, 0)
                for u in range(U):
                    src = xT[:, u * T:(u + 1) * T] if lut else ctx[:, u * NK:(u + 1) * NK]
                    vu = out[0:NK, u * D:(u + 1) * D]
                    if not lut:
                        pe.matmul(vu, consts["ones"][0:1, 0:NK], pw("bv"), start=True, stop=False)
                    mm = pe.matmul(vu, src, pw("wv"), start=lut, stop=True)
                mm.then_inc(pj_ready, 1)

            def trip(i, first=False, last=False, tail=False):
                for n in range(TAIL if tail else NU):
                    if not tail:
                        u, g = n // 4, n % 4
                        if n == 0:
                            pe.wait_ge(pj_done, job(i, 0))
                        if g == 0:
                            pe.wait_ge(k_spread, i * U + u + 1)
                        pe.wait_ge(s_done, i * NU + n - NS + 1 + S0)
                        pe.matmul(s_ps[:, n % NS, 0:G4 * NK], q[:, g * G4 // HT, u * T:(u + 1) * T],
                                  kS[:, u, g * G4:(g + 1) * G4, :].rearrange("p h k -> p (h k)"),
                                  start=True, stop=True).then_inc(s_ready, 1)
                    if n == Q_AT and not (last or tail):
                        project(i + 1, 0)
                    m = unit(n, T_LAG, first, tail)
                    if m is not None:
                        pe.wait_ge(e_ready, i * NU + m + 1 + E0)
                        pe.wait_ge(et_ready, i * NU + m + 1)
                        for j in range(G4):
                            mm = pe.transpose(t_ps[0:NK, m % 2, j, :], E[:, m % TR, j * NK:(j + 1) * NK], ident)
                        mm.then_inc(t_ready, 1)
                    m = unit(n, PV_LAG, first, tail)
                    if m is not None:
                        u, g = m % NU // 4, m % 4
                        pe.wait_ge(et_ready, i * NU + m + 3)
                        if m == 0:
                            pe.wait_ge(pj_done, job(i, 1))
                        if g == 0:
                            pe.wait_ge(on_ready, i * U + m // 4 + 1)
                        for j in range(G4):
                            mm = pe.matmul(o_ps[32 * g:32 * g + 32, u % 2, 0:T], V[:, u * G4 + g, 32 * j:32 * j + 32],
                                           ET[:, m % TR, j, :], start=(j == 0), stop=(j == G4 - 1))
                        mm.then_inc(pv_ready, 1)
                    if n == V_AT and not tail:
                        project_values(i)
                    m = unit(n, R_LAG, first, tail)
                    if m is not None and m % 4 == 3:
                        u = m % NU // 4
                        pe.wait_ge(rb_ready, i * U + m // 4 + 1 + U)
                        pe.transpose(o_ps[:, u % 2, T:2 * T], rb[:, :, :].rearrange("p h e -> p (h e)"), ident
                                     ).then_inc(o_ready, 1)
                    m = unit(n, Y_LAG, first, tail)
                    if m is not None and m % 4 == 3:
                        u = m % NU // 4
                        pe.wait_ge(on_ready, i * U + m // 4 + 1 + 2)
                        if u == 0:
                            pe.wait_ge(nm.r_ready, i + 1)
                        yu = y[:, u * D:(u + 1) * D]
                        if "bo" in table:
                            pe.matmul(yu, consts["ones"][0:1, 0:P], pw("bo"), start=True, stop=False)
                        mm = pe.matmul(yu, oT[:, u, :], pw("wo"), start="bo" not in table, stop=True)
                        if u == U - 1:
                            mm.then_inc(nm.y_ready, 1)
                    if n == X_AT and not (last or tail):
                        transpose_x(i + 1)
                    if n == K_AT and not (last or tail):
                        project(i + 1, 1)

            pe.sem_inc(t_ready, TR)
            pe.wait_ge(w_in, 16)
            transpose_x(0)
            project(0, 1)
            project(0, 0)
            pe.wait_ge(zeroed, 1)
            trip(0, first=True)
            with pe.Fori(1, NIT - 1) as i:
                trip(i)
            trip(NIT - 1, last=True)
            trip(NIT, tail=True)

        @block.scalar
        def _(act):
            def copy_x(i):
                act.wait_ge(rows.free, i + 1)
                act.activation(xT[:, :], pj[:, :], ACT.Copy).then_inc(pj_done, 1)

            def cos_sin(i):
                for a in range(2):
                    act.wait_ge(i_ready, i * 2 + a + 1)
                    act.activation(sc[:, a, :, :], kk[:, a, :, :], ACT.Sin, scale=ANG).then_inc(cs_ready, 1)

            def copy_features(i, a):
                for f in range(NF):
                    act.wait_ge(pj_ready, i * (NJ - 1) + (1 - a) * NF + f + 1)
                    dst, src = (q[:, f, :], pj[:, :]) if a == 0 else (kT[:, f, :], pj[:, 0:KW])
                    b = "bk" if a else "bq"
                    if b in table:
                        act.activation(dst, src, ACT.Identity, bias=pw(b)).then_inc(pj_done, 1)
                    elif a == 0:
                        act.activation(dst, src, ACT.Copy, scale=scale if not bias else 1.0).then_inc(pj_done, 1)
                    else:
                        act.activation(dst, src, ACT.Copy).then_inc(pj_done, 1)

            def trip(i, first=False, last=False, tail=False):
                for n in range(TAIL if tail else NU):
                    if not tail:
                        src = E[:, n % TR, :] if bias else s_ps[:, n % NS, 0:G4 * NK]
                        act.wait_ge(m_ready, i * NU + n + 1)
                        if not bias:
                            act.wait_ge(sum_ready, i * NU + n + 1)
                        for j in range(G4):
                            cut = slice(j * NK, (j + 1) * NK)
                            ex = act.activation(E[:, n % TR, cut], src[:, cut], ACT.Exp, bias=mx[:, n % TR, j:j + 1])
                        ex.then_inc(e_ready, 1)
                    if n == Q_AT and not (last or tail):
                        act.wait_ge(s_ready, (i + 1) * NU)
                        copy_features(i + 1, 0)
                    m = unit(n, T_LAG, first, tail)
                    if m is not None:
                        act.wait_ge(t_ready, i * NU + m + 1 + TR)
                        if not (first and m < TR):
                            act.wait_ge(pv_ready, i * NU + m - TR + 1)
                        act.activation(ET[:, m % TR, :, :], t_ps[0:NK, m % 2, :, :], ACT.Copy
                                       ).then_inc(et_ready, 1)
                    if n == V_AT and not tail:
                        act.wait_ge(pj_ready, J0 - 1 + i * (NJ - 1) + 1)
                        if not first:
                            act.wait_ge(pv_ready, i * NU)
                        act.activation(V[:, :, :].rearrange("k n (j e) -> k n j e", e=VP)[:, :, :, 0:HD],
                                       pj[0:NK, :].rearrange("k (n j e) -> k n j e", j=G4, e=HD),
                                       ACT.Copy).then_inc(pj_done, 1)
                    m = unit(n, R_LAG, first, tail)
                    if m is not None and m % 4 == 3:
                        u = m % NU // 4
                        act.wait_ge(o_ready, i * U + m // 4 + 1)
                        act.wait_ge(on_ready, i * U + m // 4 + 1)
                        act.activation(rT[:, u % 2, :], o_ps[:, u % 2, T:2 * T], ACT.Copy).then_inc(rt_ready, 1)
                    if n == X_AT and not (last or tail):
                        copy_x(i + 1)
                    if lut and n == SIN_AT and not (last or tail):
                        cos_sin(i + 1)
                    if n == K_AT and not (last or tail):
                        act.wait_ge(k_spread, (i + 1) * U)
                        copy_features(i + 1, 1)

            act.sem_inc(et_ready, 2)
            act.wait_ge(w_in, 16)
            act.wait_ge(zeroed, 1)
            copy_x(0)
            if lut:
                cos_sin(0)
            copy_features(0, 1)
            copy_features(0, 0)
            trip(0, first=True)
            with act.Fori(1, NIT - 1) as i:
                trip(i)
            trip(NIT - 1, last=True)
            trip(NIT, tail=True)

        @block.vector
        def _(dve):
            def angle_steps(i, k):
                for a in range(2):
                    if k == 0:
                        dve.tensor_scalar(ang[:, a, :], xT[:, :], rw[:, a:a + 1], pw("shift")[:, a:a + 1],
                                          ALU.mult, ALU.add).then_inc(a_ready, 1)
                    if k == 1:
                        dve.wait_ge(a_ready, i * 2 + a + 1)
                        for f in range(2):
                            dve.tensor_scalar(rr[:, a, f, :], ang[:, a, :], TWO_PI_INV, MAGIC, ALU.mult,
                                              ALU.add).then_inc(k_ready, 1)
                    if k == 2:
                        dve.wait_ge(k_ready, i * 4 + 2 * a + 2)
                        for f in range(2):
                            dve.tensor_scalar(kk[:, a, f, :], rr[:, a, f, :], -MAGIC, 128.0 * (1 - f), ALU.add,
                                              ALU.add).then_inc(r1_ready, 1)
                    if k == 3:
                        dve.wait_ge(r1_ready, i * 4 + 2 * a + 2)
                        dve.tensor_scalar(rr[:, a, :, :], kk[:, a, :, :], 1.0 / 512, MAGIC, ALU.mult,
                                          ALU.add).then_inc(r2_ready, 1)
                    if k == 4:
                        dve.wait_ge(r2_ready, i * 4 + a + 1)
                        dve.tensor_scalar(rr[:, a, :, :], rr[:, a, :, :], -MAGIC, -512.0, ALU.add,
                                          ALU.mult).then_inc(r2_ready, 1)
                    if k == 5:
                        dve.wait_ge(r2_ready, i * 4 + 2 + a + 1)
                        dve.tensor_tensor(kk[:, a, :, :], kk[:, a, :, :], rr[:, a, :, :],
                                          ALU.add).then_inc(i_ready, 1)

            def mask_bias(i, u):
                dve.wait_ge(m_in, i * 16 + 16)
                dve.tensor_scalar(m_bias[:, u, :], m_raw[:, u, :], 0.0, MASKED, ALU.is_equal,
                                  ALU.mult).then_inc(mb_ready, 1)

            def trip(i, first=False, last=False, tail=False):
                for n in range(TAIL if tail else NU):
                    if not tail:
                        u, g = n // 4, n % 4
                        src = s_ps[:, n % NS, 0:G4 * NK]
                        heads = lambda a: a.rearrange("p (h k) -> p h k", h=G4)
                        dve.wait_ge(s_ready, i * NU + n + 1)
                        dve.wait_ge(t_ready, i * NU + n + 1)
                        if bias:
                            dve.wait_ge(sum_ready, i * NU + n + 1)
                            if bias == "causal":
                                add = bcast(pw("causal"), 1, G4)
                            elif bias == "rows":
                                if g == 0:
                                    dve.wait_ge(mb_ready, i * U + u + 1)
                                add = bcast(m_bias[:, u, :], 1, G4)
                            else:
                                dve.wait_ge(fb_sum, i * NU + n + 1)
                                add = fb[:, n % FR, :, :]
                            dve.scalar_tensor_tensor(heads(E[:, n % TR, :]), heads(src), scale, add, ALU.mult,
                                                     ALU.add).then_inc(b_ready, 1)
                            dve.wait_ge(b_ready, i * NU + n + 1 + S0)
                            src = E[:, n % TR, :]
                        dve.tensor_reduce(mx[:, n % TR, :], heads(src), AXX, ALU.max, negate=True).then_inc(m_ready, 1)
                        if masks and n in MASK_AT and not last:
                            mask_bias(i + 1, MASK_AT.index(n))
                    m = unit(n, SUM_LAG, first, tail)
                    if m is not None:
                        u, g = m % NU // 4, m % 4
                        if g == 0:
                            dve.wait_ge(rb_ready, i * U + m // 4 + 1)
                        dve.wait_ge(e_ready, i * NU + m + 1 + E0)
                        dve.tensor_reduce(den[:, u, g * G4:(g + 1) * G4],
                                          E[:, m % TR, :].rearrange("p (h k) -> p h k", h=G4), AXX, ALU.add
                                          ).then_inc(sum_ready, 1)
                        if g == 3:
                            dve.wait_ge(sum_ready, i * NU + m + 1 + TR)
                            if not (first and u == 0):
                                dve.wait_ge(o_ready, i * U + m // 4)
                            dve.reciprocal(rd[:, u, :], den[:, u, :]).then_inc(rd_ready, 1)
                            dve.wait_ge(rd_ready, i * U + m // 4 + 1)
                            dve.tensor_copy(rb[:, :, :], bcast(rd[:, u, :], 2, HD)).then_inc(rb_ready, 1)
                    m = unit(n, MUL_LAG, first, tail)
                    if m is not None and m % 4 == 3:
                        u = m % NU // 4
                        dve.wait_ge(rt_ready, i * U + m // 4 + 1)
                        dve.tensor_tensor(oT[:, u, :], o_ps[:, u % 2, 0:T], rT[:, u % 2, :], ALU.mult
                                          ).then_inc(on_ready, 1)
                    if n == NORM_AT and not first:
                        nm.begin(dve, i - 1)
                    if n == NORM_AT + 1 and not first:
                        nm.finish(dve, i - 1)
                    if lut and 0 <= n - ANG_AT < ANG_STEPS and not (last or tail):
                        if n == ANG_AT:
                            dve.wait_ge(pj_done, job(i, 2))
                        angle_steps(i + 1, n - ANG_AT)

            dve.sem_inc(nm.r_ready, 1)
            dve.sem_inc(sum_ready, TR)
            dve.sem_inc(on_ready, 2)
            dve.sem_inc(rb_ready, U)
            dve.sem_inc(s_done, S0)
            dve.wait_ge(w_in, 16)
            if masks:
                for u in range(U):
                    mask_bias(0, u)
            if lut:
                dve.tensor_scalar(rw[:, :], pw("wid"), -1.0, None, ALU.mult).then_inc(den_ready, 1)
                dve.wait_ge(den_ready, 1)
                dve.tensor_tensor(rw[:, :], rw[:, :], pw("wid"), ALU.max).then_inc(den_ready, 1)
                dve.wait_ge(den_ready, 2)
                dve.tensor_scalar(rw[:, :], rw[:, :], 1.0, None, ALU.add).then_inc(den_ready, 1)
                dve.wait_ge(den_ready, 3)
                dve.reciprocal(rw[:, :], rw[:, :]).then_inc(den_ready, 1)
                dve.wait_ge(den_ready, 4)
                dve.wait_ge(pj_done, 1)
                for k in range(6):
                    angle_steps(0, k)
            trip(0, first=True)
            with dve.Fori(1, NIT - 1) as i:
                trip(i)
            trip(NIT - 1, last=True)
            trip(NIT, tail=True)
    ph.close()


def top_one(dve, ready, base, pr, best, eq, cum, reset, onehot):
    E = pr.shape[2]
    dve.tensor_reduce(best, pr, AXX, ALU.max).then_inc(ready, 1)
    dve.wait_ge(ready, base + 1)
    dve.tensor_tensor(eq, pr, bcast(best, 2, E), ALU.is_equal).then_inc(ready, 1)
    dve.wait_ge(ready, base + 2)
    dve.tensor_tensor_scan(cum.rearrange("p u e -> p (u e)"), reset, eq.rearrange("p u e -> p (u e)"), 0.0,
                           ALU.mult, ALU.add).then_inc(ready, 1)
    dve.wait_ge(ready, base + 3)
    dve.scalar_tensor_tensor(onehot, cum, 1.0, eq, ALU.is_equal, ALU.mult).then_inc(ready, 1)
    dve.wait_ge(ready, base + 4)


def moe_phase(nc, name, x, consts, weights, table, *, F, gated, capacity=None):
    ph = Phase(nc, name)
    E, FC = 8, 4
    FW = F // FC
    HR = 4
    w, w_in = weights, weights.loaded
    xT = ph.sb("xT", [P, W])
    G = ph.sb("hidden", [FW, 2, FC, W])
    small = lambda n, shape=(P, U, E): ph.sb(n, list(shape))
    pr, p2, eq, cum, cw = (small(n) for n in ("probs", "rest", "equal", "cumul", "share"))
    oh, kept, part = (small(n, (P, U, 2, E)) for n in ("onehot", "kept", "gated"))
    v = small("best", (P, U, 2))
    gate = small("gate", (P, U, 2))
    m1, sm, rs, ss, rss = (small(n, (P, U)) for n in ("lmax", "lsum", "rlsum", "vsum", "rvsum"))
    run = small("run", (P, 2, E))
    misc = ph.ps("misc", [P, 512])
    rt = ph.ps("router", [P, 512])
    h_ps = ph.ps("h", [P, HR, W])
    ye = ph.ps("ye", [P, 2, W])
    rows = Rows(ph, x)
    nm = Norm(ph, x, consts, None)
    (xt, lg_ready, rstep, ex_ready, oh_ready, pos_ready, run_ready, h_ready, act_ready, g_ready, ye_ready,
     acc_ready, cw_ready) = (ph.sem(n) for n in (
         "xT_ready", "logits_ready", "router_step", "exp_ready", "onehot_ready", "pos_ready", "run_ready",
         "h_ready", "act_ready", "hidden_ready", "ye_ready", "acc_ready", "share_ready"))
    pw = lambda n: pick(w, table, n)
    RS = 19
    NH = 2 if gated else 1
    NHE = E * FC * NH
    cw2 = ph.sem("weights_ready")
    if gated:
        a_sb = ph.sb("silu", [FW, 2, W])

    def w1(e, f, k):
        o = (e * FC + f) * FW
        return pw("w1" if k == 0 else "w3")[:, o:o + FW]

    with nc.Block() as block:
        @block.sync
        def _(sp):
            weights.load_next(sp)

        @block.gpsimd
        def _(pool):
            rows.gpsimd(pool, 0, first=True)
            with pool.Fori(0, NIT - 1) as i:
                rows.gpsimd(pool, i + 1)
                nm.gpsimd(pool, i)
            nm.gpsimd(pool, NIT - 1)

        @block.tensor
        def _(pe):
            def trip(i, last=False):
                pe.wait_ge(xt, i + 1)
                for u in range(U):
                    mm = pe.matmul(rt[:, u * E:(u + 1) * E], xT[:, u * T:(u + 1) * T], pw("router"), start=True,
                                   stop=True)
                mm.then_inc(lg_ready, 1)

                def hidden(e):
                    for f in range(FC):
                        for k in range(NH):
                            n = (e * FC + f) * NH + k
                            if gated:
                                pe.wait_ge(g_ready, i * E * FC + (e * FC + f) + 1)
                            else:
                                pe.wait_ge(g_ready, i * NHE + n + 1)
                            pe.matmul(h_ps[0:FW, n % HR, :], w1(e, f, k), xT[:, :], start=True,
                                      stop=True).then_inc(h_ready, 1)

                def down(e):
                    pe.wait_ge(acc_ready, i * E + e + 1)
                    for u in range(U):
                        for f in range(FC):
                            if u == 0:
                                pe.wait_ge(g_ready, i * E * FC + e * FC + f + 1 + HR // NH)
                            mm = pe.matmul(ye[:, e % 2, u * D:(u + 1) * D], G[:, e % 2, f, u * T:(u + 1) * T],
                                           pw("w2")[0:FW, (e * FC + f) * D:(e * FC + f + 1) * D],
                                           start=(f == 0), stop=(f == FC - 1))
                    mm.then_inc(ye_ready, 1)

                hidden(0)
                for e in range(1, E):
                    hidden(e)
                    down(e - 1)
                    if capacity and e == 1:
                        pe.wait_ge(oh_ready, i + 1)
                        pe.wait_ge(run_ready, i * U + 1)
                        for u in range(U):
                            out = rt[:, 64 + u * 2 * E:64 + (u + 1) * 2 * E]
                            flat = lambda q: oh[:, q, :, :].rearrange("p k e -> p (k e)")
                            pe.matmul(out, pw("upto"), flat(u), start=True, stop=False)
                            for q in range(u):
                                pe.matmul(out, consts["ones"][:, 0:P], flat(q), start=False, stop=False)
                            mm = pe.matmul(out, consts["ones"][:, 0:P], run[:, :, :].rearrange("p k e -> p (k e)"),
                                           start=False, stop=True)
                        mm.then_inc(pos_ready, 1)
                if not last:
                    rows.tensor(pe, i + 1, misc, consts["ident"][:, :])
                down(E - 1)

            pe.wait_ge(w_in, 16)
            rows.tensor(pe, 0, misc, consts["ident"][:, :])
            with pe.Fori(0, NIT - 1) as i:
                trip(i)
            trip(NIT - 1, last=True)

        @block.scalar
        def _(act):
            def copy_x(i):
                act.wait_ge(rows.free, i + 1)
                act.activation(xT[:, :], misc[:, :], ACT.Copy).then_inc(xt, 1)

            def trip(i):
                act.wait_ge(rstep, i * RS + 2)
                act.activation(pr[:, :, :], pr[:, :, :], ACT.Exp).then_inc(ex_ready, 1)
                for n in range(E * FC):
                    e, f = n // FC, n % FC
                    act.wait_ge(h_ready, i * NHE + NH * n + 1)
                    if f == 0:
                        act.wait_ge(ye_ready, i * E + e + 1)
                    if gated:
                        act.wait_ge(g_ready, i * E * FC + n + 1)
                        act.activation(a_sb[:, n % 2, :], h_ps[0:FW, (2 * n) % HR, :], ACT.Silu
                                       ).then_inc(act_ready, 1)
                    else:
                        act.activation(G[:, e % 2, f, :], h_ps[0:FW, n % HR, :], ACT.Gelu).then_inc(g_ready, 1)

            copy_x(0)
            with act.Fori(0, NIT - 1) as i:
                trip(i)
                copy_x(i + 1)
            trip(NIT - 1)

        @block.vector
        def _(dve):
            dve.sem_inc(acc_ready, 2)
            dve.sem_inc(g_ready, HR // NH)
            dve.sem_inc(ye_ready, 2)
            dve.memset(run[:, :, :], 0.0).then_inc(run_ready, 1)
            dve.wait_ge(run_ready, 1)
            dve.wait_ge(w_in, 16)
            with dve.Fori(0, NIT) as i:
                def gates(e):
                    for f in range(FC):
                        n = e * FC + f
                        dve.wait_ge(act_ready, i * E * FC + n + 1)
                        dve.wait_ge(h_ready, i * NHE + 2 * n + 2)
                        if f == 0:
                            dve.wait_ge(ye_ready, i * E + e + 1)
                        dve.tensor_tensor(G[:, e % 2, f, :], a_sb[:, n % 2, :], h_ps[0:FW, (2 * n + 1) % HR, :],
                                          ALU.mult).then_inc(g_ready, 1)

                k = i * RS
                reset = pw("reset")
                dve.wait_ge(lg_ready, i + 1)
                lg = rt[:, 0:U * E].rearrange("p (u e) -> p u e", u=U)
                dve.tensor_reduce(m1[:, :], lg, AXX, ALU.max).then_inc(rstep, 1)
                dve.wait_ge(rstep, k + 1)
                dve.tensor_tensor(pr[:, :, :], lg, bcast(m1[:, :], 2, E), ALU.subtract).then_inc(rstep, 1)
                dve.wait_ge(ex_ready, i + 1)
                dve.tensor_reduce(sm[:, :], pr[:, :, :], AXX, ALU.add).then_inc(rstep, 1)
                dve.wait_ge(rstep, k + 3)
                dve.reciprocal(rs[:, :], sm[:, :]).then_inc(rstep, 1)
                dve.wait_ge(rstep, k + 4)
                dve.tensor_tensor(pr[:, :, :], pr[:, :, :], bcast(rs[:, :], 2, E), ALU.mult).then_inc(rstep, 1)
                dve.wait_ge(rstep, k + 5)
                top_one(dve, rstep, k + 5, pr[:, :, :], v[:, :, 0], eq[:, :, :], cum[:, :, :], reset,
                        oh[:, :, 0, :])
                if gated:
                    gates(0)
                dve.scalar_tensor_tensor(p2[:, :, :], oh[:, :, 0, :], -2.0, pr[:, :, :], ALU.mult, ALU.add
                                         ).then_inc(rstep, 1)
                dve.wait_ge(rstep, k + 10)
                top_one(dve, rstep, k + 10, p2[:, :, :], v[:, :, 1], eq[:, :, :], cum[:, :, :], reset,
                        oh[:, :, 1, :])
                dve.sem_inc(oh_ready, 1)
                if gated:
                    gates(1)
                dve.tensor_tensor(ss[:, :], v[:, :, 0], v[:, :, 1], ALU.add).then_inc(rstep, 1)
                dve.wait_ge(rstep, k + 15)
                dve.reciprocal(rss[:, :], ss[:, :]).then_inc(rstep, 1)
                dve.wait_ge(rstep, k + 16)
                dve.tensor_tensor(gate[:, :, :], v[:, :, :], bcast(rss[:, :], 2, 2), ALU.mult).then_inc(rstep, 1)
                src = oh
                if capacity:
                    src = kept
                    dve.wait_ge(pos_ready, i + 1)
                    dve.scalar_tensor_tensor(kept[:, :, :, :].rearrange("p u k e -> p (u k e)"),
                                             rt[:, 64:64 + U * 2 * E], float(capacity),
                                             oh[:, :, :, :].rearrange("p u k e -> p (u k e)"),
                                             ALU.is_le, ALU.mult).then_inc(cw_ready, 1)
                    for u in range(U):
                        dve.tensor_tensor(run[:, :, :], run[:, :, :], oh[:, u, :, :], ALU.add).then_inc(run_ready, 1)
                        dve.wait_ge(run_ready, i * U + u + 2)
                    dve.wait_ge(cw_ready, i + 1)
                dve.wait_ge(rstep, k + 17)
                for q in range(2):
                    dve.tensor_tensor(part[:, :, q, :], src[:, :, q, :], bcast(gate[:, :, q], 2, E),
                                      ALU.mult).then_inc(rstep, 1)
                dve.wait_ge(rstep, k + 19)
                dve.tensor_tensor(cw[:, :, :], part[:, :, 0, :], part[:, :, 1, :], ALU.add).then_inc(cw2, 1)
                dve.wait_ge(cw2, i + 1)

                def weigh(e):
                    dve.wait_ge(ye_ready, i * E + e + 3)
                    if e == 0:
                        prev = lambda u: x[:, bass.ds(i * U + u, 1), :].rearrange("p a d -> p (a d)")
                    else:
                        dve.wait_ge(acc_ready, i * E + e + 2)
                        prev = lambda u: nm.r[:, u, :]
                    for u in range(U):
                        last = dve.scalar_tensor_tensor(nm.r[:, u, :], ye[:, e % 2, u * D:(u + 1) * D],
                                                        cw[:, u, e:e + 1], prev(u), ALU.mult, ALU.add)
                    last.then_inc(acc_ready, 1)

                for e in range(1, E):
                    if gated and e > 1:
                        gates(e)
                    weigh(e - 1)
                weigh(E - 1)
                dve.wait_ge(acc_ready, i * E + E + 2)
                nm.stats.vector(dve, i, nm.r)
                nm.finish(dve, i)
    ph.close()


def heads_phase(nc, x, consts, weights, table):
    ph = Phase(nc, "sa0")
    LAT = 32
    w, w_in = weights, weights.loaded
    xT = ph.sb("xT", [P, W])
    lat = ph.sb("latent", [LAT, W])
    RQ = U
    qkv = ph.sb("qkv", [P, RQ, 3, H, HD])
    t1 = ph.sb("rope_cos", [P, RQ, 2, H, HD])
    t2 = ph.sb("rope_sin", [P, RQ, 2, H, HD])
    qk = ph.sb("rotated", [P, RQ, 2, H, HD])
    pq = ph.sb("products", [P, RQ, H, H, HD])
    pv = ph.sb("weighted", [P, H, HD, H])
    att = ph.sb("att", [P, RQ, H, H])
    mx, sm, rs = (ph.sb(n, [P, RQ, H]) for n in ("max", "sum", "rsum"))
    ov = ph.sb("ov", [P, RQ, H, HD])
    o = ph.sb("o", [P, U, D])
    oT = ph.sb("oT", [P, U, T])
    xt_ps, lat_ps = ph.ps("xT", [P, W]), ph.ps("latent", [LAT, W])
    qkv_ps = ph.ps("qkv", [P, 2, 512])
    y = ph.ps("y", [P, W])
    rows = Rows(ph, x)
    nm = Norm(ph, x, consts, y)
    (xt, lp, lt, qkv_in, qkv_out, cos_done, rot_done, pq_done, att_done, max_done, sub_done, exp_done, sum_done,
     pv_done, ov_done, o_done, ot_in, ot_out) = (ph.sem(n) for n in (
         "xT_ready", "latent_in_psum", "latent_ready", "qkv_in_psum", "qkv_ready", "roped_parts",
         "rotated_ready", "products_ready", "att_ready", "max_ready", "shifted_ready", "exp_ready", "sum_ready",
         "weighted_ready", "ov_ready", "o_ready", "ot_in_psum", "ot_ready"))
    pw = lambda n: pick(w, table, n)
    yo = lambda u: y[:, u * D:(u + 1) * D]

    with nc.Block() as block:
        @block.sync
        def _(sp):
            weights.load_next(sp)

        @block.gpsimd
        def _(pool):
            pool.wait_ge(w_in, 16)
            pool.sem_inc(pq_done, RQ)
            rows.gpsimd(pool, 0, first=True)

            def rotate(i, rows_of):
                for u in rows_of:
                    s = u % RQ
                    n = i * U + u
                    pool.wait_ge(qkv_out, n + 1 + 2)
                    src = qkv[:, s, 0:2, :, :].rearrange("p a h e -> p (a h) e")
                    ca = t1[:, s, :, :, :].rearrange("p a h e -> p (a h) e")
                    si = t2[:, s, :, :, :].rearrange("p a h e -> p (a h) e")
                    pool.tensor_tensor(ca, src, bcast(pw("cos"), 1, 2 * H), ALU.mult).then_inc(cos_done, 1)
                    pool.tensor_tensor(si[:, :, 0:HD // 2], src[:, :, HD // 2:HD],
                                       bcast(pw("sin")[:, 0:HD // 2], 1, 2 * H), ALU.mult).then_inc(cos_done, 1)
                    pool.tensor_tensor(si[:, :, HD // 2:HD], src[:, :, 0:HD // 2],
                                       bcast(pw("sin")[:, HD // 2:HD], 1, 2 * H), ALU.mult).then_inc(cos_done, 1)
                    pool.wait_ge(cos_done, n * 3 + 3)
                    pool.tensor_tensor(qk[:, s, :, :, :].rearrange("p a h e -> p (a h) e"), ca, si,
                                       ALU.add).then_inc(rot_done, 1)
                    pool.wait_ge(rot_done, n + 1)
                    pool.wait_ge(att_done, n + 1)
                    pool.tensor_tensor(pq[:, s, :, :, :], bcast(qk[:, s, 0, :, :], 2, H),
                                       bcast(qk[:, s, 1, :, :], 1, H), ALU.mult).then_inc(pq_done, 1)

            rows.gpsimd(pool, 1)
            rotate(0, range(U))
            with pool.Fori(1, NIT - 1) as i:
                rows.gpsimd(pool, i + 1)
                rotate(i, range(2))
                nm.gpsimd(pool, i - 1)
                rotate(i, range(2, U))
            rotate(NIT - 1, range(2))
            nm.gpsimd(pool, NIT - 2)
            rotate(NIT - 1, range(2, U))
            nm.gpsimd(pool, NIT - 1)

        def out_row(pe, i, v):
            pe.wait_ge(o_done, i * U + v + 1)
            if v == 0:
                pe.wait_ge(nm.r_ready, i + 1)
            pe.transpose(yo(v), o[:, v, :], consts["ident"][:, :]).then_inc(ot_in, 1)
            pe.wait_ge(ot_out, i * U + v + 1)
            pe.matmul(yo(v), consts["ones"][0:1, 0:P], pw("bout"), start=True, stop=False)
            mm = pe.matmul(yo(v), oT[:, v, :], pw("wout"), start=False, stop=True)
            if v == U - 1:
                mm.then_inc(nm.y_ready, 1)

        @block.tensor
        def _(pe):
            def latent(i):
                rows.tensor(pe, i, xt_ps, consts["ident"][:, :])
                pe.wait_ge(xt, i + 1)
                pe.matmul(lat_ps[:, :], pw("wdown"), xT[:, :], start=True, stop=True).then_inc(lp, 1)

            def project(i, u):
                bank = qkv_ps[:, u % 2, :]
                if u == 0:
                    pe.wait_ge(lt, i + 1)
                pe.wait_ge(qkv_out, i * U + u + 1)
                pe.matmul(bank[:, 0:D], consts["ones"][0:1, 0:P], pw("bq"), start=True, stop=False)
                pe.matmul(bank[:, 0:D], xT[:, u * T:(u + 1) * T], pw("wq"), start=False, stop=True)
                pe.matmul(bank[:, D:3 * D], consts["ones"][0:1, 0:P], pw("bup"), start=True, stop=False)
                pe.matmul(bank[:, D:3 * D], lat[:, u * T:(u + 1) * T], pw("wup"), start=False,
                          stop=True).then_inc(qkv_in, 1)

            def trip(i, first=False, last=False, tail=False):
                for u in range(1 if tail else U):
                    if u == 0 and not first:
                        if not tail:
                            project(i, U - 1)
                        out_row(pe, i - 1, U - 1)
                    if u == 0 and not (last or tail):
                        latent(i + 1)
                    if u > 0:
                        if not last:
                            project(i + 1, u - 1)
                        out_row(pe, i, u - 1)

            pe.wait_ge(w_in, 16)
            latent(0)
            for u in range(U):
                project(0, u)
            trip(0, first=True)
            with pe.Fori(1, NIT - 1) as i:
                trip(i)
            trip(NIT - 1, last=True)
            trip(NIT, tail=True)

        @block.scalar
        def _(act):
            def latent(i):
                act.wait_ge(rows.free, i + 1)
                act.activation(xT[:, :], xt_ps[:, :], ACT.Copy).then_inc(xt, 1)
                act.wait_ge(lp, i + 1)
                act.activation(lat[:, :], lat_ps[:, :], ACT.Identity, bias=pw("bdown")[:, 0:1]).then_inc(lt, 1)

            def project(i, u):
                n = i * U + u
                act.wait_ge(qkv_in, n + 1)
                act.wait_ge(pv_done, n + 1)
                act.activation(qkv[:, u % RQ, :, :, :],
                               qkv_ps[:, u % 2, 0:3 * D].rearrange("p (a h e) -> p a h e", a=3, h=H),
                               ACT.Copy).then_inc(qkv_out, 1)

            def copy_out(i, v):
                act.wait_ge(ot_in, i * U + v + 1)
                act.activation(oT[:, v, :], yo(v), ACT.Copy).then_inc(ot_out, 1)

            def trip(i, first=False, last=False, tail=False):
                for u in range(1 if tail else U):
                    if not tail:
                        act.wait_ge(sub_done, i * U + u + 1)
                        act.activation(att[:, u % RQ, :, :], att[:, u % RQ, :, :], ACT.Exp,
                                       scale=HD ** -0.5).then_inc(exp_done, 1)
                    if u == 0 and not first:
                        if not tail:
                            project(i, U - 1)
                        copy_out(i - 1, U - 1)
                    if u == 0 and not (last or tail):
                        latent(i + 1)
                    if u > 0:
                        if not last:
                            project(i + 1, u - 1)
                        copy_out(i, u - 1)

            act.sem_inc(qkv_out, 2)
            act.wait_ge(w_in, 16)
            latent(0)
            for u in range(U):
                project(0, u)
            trip(0, first=True)
            with act.Fori(1, NIT - 1) as i:
                trip(i)
            trip(NIT - 1, last=True)
            trip(NIT, tail=True)

        @block.vector
        def _(dve):
            def scores(i, u):
                n, s = i * U + u, u % RQ
                dve.wait_ge(pq_done, n + 1 + RQ)
                dve.tensor_reduce(att[:, s, :, :], pq[:, s, :, :, :], AXX, ALU.add).then_inc(att_done, 1)
                dve.wait_ge(att_done, n + 1 + RQ)
                dve.tensor_reduce(mx[:, s, :], att[:, s, :, :], AXX, ALU.max).then_inc(max_done, 1)
                dve.wait_ge(max_done, n + 1)
                dve.tensor_tensor(att[:, s, :, :], att[:, s, :, :], bcast(mx[:, s, :], 2, H),
                                  ALU.subtract).then_inc(sub_done, 1)

            def outputs(i, v):
                n, s = i * U + v, v % RQ
                dve.wait_ge(exp_done, n + 1)
                dve.tensor_reduce(sm[:, s, :], att[:, s, :, :], AXX, ALU.add).then_inc(sum_done, 1)
                dve.tensor_tensor(pv[:, :, :, :], bcast(att[:, s, :, :], 2, HD),
                                  bcast(qkv[:, s, 2, :, :].rearrange("p g e -> p e g"), 1, H),
                                  ALU.mult).then_inc(pv_done, 1)
                dve.wait_ge(sum_done, 2 * n + 1)
                dve.reciprocal(rs[:, s, :], sm[:, s, :]).then_inc(sum_done, 1)
                dve.wait_ge(pv_done, n + 1 + RQ)
                dve.tensor_reduce(ov[:, s, :, :], pv[:, :, :, :], AXX, ALU.add).then_inc(ov_done, 1)
                dve.wait_ge(ov_done, n + 1)
                dve.wait_ge(sum_done, 2 * n + 2)
                dve.tensor_tensor(o[:, v, :].rearrange("p (h e) -> p h e", h=H), ov[:, s, :, :],
                                  bcast(rs[:, s, :], 2, HD), ALU.mult).then_inc(o_done, 1)

            def trip(i, first=False, tail=False):
                for u in range(3 if tail else U):
                    if not tail:
                        scores(i, u)
                    if u == 1 and not first:
                        nm.begin(dve, i - 1)
                    if u == 0 and not first:
                        outputs(i - 1, U - 1)
                    if u > 0 and not tail:
                        outputs(i, u - 1)
                    if u == 2 and not first:
                        nm.finish(dve, i - 1)

            dve.sem_inc(nm.r_ready, 1)
            dve.sem_inc(att_done, RQ)
            dve.sem_inc(pv_done, RQ)
            trip(0, first=True)
            with dve.Fori(1, NIT) as i:
                trip(i)
            trip(NIT, tail=True)
    ph.close()


HQ = 4
QW = D // HQ
RW = 4 * QW + HQ


def delta_phase(nc, x, consts, weights, table, rec, outs):
    ph = Phase(nc, "sa1")
    PC = 3 * D + 2 * H
    w, w_in = weights, weights.loaded
    pw = lambda n: pick(w, table, n)
    xT = ph.sb("xT", [P, W])
    sg = ph.sb("sigmoid", [P, 2, PC])
    qkv = ph.sb("qkv", [P, 2, 3, H, HD])
    sq = ph.sb("ksquare", [P, 2, H, HD])
    ss, nr, co, c2 = (ph.sb(n, [P, 2, H]) for n in ("ksum", "knorm", "coef", "coef_raw"))
    rc = ph.sb("records", [P, 2, HQ, RW])
    xt_ps = ph.ps("xT", [P, W])
    pj = ph.ps("pj", [P, 2, 512])
    rows = Rows(ph, x)
    (xt, pj_in, sg_out, qkv_done, sq_done, ss_done, nr_done, co_done, rc_done) = (ph.sem(n) for n in (
        "xT_ready", "pj_ready", "sigmoid_ready", "qkv_ready", "ksquare_ready", "ksum_ready", "knorm_ready",
        "coef_ready", "record_parts"))
    stored = [ph.sem(f"record_stored{r}") for r in range(2)]
    half = ph.sb("half", [P, H])
    half_set = ph.sem("half_set")
    nr2 = ph.sem("rnorm_ready")

    with nc.Block() as block:
        @block.sync
        def _(sp):
            weights.load_next(sp)
            with sp.Fori(0, NIT) as i:
                for u in range(U):
                    sp.wait_ge(rc_done, (i * U + u + 1) * 5 + 10)
                    sp.dma_start(rec[bass.ds(i * U + u, 1)].rearrange("a h t w -> t (a h) w"), rc[:, u % 2, :, :]
                                 ).then_inc(stored[u % 2], 16)
            for s in stored:
                sp.wait_ge(s, B // 2 * 16 + 16)

        @block.gpsimd
        def _(pool):
            pool.memset(half[:, :], 0.5).then_inc(half_set, 1)
            rows.gpsimd(pool, 0, first=True)
            pool.wait_ge(half_set, 1)

            def knorm(i):
                for u in range(U):
                    pool.wait_ge(ss_done, i * U + u + 1)
                    pool.tensor_tensor(nr[:, u % 2, :], ss[:, u % 2, :], half[:, :], ALU.pow
                                       ).then_inc(nr_done, 1)

            with pool.Fori(0, NIT - 1) as i:
                rows.gpsimd(pool, i + 1)
                knorm(i)
            knorm(NIT - 1)

        @block.tensor
        def _(pe):
            pe.wait_ge(w_in, 16)
            with pe.Fori(0, NIT) as i:
                rows.tensor(pe, i, xt_ps, consts["ident"][:, :])
                pe.wait_ge(xt, i + 1)
                for u in range(U):
                    pe.wait_ge(qkv_done, (i * U + u) * 1 + 1)
                    pe.matmul(pj[:, u % 2, 0:PC], xT[:, u * T:(u + 1) * T], pw("wproj"), start=True,
                              stop=True).then_inc(pj_in, 1)

        @block.scalar
        def _(act):
            with act.Fori(0, NIT) as i:
                act.wait_ge(rows.free, i + 1)
                act.activation(xT[:, :], xt_ps[:, :], ACT.Copy).then_inc(xt, 1)
                for u in range(U):
                    act.wait_ge(pj_in, i * U + u + 1)
                    act.wait_ge(rc_done, (i * U + u + 1) * 5)
                    act.activation(sg[:, u % 2, :], pj[:, u % 2, 0:PC], ACT.Sigmoid).then_inc(sg_out, 1)

        @block.vector
        def _(dve):
            dve.sem_inc(qkv_done, 2)
            dve.sem_inc(rc_done, 10)
            dve.sem_inc(stored[0], 16)
            dve.sem_inc(stored[1], 16)
            with dve.Fori(0, NIT) as i:
                for u in range(U):
                    n, s = i * U + u, u % 2
                    quarter = lambda k, a: rc[:, s, :, k * QW:(k + 1) * QW].rearrange("p q (h e) -> p q h e", e=HD)
                    heads = lambda t: t.rearrange("p (q h) e -> p q h e", q=HQ)
                    dve.wait_ge(sg_out, n + 1)
                    dve.tensor_tensor(qkv[:, s, :, :, :].rearrange("p a h e -> p (a h e)"), sg[:, s, 0:3 * D],
                                      pj[:, s, 0:3 * D], ALU.mult).then_inc(qkv_done, 1)
                    dve.tensor_tensor(c2[:, s, :], sg[:, s, 3 * D:3 * D + H], sg[:, s, 3 * D + H:PC],
                                      ALU.mult).then_inc(co_done, 1)
                    dve.wait_ge(qkv_done, n + 3)
                    dve.tensor_tensor(sq[:, s, :, :], qkv[:, s, 1, :, :], qkv[:, s, 1, :, :],
                                      ALU.mult).then_inc(sq_done, 1)
                    dve.wait_ge(co_done, 2 * n + 1)
                    dve.scalar_tensor_tensor(co[:, s, :], c2[:, s, :], -1.0, sg[:, s, 3 * D + H:PC], ALU.mult,
                                             ALU.mult).then_inc(co_done, 1)
                    dve.wait_ge(sq_done, n + 1)
                    dve.tensor_reduce(ss[:, s, :], sq[:, s, :, :], AXX, ALU.add).then_inc(ss_done, 1)
                    dve.wait_ge(stored[s], (i * 2 + u // 2 + 1) * 16)
                    rq = lambda k: rc[:, s, :, k * QW:(k + 1) * QW]
                    flat = lambda k: qkv[:, s, k, :, :].rearrange("p (q h) e -> p q (h e)", q=HQ)
                    dve.tensor_copy(rq(0), flat(0)).then_inc(rc_done, 1)
                    dve.tensor_copy(rq(2), flat(2)).then_inc(rc_done, 1)
                    dve.tensor_copy(rc[:, s, :, 4 * QW:RW],
                                    sg[:, s, 3 * D + H:PC].rearrange("p (q h) -> p q h", q=HQ)).then_inc(rc_done, 1)
                    dve.wait_ge(nr_done, n * 1 + 1)
                    dve.tensor_scalar(nr[:, s, :], nr[:, s, :], 1e-12, None, ALU.max).then_inc(nr2, 1)
                    dve.wait_ge(nr2, 2 * n + 1)
                    dve.reciprocal(nr[:, s, :], nr[:, s, :]).then_inc(nr2, 1)
                    dve.wait_ge(nr2, 2 * n + 2)
                    dve.tensor_tensor(rc[:, s, :, QW:2 * QW].rearrange("p q (h e) -> p q h e", e=HD),
                                      heads(qkv[:, s, 1, :, :]),
                                      bcast(nr[:, s, :].rearrange("p (q h) -> p q h", q=HQ), 3, HD),
                                      ALU.mult).then_inc(rc_done, 1)
                    dve.wait_ge(rc_done, n * 5 + 14)
                    dve.tensor_tensor(rc[:, s, :, 3 * QW:4 * QW].rearrange("p q (h e) -> p q h e", e=HD),
                                      rc[:, s, :, QW:2 * QW].rearrange("p q (h e) -> p q h e", e=HD),
                                      bcast(co[:, s, :].rearrange("p (q h) -> p q h", q=HQ), 3, HD),
                                      ALU.mult).then_inc(rc_done, 1)
    ph.close()

    ph = Phase(nc, "scan")
    TC, HH = 16, H // HQ
    NC = T // TC
    rb = ph.sb("records", [P, 2, TC, RW])
    SH = ph.sb("states", [P, TC + 1, HH, HD, HD])
    tmp, kU = ph.sb("aS", [P, HH, HD, HD]), ph.sb("kU", [P, HH, HD, HD])
    Sd = ph.sb("decayed", [P, 2, HH, HD, HD])
    ra, uu = ph.sb("aS_sum", [P, HH, HD]), ph.sb("u", [P, HH, HD])
    qS = ph.sb("qS", [P, TC, HH, HD, HD])
    ob = ph.sb("out", [P, 2, TC, HH, HD])
    (tmp_done, ra_done, u_done, ku_done, s_done, sd_done, qs_done, o_done) = (ph.sem(n) for n in (
        "aS_ready", "aS_sum_ready", "u_ready", "kU_ready", "state_ready", "decayed_ready", "qS_ready", "out_ready"))
    rb_in = [ph.sem(f"records_loaded{r}") for r in range(2)]
    o_out = [ph.sem(f"out_stored{r}") for r in range(2)]
    recp = rec.rearrange("b q t w -> (b q) (t w)")
    outp = outs.rearrange("b q t w -> (b q) (t w)")
    with nc.Block() as block:
        @block.sync
        def _(sp):
            for k in range(2):
                sp.dma_start(rb[:, k, :, :].rearrange("p t w -> p (t w)"), recp[:, k * TC * RW:(k + 1) * TC * RW]
                             ).then_inc(rb_in[k], 16)
            for c in range(NC):
                sp.wait_ge(o_done, c + 1 + 1)
                sp.dma_start(outp[:, c * TC * QW:(c + 1) * TC * QW],
                             ob[:, c % 2, :, :, :].rearrange("p t h e -> p (t h e)")).then_inc(o_out[c % 2], 16)
                if c + 2 < NC:
                    k = c + 2
                    sp.dma_start(rb[:, k % 2, :, :].rearrange("p t w -> p (t w)"),
                                 recp[:, k * TC * RW:(k + 1) * TC * RW]).then_inc(rb_in[k % 2], 16)
            for s in o_out:
                sp.wait_ge(s, NC // 2 * 16 + 16)

        def field(c2, t, k):
            return rb[:, c2, t, k * QW:(k + 1) * QW].rearrange("p (h e) -> p h e", h=HH)

        def read_out(pool, c, c2, t):
            if t == 1:
                pool.wait_ge(o_done, c + 1)
            pool.tensor_tensor(qS[:, t - 1, :, :, :], SH[:, t, :, :, :], bcast(field(c2, t - 1, 0), 2, HD),
                               ALU.mult).then_inc(qs_done, 1)

        @block.gpsimd
        def _(pool):
            with pool.Fori(0, NC // 2) as cc:
                for c2 in range(2):
                    c = cc * 2 + c2
                    pool.wait_ge(rb_in[c2], cc * 16 + 16)
                    for t in range(TC):
                        f = rb[:, c2, t, 4 * QW:RW]
                        pool.wait_ge(s_done, c * (TC + 1) + t + 1)
                        pool.tensor_tensor(Sd[:, t % 2, :, :, :].rearrange("p h a b -> p h (a b)"),
                                           SH[:, t, :, :, :].rearrange("p h a b -> p h (a b)"),
                                           bcast(f, 2, HD * HD), ALU.mult).then_inc(sd_done, 1)
                        if t > 0:
                            read_out(pool, c, c2, t)
                    pool.wait_ge(s_done, c * (TC + 1) + TC + 1)
                    read_out(pool, c, c2, TC)

        @block.vector
        def _(dve):
            dve.sem_inc(o_done, 1)
            dve.memset(SH[:, 0, :, :, :], 0.0).then_inc(s_done, 1)
            dve.wait_ge(s_done, 1)
            for k in range(2):
                dve.sem_inc(o_out[k], 16)
            with dve.Fori(0, NC // 2) as cc:
                for c2 in range(2):
                    c = cc * 2 + c2
                    dve.wait_ge(rb_in[c2], cc * 16 + 16)
                    for t in range(TC):
                        n = c * TC + t
                        dve.tensor_tensor(tmp[:, :, :, :], SH[:, t, :, :, :], bcast(field(c2, t, 3), 2, HD),
                                          ALU.mult).then_inc(tmp_done, 1)
                        dve.wait_ge(tmp_done, n + 1)
                        dve.tensor_reduce(ra[:, :, :], tmp[:, :, :, :], AXX, ALU.add).then_inc(ra_done, 1)
                        dve.wait_ge(ra_done, n + 1)
                        dve.tensor_tensor(uu[:, :, :], ra[:, :, :], field(c2, t, 2), ALU.add).then_inc(u_done, 1)
                        dve.wait_ge(u_done, n + 1)
                        dve.tensor_tensor(kU[:, :, :, :], bcast(uu[:, :, :], 3, HD), bcast(field(c2, t, 1), 2, HD),
                                          ALU.mult).then_inc(ku_done, 1)
                        dve.wait_ge(ku_done, n + 1)
                        dve.wait_ge(sd_done, n + 1)
                        dve.tensor_tensor(SH[:, t + 1, :, :, :], Sd[:, t % 2, :, :, :], kU[:, :, :, :],
                                          ALU.add).then_inc(s_done, 1)
                        dve.wait_ge(s_done, c * (TC + 1) + t + 2)
                    dve.wait_ge(qs_done, c * TC + TC)
                    dve.wait_ge(o_out[c2], cc * 16 + 16)
                    dve.tensor_reduce(ob[:, c2, :, :, :], qS[:, :, :, :, :], AXX, ALU.add).then_inc(o_done, 1)
                    dve.tensor_copy(SH[:, 0, :, :, :], SH[:, TC, :, :, :]).then_inc(s_done, 1)
                    dve.wait_ge(s_done, (c + 1) * (TC + 1) + 1)
    ph.close()

    ph = Phase(nc, "gate")
    w, w_in = weights, weights.loaded
    xT = ph.sb("xT", [P, W])
    g1 = ph.sb("g1", [HD, W])
    gt, ol, og, z, zn, zT = (ph.sb(n, [P, U, D]) for n in ("gate", "o", "gated", "z", "zn", "zT"))
    xt_ps, g1_ps, gt_ps, z_ps, y = (ph.ps(n, [P, W]) for n in ("xT", "g1", "gate", "zT", "y"))
    rows = Rows(ph, x)
    nm = Norm(ph, x, consts, y)
    inner = Stats(ph, consts, "inner_")
    (ol_in, xt, g1_in, g1_out, gt_in, gt_out, og_done, z_done, zn_done, zt_in, zt_out) = (ph.sem(n) for n in (
        "o_loaded", "xT_ready", "g1_in_psum", "g1_ready", "gate_in_psum", "gate_ready", "gated_ready",
        "z_ready", "zn_ready", "zT_in_psum", "zT_ready"))
    flat = lambda a: a[:, :, :].rearrange("p u d -> p (u d)")
    with nc.Block() as block:
        @block.sync
        def _(sp):
            with sp.Fori(0, NIT) as i:
                sp.wait_ge(og_done, i + 1)
                for u in range(U):
                    sp.dma_start(ol[:, u, :].rearrange("p (q e) -> p q e", q=HQ),
                                 outs[bass.ds(i * U + u, 1)].rearrange("a q t e -> t (a q) e")).then_inc(ol_in, 16)

        @block.gpsimd
        def _(pool):
            rows.gpsimd(pool, 0, first=True)
            with pool.Fori(0, NIT - 1) as i:
                rows.gpsimd(pool, i + 1)
                inner.gpsimd(pool, i)
                nm.gpsimd(pool, i)
            inner.gpsimd(pool, NIT - 1)
            nm.gpsimd(pool, NIT - 1)

        @block.tensor
        def _(pe):
            pe.wait_ge(w_in, 16)
            with pe.Fori(0, NIT) as i:
                rows.tensor(pe, i, xt_ps, consts["ident"][:, :])
                pe.wait_ge(xt, i + 1)
                pe.matmul(g1_ps[0:HD, :], pw("wg1"), xT[:, :], start=True, stop=True).then_inc(g1_in, 1)
                pe.wait_ge(g1_out, i + 1)
                for u in range(U):
                    mm = pe.matmul(gt_ps[:, u * D:(u + 1) * D], g1[:, u * T:(u + 1) * T], pw("wg2"), start=True,
                                   stop=True)
                mm.then_inc(gt_in, 1)
                pe.wait_ge(zn_done, i + 1)
                for u in range(U):
                    mm = pe.transpose(z_ps[:, u * T:(u + 1) * T], zn[:, u, :], consts["ident"][:, :])
                mm.then_inc(zt_in, 1)
                pe.wait_ge(zt_out, i + 1)
                pe.wait_ge(nm.r_ready, i + 1)
                for u in range(U):
                    mm = pe.matmul(y[:, u * D:(u + 1) * D], zT[:, u, :], pw("wo"), start=True, stop=True)
                mm.then_inc(nm.y_ready, 1)

        @block.scalar
        def _(act):
            with act.Fori(0, NIT) as i:
                act.wait_ge(rows.free, i + 1)
                act.activation(xT[:, :], xt_ps[:, :], ACT.Copy).then_inc(xt, 1)
                act.wait_ge(g1_in, i + 1)
                act.activation(g1[:, :], g1_ps[0:HD, :], ACT.Copy).then_inc(g1_out, 1)
                act.wait_ge(gt_in, i + 1)
                act.activation(flat(gt), gt_ps[:, :], ACT.Sigmoid).then_inc(gt_out, 1)
                act.wait_ge(zt_in, i + 1)
                act.activation(flat(zT), z_ps[:, :], ACT.Copy).then_inc(zt_out, 1)

        @block.vector
        def _(dve):
            dve.sem_inc(nm.r_ready, 1)
            dve.sem_inc(og_done, 1)
            dve.wait_ge(w_in, 16)
            with dve.Fori(0, NIT) as i:
                dve.wait_ge(gt_out, i + 1)
                dve.wait_ge(ol_in, (i + 1) * 16 * U)
                dve.tensor_tensor(flat(og), flat(ol), flat(gt), ALU.mult).then_inc(og_done, 1)
                dve.wait_ge(og_done, i + 2)
                inner.vector(dve, i, og)
                dve.wait_ge(inner.rstd_ready, i + 1)
                for u in range(U):
                    dve.tensor_scalar(z[:, u, :], og[:, u, :], inner.mv[:, u, 0:1], inner.rstd[:, u:u + 1],
                                      ALU.subtract, ALU.mult).then_inc(z_done, 1)
                dve.wait_ge(z_done, i * U + U)
                dve.tensor_tensor(zn[:, :, :], z[:, :, :], bcast(pw("norm_w"), 1, U), ALU.mult).then_inc(zn_done, 1)
                nm.vector(dve, i)
    ph.close()


def ssm_phase(nc, x, consts, weights, table):
    ph = Phase(nc, "ssm")
    NCH, NS, KC = 2, 16, 4
    NB = P // NS
    NR = NCH * P // NB
    PAD = KC - 1
    w = weights
    pw = lambda n: pick(w, table, n)
    xn = ph.sb("xn", [P, U, D])
    xT = ph.sb("xnT", [P, W])
    xp = ph.sb("xp", [P, NCH, U, T + PAD])
    sgate = ph.sb("silu_gate", [P, 2, NCH, W])
    cv = ph.sb("conv", [P, NCH, U, T])
    xc = ph.sb("xc", [P, 2, NCH, W])
    BC = ph.sb("BC", [P, 2, 2, W])
    sig_a = ph.sb("decay", [P, NR])
    within = ph.sb("within", [P, U, T])
    dec = ph.sb("decays", [P, NR, W])
    UR = 4
    uu, hh, hc = (ph.sb(n, [P, UR, W]) for n in ("u", "h", "hC"))
    yg, yd = ph.sb("y_gated", [P, NCH, W]), ph.sb("y_skip", [P, NCH, W])
    pj = ph.ps("pj", [P, 2, W])
    xr_ps = ph.ps("xr", [P, 2, W])
    ya = ph.ps("ya", [P, NCH, W])
    y = ph.ps("y", [P, W])
    nm = Norm(ph, x, consts, y, x_times=2.0)
    pre = Stats(ph, consts, "pre_")
    w_in = weights.loaded
    (sig_done, dec_done, pad_done, xn_done, pj_in, pj_out, cv_done, xc_done, xr_in, u_done, h_done, hc_done,
     ya_in, yd_done, yg_done) = (ph.sem(n) for n in (
         "sigmoid_ready", "decay_ready", "pads_ready", "xn_ready", "pj_ready", "pj_done", "conv_ready", "xc_ready",
         "xr_ready", "u_ready", "h_ready", "hC_ready", "ya_ready", "skip_ready", "gated_ready"))
    NJ = 1 + 4 + 2
    flat = lambda a: a.rearrange("p a b -> p (a b)")
    row = lambda i, u: x[:, bass.ds(i * U + u, 1), :].rearrange("p a d -> p (a d)")
    SCAN_LAG, HC_LAG, GATHER_LAG = 1, 2, 3
    SKIP0, SKIP1, Y_AT, NORM_A, NORM_POW, NORM_B = 21, 5, 8, 10, 11, 12
    PRE_A, PRE_POW, PRE_B, XT_AT, IN_AT, CONV_AT, BC_AT = 13, 14, 15, 16, 17, 20, 28
    TAIL = NORM_B + 1

    def block_at(n, lag, first, tail):
        m = n - lag
        return None if (m < 0 and first) or (m >= 0 and tail) else m

    with nc.Block() as block:
        @block.sync
        def _(sp):
            weights.load_next(sp)

        @block.gpsimd
        def _(pool):
            def trip(i, par, first=False, last=False, tail=False):
                for n in range(TAIL if tail else NR):
                    m = block_at(n, HC_LAG, first, tail)
                    if m is not None:
                        c_of = BC[:, par if m >= 0 else 1 - par, 1, :]
                        pool.wait_ge(h_done, i * NR + m + 1 + UR)
                        pool.wait_ge(ya_in, i * NR + m + 1)
                        pool.tensor_tensor(hc[:, m % UR, :], hh[:, m % UR, :], c_of, ALU.mult).then_inc(hc_done, 1)
                    if n == NORM_POW and not first:
                        nm.gpsimd(pool, i - 1)
                    if n == PRE_POW and not (last or tail):
                        pre.gpsimd(pool, i + 1)

            pool.memset(xp[:, :, :, :], 0.0).then_inc(pad_done, 1)
            pool.memset(within[:, :, :], 1.0).then_inc(pad_done, 1)
            pool.wait_ge(pad_done, 2)
            pool.memset(within[:, :, 0:1], 0.0).then_inc(pad_done, 1)
            pool.sem_inc(hc_done, UR)
            pre.gpsimd(pool, 0)
            trip(0, 0, first=True)
            with pool.Fori(1, NIT - 2, 2) as i:
                trip(i, 1)
                trip(i + 1, 0)
            trip(NIT - 1, 1, last=True)
            trip(NIT, 0, tail=True)

        @block.tensor
        def _(pe):
            def transpose_x(g):
                pe.wait_ge(xn_done, (g + 1) * U)
                if not (isinstance(g, int) and g == 0):
                    pe.wait_ge(pj_out, g * NJ)
                for u in range(U):
                    mm = pe.transpose(pj[:, 0, u * T:(u + 1) * T], xn[:, u, :], consts["ident"][:, :])
                mm.then_inc(pj_in, 1)

            def project_in(g, j):
                pe.wait_ge(pj_out, g * NJ + max(j - 1, 1))
                pe.matmul(pj[:, j % 2, :], pw("w_in")[:, (j - 1) * P:j * P], xT[:, :], start=True,
                          stop=True).then_inc(pj_in, 1)

            def project_bc(g, par, k):
                if k == 0:
                    pe.wait_ge(xc_done, (g + 1) * NCH)
                pe.wait_ge(pj_out, g * NJ + 4 + k)
                for c in range(NCH):
                    mm = pe.matmul(pj[:, (5 + k) % 2, :], pw("w_bc")[:, (k * NCH + c) * P:(k * NCH + c + 1) * P],
                                   xc[:, par, c, :], start=(c == 0), stop=(c == NCH - 1))
                mm.then_inc(pj_in, 1)

            def trip(i, par, first=False, last=False, tail=False):
                for n in range(TAIL if tail else NR):
                    if not tail:
                        c, q = n // NS, n % NS
                        pe.wait_ge(u_done, i * NR + n + 1)
                        pe.matmul(xr_ps[:, n % 2, :], pw("spread")[:, q * P:(q + 1) * P], xc[:, par, c, :],
                                  start=True, stop=True).then_inc(xr_in, 1)
                    m = block_at(n, GATHER_LAG, first, tail)
                    if m is not None:
                        c, q = m % NR // NS, m % NS
                        pe.wait_ge(hc_done, i * NR + m + 1 + UR)
                        if q == 0:
                            pe.wait_ge(yd_done, i * NCH + c + 1)
                        pe.matmul(ya[:, c, :], pw("gather")[:, q * P:(q + 1) * P], hc[:, m % UR, :], start=(q == 0),
                                  stop=(q == NS - 1)).then_inc(ya_in, 1)
                    if n == Y_AT and not first:
                        pe.wait_ge(yg_done, i * NCH)
                        pe.wait_ge(nm.r_ready, i)
                        for u in range(U):
                            yu = y[:, u * D:(u + 1) * D]
                            pe.matmul(yu, consts["ones"][0:1, 0:P], pw("b_out"), start=True, stop=False)
                            for c in range(NCH):
                                mm = pe.matmul(yu, yg[:, c, u * T:(u + 1) * T], pw("w_out")[:, c * D:(c + 1) * D],
                                               start=False, stop=(c == NCH - 1))
                        mm.then_inc(nm.y_ready, 1)
                    if not (last or tail):
                        if n == XT_AT:
                            transpose_x(i + 1)
                        if 0 <= n - IN_AT < 4:
                            project_in(i + 1, n - IN_AT + 1)
                        if 0 <= n - BC_AT < 2:
                            project_bc(i + 1, 1 - par, n - BC_AT)

            pe.sem_inc(ya_in, UR)
            pe.wait_ge(w_in, 16)
            transpose_x(0)
            for j in range(1, 5):
                project_in(0, j)
            for k in range(2):
                project_bc(0, 0, k)
            trip(0, 0, first=True)
            with pe.Fori(1, NIT - 2, 2) as i:
                trip(i, 1)
                trip(i + 1, 0)
            trip(NIT - 1, 1, last=True)
            trip(NIT, 0, tail=True)

        @block.scalar
        def _(act):
            def copy_in(g, par, j):
                act.wait_ge(pj_in, g * NJ + j + 1)
                if j == 0:
                    act.activation(xT[:, :], pj[:, 0, :], ACT.Identity, scale=pw("ln_g")[:, 0:1],
                                   bias=pw("ln_b")[:, 0:1]).then_inc(pj_out, 1)
                    return
                c, b = (j - 1) % 2, pw("b_in")[:, j - 1:j]
                if j < 3:
                    act.activation(xp[:, c, :, PAD:], pj[:, j % 2, :].rearrange("p (u t) -> p u t", u=U),
                                   ACT.Identity, bias=b).then_inc(pj_out, 1)
                else:
                    act.activation(sgate[:, par, c, :], pj[:, j % 2, :], ACT.Silu, bias=b).then_inc(pj_out, 1)

            def convolved(g, par, c):
                act.wait_ge(cv_done, (g * NCH + c + 1) * KC)
                act.activation(xc[:, par, c, :], flat(cv[:, c, :, :]), ACT.Silu).then_inc(xc_done, 1)

            def copy_bc(g, par, k):
                act.wait_ge(pj_in, g * NJ + 6 + k)
                act.activation(BC[:, par, k, :], pj[:, (5 + k) % 2, :], ACT.Identity, bias=pw("b_bc")[:, k:k + 1]
                               ).then_inc(pj_out, 1)

            def trip(i, par):
                if not (isinstance(i, int) and i == 0):
                    act.wait_ge(yg_done, i * NCH)
                for j in range(5):
                    copy_in(i + 1, 1 - par, j)
                for c in range(NCH):
                    convolved(i + 1, 1 - par, c)
                for k in range(2):
                    copy_bc(i + 1, 1 - par, k)

            act.wait_ge(w_in, 16)
            act.wait_ge(pad_done, 3)
            act.activation(sig_a[:, :], pw("a"), ACT.Sigmoid).then_inc(sig_done, 1)
            for j in range(5):
                copy_in(0, 0, j)
            for c in range(NCH):
                convolved(0, 0, c)
            for k in range(2):
                copy_bc(0, 0, k)
            act.wait_ge(sig_done, 1)
            for r in range(NR):
                act.activation(dec[:, r, :], flat(within[:, :, :]), ACT.Copy, scale=sig_a[:, r:r + 1]
                               ).then_inc(dec_done, 1)
            trip(0, 0)
            with act.Fori(1, NIT - 2, 2) as i:
                trip(i, 1)
                trip(i + 1, 0)

        @block.vector
        def _(dve):
            def prenorm_begin(g):
                pre.vector(dve, g, x[:, bass.ds(g * U, U), :])

            def prenorm_end(g):
                dve.wait_ge(pre.rstd_ready, g + 1)
                if not (isinstance(g, int) and g == 0):
                    dve.wait_ge(pj_in, (g - 1) * NJ + 1)
                for u in range(U):
                    dve.tensor_scalar(xn[:, u, :], row(g, u), pre.mv[:, u, 0:1], pre.rstd[:, u:u + 1],
                                      ALU.subtract, ALU.mult).then_inc(xn_done, 1)
                dve.wait_ge(xn_done, (g + 1) * U)

            def tap(g, c, k):
                taps = xp[:, c, :, k:k + T]
                wk = pw("conv_w")[:, c * KC + k:c * KC + k + 1]
                if k == 0:
                    dve.wait_ge(pj_out, g * NJ + 2 + c)
                    if not (isinstance(g, int) and g == 0):
                        dve.wait_ge(xc_done, (g - 1) * NCH + c + 1)
                    dve.tensor_scalar(cv[:, c, :, :], taps, wk, pw("conv_b")[:, c:c + 1], ALU.mult,
                                      ALU.add).then_inc(cv_done, 1)
                else:
                    dve.wait_ge(cv_done, (g * NCH + c) * KC + k)
                    dve.scalar_tensor_tensor(cv[:, c, :, :], taps, wk, cv[:, c, :, :], ALU.mult,
                                             ALU.add).then_inc(cv_done, 1)

            def skip(g, par, c):
                dve.wait_ge(ya_in, g * NR + NS * (c + 1) + UR)
                if not (isinstance(g, int) and g == 0):
                    dve.wait_ge(yg_done, (g - 1) * NCH + c + 1)
                dve.scalar_tensor_tensor(yd[:, c, :], xc[:, par, c, :], pw("d")[:, c:c + 1], ya[:, c, :],
                                         ALU.mult, ALU.add).then_inc(yd_done, 1)

            def gate(g, par, c):
                dve.wait_ge(yd_done, (g + 1) * NCH + c + 1)
                dve.tensor_tensor(yg[:, c, :], yd[:, c, :], sgate[:, par, c, :], ALU.mult).then_inc(yg_done, 1)

            def trip(i, par, first=False, last=False, tail=False):
                for n in range(TAIL if tail else NR):
                    if not tail:
                        dve.wait_ge(xr_in, i * NR + n + 1)
                        if n == 0:
                            dve.wait_ge(pj_out, (i + 1) * NJ)
                        dve.wait_ge(h_done, i * NR + n + 1)
                        dve.tensor_tensor(uu[:, n % UR, :], xr_ps[:, n % 2, :], BC[:, par, 0, :], ALU.mult
                                          ).then_inc(u_done, 1)
                    m = block_at(n, SCAN_LAG, first, tail)
                    if m is not None:
                        if first:
                            dve.wait_ge(dec_done, m + 1)
                        dve.wait_ge(u_done, i * NR + m + 3)
                        dve.wait_ge(hc_done, i * NR + m + 1)
                        dve.tensor_tensor_scan(hh[:, m % UR, :], dec[:, m % NR, :], uu[:, m % UR, :], 0.0,
                                               ALU.mult, ALU.add).then_inc(h_done, 1)
                    if not tail and n == SKIP0:
                        skip(i, par, 0)
                    if not tail and n == SKIP0 + 1:
                        gate(i, par, 0)
                    if not first:
                        if n == SKIP1:
                            skip(i - 1, 1 - par, 1)
                        if n == SKIP1 + 1:
                            gate(i - 1, 1 - par, 1)
                        if n == NORM_A:
                            nm.begin(dve, i - 1)
                        if n == NORM_B:
                            nm.finish(dve, i - 1)
                    if not (last or tail):
                        if n == PRE_A:
                            prenorm_begin(i + 1)
                        if n == PRE_B:
                            prenorm_end(i + 1)
                        k = n - CONV_AT
                        if 0 <= k < NCH * KC:
                            tap(i + 1, k // KC, k % KC)

            dve.sem_inc(nm.r_ready, 1)
            dve.sem_inc(u_done, 2)
            dve.sem_inc(h_done, UR)
            dve.sem_inc(yd_done, NCH)
            dve.wait_ge(w_in, 16)
            prenorm_begin(0)
            prenorm_end(0)
            for c in range(NCH):
                for k in range(KC):
                    tap(0, c, k)
            trip(0, 0, first=True)
            with dve.Fori(1, NIT - 2, 2) as i:
                trip(i, 1)
                trip(i + 1, 0)
            trip(NIT - 1, 1, last=True)
            trip(NIT, 0, tail=True)
    ph.close()


def wide_moe_phase(nc, x, consts, weights, table):
    ph = Phase(nc, "ff3")
    E, K, EH = 64, 8, 32
    NR = E * EH // P
    NSH = 4
    NCK = NR + NSH
    w, w_in = weights, weights.loaded
    pw = lambda n: pick(w, table, n)
    xT = ph.sb("xT", [P, W])
    big = lambda n: ph.sb(n, [P, U, E])
    pr, gt, eq, cum, le, sel, cw = (big(n) for n in ("probs", "above", "equal", "cumul", "fits", "chosen", "share"))
    m1, sm, rs, cnt, need, s8, rs8 = (ph.sb(n, [P, U]) for n in ("lmax", "lsum", "rlsum", "above_n", "need", "sum8",
                                                                  "rsum8"))
    top = ph.sb("top8", [P, U, 8])
    cwT = ph.sb("shareT", [E, W])
    AR = 8
    LEAD = 7
    act_sb = ph.sb("silu", [P, AR, W])
    hid = ph.sb("hidden", [P, NCK, W])
    xt_ps = ph.ps("xT", [P, W])
    h_ps = ph.ps("h", [P, 3, W])
    cb_ps = ph.ps("share", [P, 2, W])
    y = ph.ps("y", [P, W])
    rows = Rows(ph, x)
    nm = Norm(ph, x, consts, y)
    (xt, lg, st, ex, cw_done, ct_in, ct_out, h_in, a_done, cb_in, hid_done, sh_done) = (ph.sem(n) for n in (
        "xT_ready", "logits_ready", "router_step", "exp_ready", "share_ready", "shareT_in_psum",
        "shareT_ready", "h_ready", "silu_ready", "share_spread", "hidden_ready", "shared_ready"))
    NSTEP = 18

    with nc.Block() as block:
        @block.sync
        def _(sp):
            weights.load_next(sp)

        @block.gpsimd
        def _(pool):
            rows.gpsimd(pool, 0, first=True)
            with pool.Fori(0, NIT - 1) as i:
                rows.gpsimd(pool, i + 1)
                nm.gpsimd(pool, i)
            nm.gpsimd(pool, NIT - 1)

        @block.tensor
        def _(pe):
            pe.wait_ge(w_in, 16)
            with pe.Fori(0, NIT) as i:
                rows.tensor(pe, i, xt_ps, consts["ident"][:, :])
                pe.wait_ge(xt, i + 1)
                for u in range(U):
                    o = xt_ps[:, u * E:(u + 1) * E]
                    pe.matmul(o, consts["ones"][0:1, 0:P], pw("router_b"), start=True, stop=False)
                    mm = pe.matmul(o, xT[:, u * T:(u + 1) * T], pw("router"), start=False, stop=True)
                mm.then_inc(lg, 1)

                def hidden(j):
                    pe.wait_ge(a_done, i * NCK + j + 1)
                    pe.matmul(h_ps[:, j % 3, :], pw("w1")[:, j * P:(j + 1) * P], xT[:, :], start=True,
                              stop=True).then_inc(h_in, 1)

                for j in range(NSH):
                    hidden(j)
                for r in range(LEAD - 1):
                    hidden(NSH + r)
                pe.wait_ge(cw_done, i + 1)
                hidden(NSH + LEAD - 1)
                for u in range(U):
                    mm = pe.transpose(xt_ps[0:E, u * T:(u + 1) * T], cw[:, u, :], consts["ident"][:, :])
                mm.then_inc(ct_in, 1)
                pe.wait_ge(ct_out, i + 1)
                for r in range(NR):
                    if 0 < r <= NR - LEAD:
                        hidden(NSH + LEAD + r - 1)
                    pe.wait_ge(hid_done, i * NR + r + 1)
                    pe.matmul(cb_ps[:, r % 2, :], pw("spread")[:, r * P:(r + 1) * P], cwT[:, :], start=True,
                              stop=True).then_inc(cb_in, 1)
                pe.wait_ge(nm.r_ready, i + 1)
                for u in range(U):
                    yu = y[:, u * D:(u + 1) * D]
                    for k in range(2):
                        pe.matmul(yu, consts["ones"][0:1, 0:P], pw(f"sb2_{k}"), start=(k == 0), stop=False)
                    pe.matmul(yu, cwT[:, u * T:(u + 1) * T], pw("b2"), start=False, stop=False)
                    for j in range(NCK):
                        if u == 0 and j >= NSH:
                            pe.wait_ge(hid_done, i * NR + (j - NSH) + 1 + 2)
                        if u == 0 and j == 0:
                            pe.wait_ge(sh_done, (i + 1) * NSH)
                        mm = pe.matmul(yu, hid[:, j, u * T:(u + 1) * T], pw("w2")[:, j * D:(j + 1) * D],
                                       start=False, stop=(j == NCK - 1))
                mm.then_inc(nm.y_ready, 1)

        @block.scalar
        def _(act):
            act.sem_inc(a_done, 3)
            act.wait_ge(w_in, 16)
            with act.Fori(0, NIT) as i:
                act.wait_ge(rows.free, i + 1)
                act.activation(xT[:, :], xt_ps[:, :], ACT.Copy).then_inc(xt, 1)
                act.wait_ge(st, i * NSTEP + 2)
                act.activation(pr[:, :, :], pr[:, :, :], ACT.Exp).then_inc(ex, 1)
                for j in range(NCK):
                    n = i * NCK + j
                    if j == NSH + LEAD:
                        act.wait_ge(ct_in, i + 1)
                        act.activation(cwT[:, :], xt_ps[0:E, :], ACT.Copy).then_inc(ct_out, 1)
                    act.wait_ge(h_in, n + 1)
                    b = pw("b1")[:, j:j + 1]
                    if j < NSH:
                        act.activation(hid[:, j, :], h_ps[:, j % 3, :], ACT.Silu, bias=b).then_inc(a_done, 1)
                        act.wait_ge(a_done, n + 4)
                        act.sem_inc(sh_done, 1)
                    else:
                        if j >= NSH + AR:
                            act.wait_ge(hid_done, i * NR + (j - NSH) + 1 - AR + 2)
                        act.activation(act_sb[:, (j - NSH) % AR, :], h_ps[:, j % 3, :], ACT.Silu, bias=b).then_inc(a_done, 1)

        @block.vector
        def _(dve):
            dve.sem_inc(nm.r_ready, 1)
            dve.sem_inc(hid_done, 2)
            dve.wait_ge(w_in, 16)
            with dve.Fori(0, NIT) as i:
                k0 = i * NSTEP
                dve.wait_ge(lg, i + 1)
                l = xt_ps[:, 0:U * E].rearrange("p (u e) -> p u e", u=U)
                step = [0]

                def done(ins, hold=True):
                    ins.then_inc(st, 1)
                    step[0] += 1
                    if hold:
                        dve.wait_ge(st, k0 + step[0])

                done(dve.tensor_reduce(m1[:, :], l, AXX, ALU.max))
                done(dve.tensor_tensor(pr[:, :, :], l, bcast(m1[:, :], 2, E), ALU.subtract), hold=False)
                dve.wait_ge(ex, i + 1)
                done(dve.tensor_reduce(sm[:, :], pr[:, :, :], AXX, ALU.add))
                done(dve.reciprocal(rs[:, :], sm[:, :]))
                done(dve.tensor_tensor(pr[:, :, :], pr[:, :, :], bcast(rs[:, :], 2, E), ALU.mult))
                dve.memset(cnt[:, :], 0.0)
                for u in range(U):
                    ins = dve.max(top[:, u, :], pr[:, u, :])
                done(ins)
                done(dve.tensor_tensor(gt[:, :, :], pr[:, :, :], bcast(top[:, :, 7], 2, E), ALU.is_gt), hold=False)
                done(dve.tensor_tensor(eq[:, :, :], pr[:, :, :], bcast(top[:, :, 7], 2, E), ALU.is_equal))
                done(dve.tensor_reduce(cnt[:, :], gt[:, :, :], AXX, ALU.add), hold=False)
                done(dve.tensor_tensor_scan(flat3(cum), pw("reset"), flat3(eq), 0.0, ALU.mult, ALU.add))
                done(dve.tensor_scalar(need[:, :], cnt[:, :], -1.0, float(K), ALU.mult, ALU.add))
                done(dve.tensor_tensor(le[:, :, :], cum[:, :, :], bcast(need[:, :], 2, E), ALU.is_le))
                done(dve.tensor_tensor(sel[:, :, :], le[:, :, :], eq[:, :, :], ALU.mult))
                done(dve.tensor_tensor(sel[:, :, :], sel[:, :, :], gt[:, :, :], ALU.add), hold=False)
                done(dve.tensor_reduce(s8[:, :], top[:, :, :], AXX, ALU.add))
                done(dve.reciprocal(rs8[:, :], s8[:, :]), hold=False)
                done(dve.tensor_tensor(sel[:, :, :], sel[:, :, :], pr[:, :, :], ALU.mult))
                assert step[0] == NSTEP - 1
                done(dve.tensor_tensor(cw[:, :, :], sel[:, :, :], bcast(rs8[:, :], 2, E), ALU.mult))
                dve.sem_inc(cw_done, 1)
                for r in range(NR):
                    j = NSH + r
                    dve.wait_ge(a_done, i * NCK + j + 4)
                    dve.wait_ge(cb_in, i * NR + r + 1)
                    dve.tensor_tensor(hid[:, j, :], act_sb[:, r % AR, :], cb_ps[:, r % 2, :], ALU.mult
                                      ).then_inc(hid_done, 1)
                nm.vector(dve, i)
    ph.close()


def flat3(a):
    return a[:, :, :].rearrange("p u e -> p (u e)")


def build(nc, t, tables, out, stages):
    ctx = ExitStack()
    with ctx:
        sb = lambda n, s, d=F32: ctx.enter_context(nc.sbuf_tensor(n, s, d))
        x = sb("x", [P, B, D])
        consts = {"ident": sb("ident", [P, P]), "ones": sb("ones", [P, 512]), "neghalf": sb("neghalf", [P, 16])}
        names = [NAMES[s] for s in stages]
        widths = [t[n].shape[1] for n in names] or [1]
        room = max(a + b for a, b in zip(widths, widths[1:] + [0]))
        wt = sb("weights", [P, room])
        weights = [Weights(wt, 0 if k % 2 == 0 else room - widths[k], t[n],
                           ctx.enter_context(nc.semaphore(n + "_weights_loaded"))) for k, n in enumerate(names)]
        for a, b in zip(weights, weights[1:]):
            a.next = b
        x_in = ctx.enter_context(nc.semaphore("x_loaded"))
        const_ready = ctx.enter_context(nc.semaphore("const_ready"))
        stored = ctx.enter_context(nc.semaphore("stored"))
        with nc.Block() as block:
            @block.sync
            def _(sp):
                sp.dma_start(x[:, :, :], t["x"].rearrange("b t d -> t b d")).then_inc(x_in, 16)
                for wts in weights[:1]:
                    wts.load(sp)
                sp.wait_ge(x_in, 16)

            @block.gpsimd
            def _(pool):
                pool.memset(consts["ident"][:, :], 0.0).then_inc(const_ready, 1)
                pool.memset(consts["ones"][:, :], 1.0).then_inc(const_ready, 1)
                pool.memset(consts["neghalf"][:, :], -0.5).then_inc(const_ready, 1)
                pool.wait_ge(const_ready, 3)
                pool.affine_select(out=consts["ident"][:, :], in_=consts["ident"][:, :],
                                   compare_op=ALU.not_equal, fill=1.0, base=0, pattern=[[-1, P]],
                                   channel_multiplier=1).then_inc(const_ready, 1)
                pool.wait_ge(const_ready, 4)
        for s, wts in zip(stages, weights):
            PHASES[s](nc, x, consts, wts, t, tables[NAMES[s]])
        with nc.Block() as block:
            @block.sync
            def _(sp):
                sp.dma_start(out.rearrange("b t d -> t b d"), x[:, :, :]).then_inc(stored, 16)
                sp.wait_ge(stored, 16)


NAMES = ("sa0", "xa0", "ff0", "sa1", "xa1", "ff1", "sa2", "xa2", "pw", "ssm", "xa3", "ff3")
PHASES = {
    0: lambda nc, x, c, w, t, tb: heads_phase(nc, x, c, w, tb),
    1: lambda nc, x, c, w, t, tb: attention_phase(nc, "xa0", x, c, t, w, tb, scale=HD ** -0.5, bias="causal"),
    2: lambda nc, x, c, w, t, tb: moe_phase(nc, "ff0", x, c, w, tb, F=512, gated=False,
                                            capacity=max(1, int(1.25 * (B * T) / 8 * 2))),
    3: lambda nc, x, c, w, t, tb: delta_phase(nc, x, c, w, tb,
                                              nc.dram_tensor("records", (B, HQ, T, RW), F32, kind="Internal").ap(),
                                              nc.dram_tensor("recurrence", (B, HQ, T, QW), F32, kind="Internal").ap()),
    4: lambda nc, x, c, w, t, tb: attention_phase(nc, "xa1", x, c, t, w, tb, scale=HD ** -0.5, bias="rows"),
    5: lambda nc, x, c, w, t, tb: moe_phase(nc, "ff1", x, c, w, tb, F=448, gated=True),
    6: lambda nc, x, c, w, t, tb: attention_phase(nc, "sa2", x, c, t, w, tb, scale=0.25, bias="causal", lut=True),
    7: lambda nc, x, c, w, t, tb: attention_phase(nc, "xa2", x, c, t, w, tb, scale=HD ** -0.5),
    8: lambda nc, x, c, w, t, tb: piecewise_phase(nc, x, c, w, tb),
    9: lambda nc, x, c, w, t, tb: ssm_phase(nc, x, c, w, tb),
    10: lambda nc, x, c, w, t, tb: attention_phase(nc, "xa3", x, c, t, w, tb, scale=HD ** -0.5, bias="heads"),
    11: lambda nc, x, c, w, t, tb: wide_moe_phase(nc, x, c, w, tb),
}


STAGES = list(range(12))


def _pack(np, parts):
    table, cols = {}, 0
    for name, a in parts:
        table[name] = (a.shape[0], cols, a.shape[1])
        cols += a.shape[1]
    out = np.zeros((P, cols), np.float32)
    for name, a in parts:
        r, o, c = table[name]
        out[0:r, o:o + c] = a
    return out, table


def _layouts(np, g):
    packs = {}
    W1, b1, W2 = (g("L2_ffn_" + n).reshape(64, 8, 2) for n in ("W1", "b1", "W2"))
    pair = lambda a: np.concatenate([a[:, :, 0], a[:, :, 1]], 0)
    dup = lambda a: np.concatenate([a, a], -1)
    Wout = g("L2_ffn_Wout")
    packs["pw"] = [("Win", dup(g("L2_ffn_Win"))), ("bin", dup(g("L2_ffn_bin_"))[:, None]),
                   ("W1", pair(W1)), ("b1", pair(b1)), ("W2", pair(W2)),
                   ("Wout", Wout), ("Wout2", np.concatenate([Wout, Wout], 0)),
                   ("b2", np.repeat(g("L2_ffn_b2")[:, None], P, 1)),
                   ("bout", g("L2_ffn_bout")[None, :])]

    def own(hf):
        return (np.arange(P)[:, None] // hf == np.arange(P // hf)[None, :]).astype(np.float32)

    def causal(nk):
        return np.where(np.arange(nk)[None, :] <= np.arange(T)[:, None], 0.0, MASKED).astype(np.float32)

    def attn(wq, bq, wk, bk, wv, bv, wo, bo):
        parts = [("wq", wq), ("wk", wk), ("wv", wv), ("wo", wo), ("own", own(HD))]
        if bq is not None:
            parts += [("bq", bq[:, None]), ("bk", bk[:, None])]
        parts += [("bv", np.zeros((1, D), np.float32) if bv is None else bv[None, :])]
        return parts + [("bo", bo[None, :])]

    packs["xa0"] = attn(*(g("L0_xattn_" + n) for n in ("q_w", "q_b", "k_w", "k_b", "v_w", "v_b", "o_w", "o_b")))
    packs["xa0"] += [("causal", causal(S2))]
    L1 = lambda n: g("L1_xattn_" + n)
    packs["xa1"] = attn(L1("Wq").T, L1("bq"), L1("Wk").T, L1("bk"), L1("Wv").T, L1("bv"), L1("Wo").T, L1("bo"))
    kv = g("L2_xattn_Wkv")
    packs["xa2"] = attn(g("L2_xattn_Wq").T, None, kv[:D].T, None, kv[D:].T, None, g("L2_xattn_Wproj").T,
                        g("L2_xattn_bproj"))
    packs["xa3"] = attn(*(g("L3_xattn_" + n) for n in ("Wq", "bq", "Wk", "bk", "Wv", "bv", "Wo", "bo")))
    eye = np.eye(P, dtype=np.float32)
    L2 = lambda n: g("L2_attn_" + n)
    cols = lambda a, b: np.stack([a.reshape(-1), b.reshape(-1)], 1)
    packs["sa2"] = [("wid", cols(L2("w_q"), L2("w_k"))), ("shift", cols(L2("b_q"), L2("b_k"))),
                    ("own", own(2 * HD)),
                    ("wv", L2("v_w").T), ("wo", L2("out_w").T), ("causal", causal(T))]
    for f in range(2):
        for k in range(2):
            sel = np.zeros((P, 8, 2, HD), np.float32)
            sel[:, :, k, :] = eye[:, f * 64:(f + 1) * 64].reshape(P, 8, HD)
            packs["sa2"] += [(f"sel{f}{k}", sel.reshape(P, P))]

    reset = np.tile((np.arange(U * 8) % 8 != 0).astype(np.float32)[None, :], (P, 1))
    upto = np.triu(np.ones((T, T), np.float32))
    packs["ff0"] = [("router", g("L0_ffn_router_w").T), ("reset", reset), ("upto", upto),
                    ("w1", g("L0_ffn_w1").transpose(1, 0, 2).reshape(D, -1)),
                    ("w2", g("L0_ffn_w2").reshape(8, 4, 128, D).transpose(2, 0, 1, 3).reshape(128, -1))]
    packs["ff1"] = [("router", g("L1_ffn_gate_w").T), ("reset", reset),
                    ("w1", g("L1_ffn_w1").transpose(2, 0, 1).reshape(D, -1)),
                    ("w3", g("L1_ffn_w3").transpose(2, 0, 1).reshape(D, -1)),
                    ("w2", g("L1_ffn_w2").transpose(0, 2, 1).reshape(8, 4, 112, D).transpose(2, 0, 1, 3)
                     .reshape(112, -1))]

    A0 = lambda n: g("L0_attn_" + n)
    up = A0("Wup").reshape(32, H, 2, HD).transpose(0, 2, 1, 3).reshape(32, 2 * D)
    bup = A0("bup").reshape(H, 2, HD).transpose(1, 0, 2).reshape(1, 2 * D)
    freq = 1.0 / 10000.0 ** (np.arange(0, HD, 2, dtype=np.float32) / HD)
    angle = np.arange(T, dtype=np.float32)[:, None] * freq[None, :].astype(np.float32)
    cos, sin = np.cos(angle).astype(np.float32), np.sin(angle).astype(np.float32)
    packs["sa0"] = [("wq", A0("Wq")), ("bq", A0("bq")[None, :]), ("wdown", A0("Wdown")), ("bdown", A0("bdown")[:, None]),
                    ("wup", up), ("bup", bup), ("wout", A0("Wout")), ("bout", A0("bout")[None, :]),
                    ("cos", np.concatenate([cos, cos], 1)), ("sin", np.concatenate([-sin, sin], 1))]

    A1 = lambda n: g("L1_attn_" + n)
    packs["sa1"] = [("wproj", np.concatenate([A1(n) for n in ("Wq", "Wk", "Wv", "Wgamma", "Wf")], 1)),
                    ("wg1", A1("Wg1")), ("wg2", A1("Wg2")), ("wo", A1("Wo")),
                    ("norm_w", np.tile(A1("norm_w")[None, :], (P, 1)))]

    A3 = lambda n: g("L3_attn_" + n)
    by_chunk = lambda a: a.reshape(-1, P).T
    wb, wc = (np.tile(A3(n).reshape(2, P, 1, 16), (1, 1, 8, 1)).reshape(2, P, P) for n in ("W_B", "W_C"))
    block = np.arange(16)[:, None, None] * 8 + np.arange(P)[None, None, :] // 16
    spread = (np.arange(P)[None, :, None] == block).astype(np.float32)
    packs["ssm"] = [("ln_g", A3("ln_g")[:, None]), ("ln_b", A3("ln_b")[:, None]), ("w_in", A3("W_in")),
                    ("b_in", by_chunk(A3("b_in"))),
                    ("conv_w", A3("conv_w").reshape(2, P, 4).transpose(1, 0, 2).reshape(P, 8)),
                    ("conv_b", by_chunk(A3("conv_b"))),
                    ("w_bc", np.concatenate([wb[0], wb[1], wc[0], wc[1]], 1)),
                    ("b_bc", np.stack([np.tile(A3("b_B"), 8), np.tile(A3("b_C"), 8)], 1)),
                    ("a", A3("A").reshape(32, P).T), ("d", by_chunk(A3("D"))),
                    ("spread", spread.transpose(1, 0, 2).reshape(P, -1)),
                    ("gather", spread.transpose(2, 0, 1).reshape(P, -1)),
                    ("w_out", A3("W_out").reshape(2, P, D).transpose(1, 0, 2).reshape(P, -1)),
                    ("b_out", A3("b_out")[None, :])]

    F3 = lambda n: g("L3_ffn_" + n)
    w1 = np.concatenate([F3("sw1").transpose(1, 0, 2).reshape(D, 512), F3("w1").transpose(1, 0, 2).reshape(D, 2048)], 1)
    w2 = np.concatenate([F3("sw2").reshape(512, D), F3("w2").reshape(2048, D)], 0)
    b1 = np.concatenate([F3("sb1").reshape(-1), F3("b1").reshape(-1)])
    ex = np.arange(2048)[None, :] // 32 == np.arange(64)[:, None]
    packs["ff3"] = [("router", F3("router_w")), ("router_b", F3("router_b")[None, :]),
                    ("reset", np.tile((np.arange(U * 64) % 64 != 0).astype(np.float32)[None, :], (P, 1))),
                    ("w1", w1), ("b1", by_chunk(b1)), ("w2", w2.reshape(20, P, D).transpose(1, 0, 2).reshape(P, -1)),
                    ("b2", F3("b2")), ("sb2_0", F3("sb2")[0:1]), ("sb2_1", F3("sb2")[1:2]),
                    ("spread", ex.astype(np.float32))]
    return packs


def kernel(**inputs):
    import numpy as np
    import concourse.bacc as bacc
    from concourse.bass_utils import run_bass_kernel_spmd

    nc = bacc.Bacc("TRN2", target_bir_lowering=False, num_devices=1)
    g = lambda n: np.asarray(inputs[n])
    arrays, tables = {}, {}
    for name, parts in _layouts(np, g).items():
        arrays[name], tables[name] = _pack(np, parts)
    arrays["x"] = g("x")
    arrays["ctxT"] = g("ctx_1024").reshape(B * S2, D).T
    arrays["fside"] = g("fside_Bx16xSxS2_0")
    arrays["xa1_mask"] = g("mask_BxSxS2_bf1").view(np.uint8)
    arrays["xa3_mask"] = g("mask_Bx1xSxS2_ik1").reshape(B, T, S2)
    t = {}
    for name, a in arrays.items():
        t[name] = nc.dram_tensor(f"in_{name}", a.shape, mybir.dt.from_np(a.dtype), kind="ExternalInput").ap()
    out = nc.dram_tensor("out_x", (B, T, D), F32, kind="ExternalOutput").ap()
    build(nc, t, tables, out, STAGES)
    feed = {f"in_{n}": np.ascontiguousarray(a) for n, a in arrays.items()}
    r = run_bass_kernel_spmd(nc, [feed], core_ids=[0])
    return r.results[0]["out_x"]
```
